# Optimizing a Trainium2 kernel written in Bass

```python
import numpy as np
import jax
import jax.numpy as jnp

def _softmax(x, axis=-1):
    return jax.nn.softmax(x, axis=axis)

def _gelu(x):
    return jax.nn.gelu(x, approximate=True)

def _silu(x):
    return jax.nn.silu(x)

def _sigmoid(x):
    return jax.nn.sigmoid(x)

def _layernorm(x, axis=-1, eps=1e-05):
    m = jnp.mean(x, axis=axis, keepdims=True)
    v = jnp.var(x, axis=axis, keepdims=True)
    return (x - m) / jnp.sqrt(v + eps)

def _scatter_add(tgt, idx, src, axis=0):
    return tgt.at[idx].add(src)

def _segment_sum(src, seg, n):
    return jax.ops.segment_sum(src, seg, n)
kernel_name = 'mk_vit_tower_cls_d2_tok_img512_r4_004ea7'

def setup_inputs(seed: int=0):
    np.random.seed(seed)
    _w = jnp.asarray

    def _rec_inputs():
        import jax
        import jax.numpy as jnp
        _rk = jax.random.key(seed)
        x = -0.000222058 + 0.999998 * jax.random.normal(jax.random.fold_in(_rk, 1), (128, 3, 64, 64), jnp.float32)
        cls_tok = 0.02 * jax.random.normal(jax.random.fold_in(_rk, 5), (1, 1, 128), jnp.float32)
        return (x, cls_tok)
    x, cls_tok = _rec_inputs()

    def _L0_tok_setup():
        import jax, jax.numpy as jnp
        import numpy as np
        IMG, P, C, D = (64, 16, 3, 128)
        NP = (IMG // P) ** 2
        PD = P * P * C
        key = jax.random.key(seed)
        k1, k2, k3 = jax.random.split(key, 3)
        x = jax.random.normal(k1, (128, C, IMG, IMG), dtype=jnp.float32)
        W = jax.random.normal(k2, (D, PD), dtype=jnp.float32) * (1.0 / np.sqrt(PD))
        b = jax.random.normal(k3, (D,), dtype=jnp.float32) * 0.01
        return {'x': x, 'W': W, 'b': b}
    _L0_tok_all = _L0_tok_setup()
    _L0_tok_in = {k: v for k, v in _L0_tok_all.items() if k in ('W', 'b')}
    del _L0_tok_all

    def _L0_attn_setup():
        import jax, jax.numpy as jnp
        import numpy as np
        H = 8
        W = 64
        SHIFT = True
        DIM = 128
        SCALE = (DIM // H) ** (-0.5)
        key = jax.random.key(seed)
        k1, k2, k3, k4 = jax.random.split(key, 4)
        x = jax.random.normal(k1, (8, 1024, DIM), dtype=jnp.float32)
        w_qkv = jax.random.normal(k2, (3 * DIM, DIM), dtype=jnp.float32) * 0.02
        w_proj = jax.random.normal(k3, (DIM, DIM), dtype=jnp.float32) * 0.02
        b_proj = jax.random.normal(k4, (DIM,), dtype=jnp.float32) * 0.02
        return {'x': x, 'w_qkv': w_qkv, 'w_proj': w_proj, 'b_proj': b_proj}
    _L0_attn_all = _L0_attn_setup()
    _L0_attn_in = {k: v for k, v in _L0_attn_all.items() if k in ('w_qkv', 'w_proj', 'b_proj')}
    del _L0_attn_all

    def _L0_ffn_setup():
        import jax, jax.numpy as jnp
        import numpy as np
        D_MODEL = 128
        D_FF = 512
        N_EXPERTS = 8
        TOP_K = 2
        key = jax.random.key(seed)
        ks = jax.random.split(key, 7)
        x = jax.random.normal(ks[0], (8, 1024, D_MODEL), dtype=jnp.float32)
        router_w = jax.random.normal(ks[1], (D_MODEL, N_EXPERTS), dtype=jnp.float32) * 0.02
        router_b = jnp.zeros((N_EXPERTS,), dtype=jnp.float32)
        s1 = 1.0 / np.sqrt(D_MODEL)
        s2 = 1.0 / np.sqrt(D_FF)
        w1 = jax.random.uniform(ks[2], (N_EXPERTS, D_MODEL, D_FF), jnp.float32, -s1, s1)
        b1 = jax.random.uniform(ks[3], (N_EXPERTS, D_FF), jnp.float32, -s1, s1)
        w2 = jax.random.uniform(ks[4], (N_EXPERTS, D_FF, D_MODEL), jnp.float32, -s2, s2)
        b2 = jax.random.uniform(ks[5], (N_EXPERTS, D_MODEL), jnp.float32, -s2, s2)
        return {'x': x, 'router_w': router_w, 'router_b': router_b, 'w1': w1, 'b1': b1, 'w2': w2, 'b2': b2}
    _L0_ffn_all = _L0_ffn_setup()
    _L0_ffn_in = {k: v for k, v in _L0_ffn_all.items() if k in ('router_w', 'router_b', 'w1', 'b1', 'w2', 'b2')}
    del _L0_ffn_all

    def _L1_attn_setup():
        import jax, jax.numpy as jnp
        import numpy as np
        B, L, D, H = (4, 256, 128, 8)
        HEAD_DIM = D // H
        WINDOW = 32
        HALF = WINDOW // 2
        TEMP = 1.0
        PAT_TEMP = 0.3
        THRESHOLD = 0.05
        SPARSITY = 0.3

        def _forward(x, qkv_w, proj_w, proj_b, ps_w1, ps_b1, ps_w2, ps_b2, ps_w3, ps_b3, pattern_bias, sparse_w, sparse_b):
            b, l, d = x.shape
            scale = HEAD_DIM ** (-0.5)
            qkv = (x @ qkv_w.T).reshape(b, l, 3, H, HEAD_DIM)
            qkv = jnp.transpose(qkv, (2, 0, 3, 1, 4))
            q, k, v = (qkv[0], qkv[1], qkv[2])
            scores = jnp.einsum('bhqd,bhkd->bhqk', q, k) * scale
            pooled = x.mean(axis=1)
            h1 = jax.nn.relu(pooled @ ps_w1.T + ps_b1)
            h2 = jax.nn.relu(h1 @ ps_w2.T + ps_b2)
            logits = h2 @ ps_w3.T + ps_b3 + pattern_bias
            pw = jax.nn.softmax(logits / PAT_TEMP, axis=-1)
            idx = jnp.arange(l)
            local_mask = (jnp.abs(idx[:, None] - idx[None, :]) <= HALF).astype(jnp.float32)
            s2 = scores * sparse_w[None, :, None, None] + sparse_b[None, :, None, None]
            k_top = max(1, min(l, int(l * (1.0 - SPARSITY))))
            _, ti = jax.lax.top_k(s2, k_top)
            flat_idx = ti.reshape(-1, k_top)
            rows = jnp.arange(flat_idx.shape[0])[:, None]
            sparse_mask = jnp.zeros((b * H * l, l), jnp.float32).at[rows, flat_idx].set(1.0)
            sparse_mask = sparse_mask.reshape(b, H, l, l)
            combined = pw[:, 0, None, None, None] * local_mask + pw[:, 1, None, None, None] + pw[:, 2, None, None, None] * sparse_mask
            allow = combined > THRESHOLD
            masked = jnp.where(allow, scores, -jnp.inf)
            all_masked = ~allow.any(axis=-1)
            masked = masked.at[..., 0].set(jnp.where(all_masked, 0.0, masked[..., 0]))
            attn = jax.nn.softmax(masked / TEMP, axis=-1)
            out = jnp.einsum('bhqk,bhkd->bhqd', attn, v)
            out = jnp.transpose(out, (0, 2, 1, 3)).reshape(b, l, d)
            return out @ proj_w.T + proj_b
        key = jax.random.key(seed)
        ks = jax.random.split(key, 12)
        s = 0.02
        x = jax.random.normal(ks[0], (B, L, D), jnp.float32)
        qkv_w = jax.random.normal(ks[1], (3 * D, D), jnp.float32) * s
        proj_w = jax.random.normal(ks[2], (D, D), jnp.float32) * s
        proj_b = jnp.zeros((D,), jnp.float32)
        ps_w1 = jax.random.normal(ks[3], (D, D), jnp.float32) * s
        ps_b1 = jnp.zeros((D,), jnp.float32)
        ps_w2 = jax.random.normal(ks[4], (D // 2, D), jnp.float32) * s
        ps_b2 = jnp.zeros((D // 2,), jnp.float32)
        ps_w3 = jax.random.normal(ks[5], (3, D // 2), jnp.float32) * 0.1
        ps_b3 = jnp.array([1.0, -0.5, -0.5], jnp.float32)
        pattern_bias = jnp.array([0.2, -0.1, -0.1], jnp.float32)
        sparse_w = jax.random.normal(ks[6], (H,), jnp.float32) * 0.3
        sparse_b = jnp.zeros((H,), jnp.float32)
        return dict(x=x, qkv_w=qkv_w, proj_w=proj_w, proj_b=proj_b, ps_w1=ps_w1, ps_b1=ps_b1, ps_w2=ps_w2, ps_b2=ps_b2, ps_w3=ps_w3, ps_b3=ps_b3, pattern_bias=pattern_bias, sparse_w=sparse_w, sparse_b=sparse_b)
    _L1_attn_all = _L1_attn_setup()
    _L1_attn_in = {k: v for k, v in _L1_attn_all.items() if k in ('qkv_w', 'proj_w', 'proj_b', 'ps_w1', 'ps_b1', 'ps_w2', 'ps_b2', 'ps_w3', 'ps_b3', 'pattern_bias', 'sparse_w', 'sparse_b')}
    del _L1_attn_all

    def _L1_ffn_setup():
        import jax, jax.numpy as jnp
        import numpy as np
        B, S, D = (4, 256, 128)
        E = 16
        DH = 4 * D
        DS = 2 * D
        TOP_K = 2
        TEMP = 0.7
        SHARED_SCALE = 0.25
        EPS = 1e-05

        def layer_norm(x, g, b):
            mu = jnp.mean(x, axis=-1, keepdims=True)
            var = jnp.mean(jnp.square(x - mu), axis=-1, keepdims=True)
            return (x - mu) * jax.lax.rsqrt(var + EPS) * g + b
        key = jax.random.key(seed)
        ks = jax.random.split(key, 12)
        s = 0.02
        return {'x': jax.random.normal(ks[0], (B, S, D), jnp.float32), 'ln_in_g': jnp.ones((D,), jnp.float32), 'ln_in_b': jnp.zeros((D,), jnp.float32), 'router_w': jax.random.normal(ks[1], (D, E), jnp.float32) * s, 'router_b': jnp.zeros((E,), jnp.float32), 'ew1': jax.random.normal(ks[2], (E, D, DH), jnp.float32) * s, 'eb1': jnp.zeros((E, DH), jnp.float32), 'ew2': jax.random.normal(ks[3], (E, DH, D), jnp.float32) * s, 'eb2': jnp.zeros((E, D), jnp.float32), 'sw1': jax.random.normal(ks[4], (D, DS), jnp.float32) * s, 'sb1': jnp.zeros((DS,), jnp.float32), 'sw2': jax.random.normal(ks[5], (DS, D), jnp.float32) * s, 'sb2': jnp.zeros((D,), jnp.float32), 'ff_ln_g': jnp.ones((D,), jnp.float32), 'ff_ln_b': jnp.zeros((D,), jnp.float32), 'ff_w1': jax.random.normal(ks[6], (D, DH), jnp.float32) * s, 'ff_b1': jnp.zeros((DH,), jnp.float32), 'ff_w2': jax.random.normal(ks[7], (DH, D), jnp.float32) * s, 'ff_b2': jnp.zeros((D,), jnp.float32)}
    _L1_ffn_all = _L1_ffn_setup()
    _L1_ffn_in = {k: v for k, v in _L1_ffn_all.items() if k in ('ln_in_g', 'ln_in_b', 'router_w', 'router_b', 'ew1', 'eb1', 'ew2', 'eb2', 'sw1', 'sb1', 'sw2', 'sb2', 'ff_ln_g', 'ff_ln_b', 'ff_w1', 'ff_b1', 'ff_w2', 'ff_b2')}
    del _L1_ffn_all
    return {'x': x, 'cls_tok': cls_tok, 'L0_tok_W': _L0_tok_in['W'], 'L0_tok_b': _L0_tok_in['b'], 'L0_attn_w_qkv': _L0_attn_in['w_qkv'], 'L0_attn_w_proj': _L0_attn_in['w_proj'], 'L0_attn_b_proj': _L0_attn_in['b_proj'], 'L0_ffn_router_w': _L0_ffn_in['router_w'], 'L0_ffn_router_b': _L0_ffn_in['router_b'], 'L0_ffn_w1': _L0_ffn_in['w1'], 'L0_ffn_b1': _L0_ffn_in['b1'], 'L0_ffn_w2': _L0_ffn_in['w2'], 'L0_ffn_b2': _L0_ffn_in['b2'], 'L1_attn_qkv_w': _L1_attn_in['qkv_w'], 'L1_attn_proj_w': _L1_attn_in['proj_w'], 'L1_attn_proj_b': _L1_attn_in['proj_b'], 'L1_attn_ps_w1': _L1_attn_in['ps_w1'], 'L1_attn_ps_b1': _L1_attn_in['ps_b1'], 'L1_attn_ps_w2': _L1_attn_in['ps_w2'], 'L1_attn_ps_b2': _L1_attn_in['ps_b2'], 'L1_attn_ps_w3': _L1_attn_in['ps_w3'], 'L1_attn_ps_b3': _L1_attn_in['ps_b3'], 'L1_attn_pattern_bias': _L1_attn_in['pattern_bias'], 'L1_attn_sparse_w': _L1_attn_in['sparse_w'], 'L1_attn_sparse_b': _L1_attn_in['sparse_b'], 'L1_ffn_ln_in_g': _L1_ffn_in['ln_in_g'], 'L1_ffn_ln_in_b': _L1_ffn_in['ln_in_b'], 'L1_ffn_router_w': _L1_ffn_in['router_w'], 'L1_ffn_router_b': _L1_ffn_in['router_b'], 'L1_ffn_ew1': _L1_ffn_in['ew1'], 'L1_ffn_eb1': _L1_ffn_in['eb1'], 'L1_ffn_ew2': _L1_ffn_in['ew2'], 'L1_ffn_eb2': _L1_ffn_in['eb2'], 'L1_ffn_sw1': _L1_ffn_in['sw1'], 'L1_ffn_sb1': _L1_ffn_in['sb1'], 'L1_ffn_sw2': _L1_ffn_in['sw2'], 'L1_ffn_sb2': _L1_ffn_in['sb2'], 'L1_ffn_ff_ln_g': _L1_ffn_in['ff_ln_g'], 'L1_ffn_ff_ln_b': _L1_ffn_in['ff_ln_b'], 'L1_ffn_ff_w1': _L1_ffn_in['ff_w1'], 'L1_ffn_ff_b1': _L1_ffn_in['ff_b1'], 'L1_ffn_ff_w2': _L1_ffn_in['ff_w2'], 'L1_ffn_ff_b2': _L1_ffn_in['ff_b2']}

def reference(x, cls_tok, L0_tok_W, L0_tok_b, L0_attn_w_qkv, L0_attn_w_proj, L0_attn_b_proj, L0_ffn_router_w, L0_ffn_router_b, L0_ffn_w1, L0_ffn_b1, L0_ffn_w2, L0_ffn_b2, L1_attn_qkv_w, L1_attn_proj_w, L1_attn_proj_b, L1_attn_ps_w1, L1_attn_ps_b1, L1_attn_ps_w2, L1_attn_ps_b2, L1_attn_ps_w3, L1_attn_ps_b3, L1_attn_pattern_bias, L1_attn_sparse_w, L1_attn_sparse_b, L1_ffn_ln_in_g, L1_ffn_ln_in_b, L1_ffn_router_w, L1_ffn_router_b, L1_ffn_ew1, L1_ffn_eb1, L1_ffn_ew2, L1_ffn_eb2, L1_ffn_sw1, L1_ffn_sb1, L1_ffn_sw2, L1_ffn_sb2, L1_ffn_ff_ln_g, L1_ffn_ff_ln_b, L1_ffn_ff_w1, L1_ffn_ff_b1, L1_ffn_ff_w2, L1_ffn_ff_b2):
    import jax
    import jax.numpy as jnp

    def _L0_tok_ref(x, W, b):
        import jax, jax.numpy as jnp
        import numpy as np
        IMG, P, C, D = (64, 16, 3, 128)
        NP = (IMG // P) ** 2
        PD = P * P * C
        B, c, H, Wd = x.shape
        xp = x.reshape(B, c, H // P, P, Wd // P, P)
        xp = xp.transpose(0, 2, 4, 1, 3, 5).reshape(B, NP, c * P * P)
        return jnp.einsum('bnk,dk->bnd', xp, W) + b

    def _L0_attn_ref(x, w_qkv, w_proj, b_proj):
        import jax, jax.numpy as jnp
        import numpy as np
        H = 8
        W = 64
        SHIFT = True
        DIM = 128
        SCALE = (DIM // H) ** (-0.5)
        B, N, C = x.shape
        if SHIFT:
            x = jnp.roll(x, -W // 2, axis=1)
        pad = (W - N % W) % W
        if pad:
            x = jnp.pad(x, ((0, 0), (0, pad), (0, 0)))
        nw = x.shape[1] // W
        xw = x.reshape(B * nw, W, C)
        qkv = xw @ w_qkv.T
        qkv = qkv.reshape(B * nw, W, 3, H, C // H)
        q, k, v = (qkv[:, :, 0], qkv[:, :, 1], qkv[:, :, 2])
        attn = jnp.einsum('bwhd,bwgd->bwhg', q, k) * SCALE
        attn = jax.nn.softmax(attn, axis=-1)
        out = jnp.einsum('bwhg,bwgd->bwhd', attn, v)
        out = out.transpose(0, 2, 1, 3).reshape(B * nw, W, C)
        out = out @ w_proj.T + b_proj
        out = out.reshape(B, nw * W, C)[:, :N]
        if SHIFT:
            out = jnp.roll(out, W // 2, axis=1)
        return out

    def _L0_ffn_ref(x, router_w, router_b, w1, b1, w2, b2):
        import jax, jax.numpy as jnp
        import numpy as np
        D_MODEL = 128
        D_FF = 512
        N_EXPERTS = 8
        TOP_K = 2
        leading = x.shape[:-1]
        d = x.shape[-1]
        x_flat = x.reshape(-1, d)
        T = x_flat.shape[0]
        logits = x_flat @ router_w + router_b
        probs = jax.nn.softmax(logits, axis=-1)
        sel_w, sel_idx = jax.lax.top_k(probs, TOP_K)
        sel_w = sel_w / (jnp.sum(sel_w, axis=-1, keepdims=True) + 1e-09)
        tok = jnp.arange(T)
        comb = jnp.zeros((T, N_EXPERTS), dtype=x_flat.dtype)
        for k in range(TOP_K):
            comb = comb.at[tok, sel_idx[:, k]].add(sel_w[:, k])
        out = jnp.zeros_like(x_flat)
        for e in range(N_EXPERTS):
            h = jax.nn.gelu(x_flat @ w1[e] + b1[e], approximate=False)
            y = h @ w2[e] + b2[e]
            out = out + comb[:, e:e + 1] * y
        return out.reshape(*leading, d)

    def _L1_attn_ref(x, qkv_w, proj_w, proj_b, ps_w1, ps_b1, ps_w2, ps_b2, ps_w3, ps_b3, pattern_bias, sparse_w, sparse_b):
        import jax, jax.numpy as jnp
        import numpy as np
        B, L, D, H = (4, 256, 128, 8)
        HEAD_DIM = D // H
        WINDOW = 32
        HALF = WINDOW // 2
        TEMP = 1.0
        PAT_TEMP = 0.3
        THRESHOLD = 0.05
        SPARSITY = 0.3

        def _forward(x, qkv_w, proj_w, proj_b, ps_w1, ps_b1, ps_w2, ps_b2, ps_w3, ps_b3, pattern_bias, sparse_w, sparse_b):
            b, l, d = x.shape
            scale = HEAD_DIM ** (-0.5)
            qkv = (x @ qkv_w.T).reshape(b, l, 3, H, HEAD_DIM)
            qkv = jnp.transpose(qkv, (2, 0, 3, 1, 4))
            q, k, v = (qkv[0], qkv[1], qkv[2])
            scores = jnp.einsum('bhqd,bhkd->bhqk', q, k) * scale
            pooled = x.mean(axis=1)
            h1 = jax.nn.relu(pooled @ ps_w1.T + ps_b1)
            h2 = jax.nn.relu(h1 @ ps_w2.T + ps_b2)
            logits = h2 @ ps_w3.T + ps_b3 + pattern_bias
            pw = jax.nn.softmax(logits / PAT_TEMP, axis=-1)
            idx = jnp.arange(l)
            local_mask = (jnp.abs(idx[:, None] - idx[None, :]) <= HALF).astype(jnp.float32)
            s2 = scores * sparse_w[None, :, None, None] + sparse_b[None, :, None, None]
            k_top = max(1, min(l, int(l * (1.0 - SPARSITY))))
            _, ti = jax.lax.top_k(s2, k_top)
            flat_idx = ti.reshape(-1, k_top)
            rows = jnp.arange(flat_idx.shape[0])[:, None]
            sparse_mask = jnp.zeros((b * H * l, l), jnp.float32).at[rows, flat_idx].set(1.0)
            sparse_mask = sparse_mask.reshape(b, H, l, l)
            combined = pw[:, 0, None, None, None] * local_mask + pw[:, 1, None, None, None] + pw[:, 2, None, None, None] * sparse_mask
            allow = combined > THRESHOLD
            masked = jnp.where(allow, scores, -jnp.inf)
            all_masked = ~allow.any(axis=-1)
            masked = masked.at[..., 0].set(jnp.where(all_masked, 0.0, masked[..., 0]))
            attn = jax.nn.softmax(masked / TEMP, axis=-1)
            out = jnp.einsum('bhqk,bhkd->bhqd', attn, v)
            out = jnp.transpose(out, (0, 2, 1, 3)).reshape(b, l, d)
            return out @ proj_w.T + proj_b
        return _forward(x, qkv_w, proj_w, proj_b, ps_w1, ps_b1, ps_w2, ps_b2, ps_w3, ps_b3, pattern_bias, sparse_w, sparse_b)

    def _L1_ffn_ref(x, ln_in_g, ln_in_b, router_w, router_b, ew1, eb1, ew2, eb2, sw1, sb1, sw2, sb2, ff_ln_g, ff_ln_b, ff_w1, ff_b1, ff_w2, ff_b2):
        import jax, jax.numpy as jnp
        import numpy as np
        B, S, D = (4, 256, 128)
        E = 16
        DH = 4 * D
        DS = 2 * D
        TOP_K = 2
        TEMP = 0.7
        SHARED_SCALE = 0.25
        EPS = 1e-05

        def layer_norm(x, g, b):
            mu = jnp.mean(x, axis=-1, keepdims=True)
            var = jnp.mean(jnp.square(x - mu), axis=-1, keepdims=True)
            return (x - mu) * jax.lax.rsqrt(var + EPS) * g + b
        h = layer_norm(x, ln_in_g, ln_in_b)
        gate = jax.nn.softmax((h @ router_w + router_b) / TEMP, axis=-1)
        vals, idx = jax.lax.top_k(gate, TOP_K)
        comb = jnp.sum(jax.nn.one_hot(idx, E, dtype=h.dtype) * vals[..., None], axis=-2)
        eh = jax.nn.silu(jnp.einsum('bsd,edh->ebsh', h, ew1) + eb1[:, None, None, :])
        ey = jnp.einsum('ebsh,ehd->ebsd', eh, ew2) + eb2[:, None, None, :]
        mix = jnp.einsum('bse,ebsd->bsd', comb, ey)
        shared = (jax.nn.silu(h @ sw1 + sb1) @ sw2 + sb2) * SHARED_SCALE
        moe_out = mix + shared
        fh = layer_norm(moe_out, ff_ln_g, ff_ln_b)
        ff_out = jax.nn.silu(fh @ ff_w1 + ff_b1) @ ff_w2 + ff_b2
        return x + moe_out + ff_out
    h = _L0_tok_ref(x, L0_tok_W, L0_tok_b)
    h = jnp.concatenate([jnp.broadcast_to(cls_tok, (h.shape[0], 1, h.shape[2])), h], axis=1)
    h = h + _L0_attn_ref(_layernorm(h, axis=-1), L0_attn_w_qkv, L0_attn_w_proj, L0_attn_b_proj)
    h = h + _L0_ffn_ref(_layernorm(h, axis=-1), L0_ffn_router_w, L0_ffn_router_b, L0_ffn_w1, L0_ffn_b1, L0_ffn_w2, L0_ffn_b2)
    h = h + _L1_attn_ref(_layernorm(h, axis=-1), L1_attn_qkv_w, L1_attn_proj_w, L1_attn_proj_b, L1_attn_ps_w1, L1_attn_ps_b1, L1_attn_ps_w2, L1_attn_ps_b2, L1_attn_ps_w3, L1_attn_ps_b3, L1_attn_pattern_bias, L1_attn_sparse_w, L1_attn_sparse_b)
    h = h + _L1_ffn_ref(_layernorm(h, axis=-1), L1_ffn_ln_in_g, L1_ffn_ln_in_b, L1_ffn_router_w, L1_ffn_router_b, L1_ffn_ew1, L1_ffn_eb1, L1_ffn_ew2, L1_ffn_eb2, L1_ffn_sw1, L1_ffn_sb1, L1_ffn_sw2, L1_ffn_sb2, L1_ffn_ff_ln_g, L1_ffn_ff_ln_b, L1_ffn_ff_w1, L1_ffn_ff_b1, L1_ffn_ff_w2, L1_ffn_ff_b2)
    return h

_drawn_inputs = setup_inputs


def setup_inputs(seed=0):
    import zlib

    import numpy as np

    out = dict(_drawn_inputs(seed))
    spreads = {'L0_ffn_router_b': (0.0, 0.1),
     'L1_attn_proj_b': (0.0, 0.1),
     'L1_attn_ps_b1': (0.0, 0.1),
     'L1_attn_ps_b2': (0.0, 0.1),
     'L1_attn_sparse_b': (0.0, 0.1),
     'L1_ffn_ln_in_g': (1.0, 0.6),
     'L1_ffn_ln_in_b': (0.0, 0.8),
     'L1_ffn_router_b': (0.0, 0.69),
     'L1_ffn_eb1': (0.0, 0.8),
     'L1_ffn_eb2': (0.0, 0.544),
     'L1_ffn_sb1': (0.0, 0.8),
     'L1_ffn_sb2': (0.0, 1.233),
     'L1_ffn_ff_ln_g': (1.0, 0.6),
     'L1_ffn_ff_ln_b': (0.0, 2.0),
     'L1_ffn_ff_b1': (0.0, 0.703),
     'L1_ffn_ff_b2': (0.0, 0.31)}
    factors = {'L0_tok_b': 4.13,
     'L0_ffn_b1': 3.453,
     'L1_attn_qkv_w': 3.556,
     'L1_attn_proj_w': 3.535,
     'L1_attn_ps_b3': 6.617,
     'L1_ffn_router_w': 3.691,
     'L1_ffn_ew1': 7.015,
     'L1_ffn_ew2': 6.463,
     'L1_ffn_sw1': 6.044,
     'L1_ffn_sw2': 5.492}
    for name, (base, spread) in spreads.items():
        noise = np.random.default_rng([zlib.crc32(name.encode()), seed]).standard_normal(out[name].shape)
        drawn = base * np.exp(spread * noise) if base else spread * noise
        out[name] = jnp.asarray(drawn.astype(out[name].dtype))
    for name, factor in factors.items():
        out[name] = (out[name] * factor).astype(out[name].dtype)
    return out
```

```python
from contextlib import ExitStack

import concourse.bass as bass
from concourse import mybir

F32 = mybir.dt.float32
BF16 = mybir.dt.bfloat16
I32 = mybir.dt.int32
U32 = mybir.dt.uint32
ALU = mybir.AluOpType
ACT = mybir.ActivationFunctionType
AX = mybir.AxisListType

P = 128
D = 128
IMAGES = 128
CHANNELS, SIDE, PATCH = 3, 64, 16
GRID = SIDE // PATCH
PATCHES = GRID * GRID
SEQ = PATCHES + 1
TOKENS = IMAGES * SEQ
HEADS = 8
HDIM = D // HEADS
IPT = P // SEQ
TT = IPT * SEQ
ROWS = (P, TT)
TILES = (SEQ, -(-TOKENS // TT))
LAST = TOKENS - (TILES[1] - 1) * TT
PADDED = TILES[1] * TT
G = 4
GROUPS = tuple(-(-t // G) for t in TILES)
PIX = PATCH * PATCH * CHANNELS // P
FF = 512
FC = FF // P
SHARED = 256
SC = SHARED // P
WINDOW = 64
HALF = WINDOW // 2
KEEP = max(1, min(SEQ, int(SEQ * (1.0 - 0.3))))
DROP = SEQ - KEEP
EXPERTS = (8, 16)
TEMPERATURE = (1.0, 0.7)
PATTERN_TEMPERATURE = 0.3
PAIRS = 2 * TOKENS
SLOT_TILES = tuple((PAIRS + E * (P - 1)) // P for E in EXPERTS)
MAX_SLOT_TILES = max(SLOT_TILES)
SLOT_GROUPS = tuple(-(-t // G) for t in SLOT_TILES)
NEG = -1e30
EPS = 1e-5

MIXED_ROWS = [r for r in range(SEQ) if 8 * (r % 8) < SEQ]
QHEADS = max(r // 8 for r in MIXED_ROWS) + 1
QKV0 = QHEADS * HDIM + 2 * D


def position_of_window_row(w):
    return (w + HALF) % SEQ


def vit_tower(nc, a, out):
    with ExitStack() as ctx:
        def sb(name, shape, dt=F32):
            return ctx.enter_context(nc.sbuf_tensor(name, shape, dt))

        residual_dram = nc.dram_tensor("residual_tokens", [PADDED, D], F32).ap()
        choice_dram = nc.dram_tensor("choice_tokens", [PADDED, 4], F32).ap()
        xs_dram = nc.dram_tensor("expert_in", [MAX_SLOT_TILES * P, D], F32).ap()
        ys_dram = nc.dram_tensor("expert_out", [MAX_SLOT_TILES * P, D], F32).ap()

        region = sb("region", [P, 24576])
        scratch = sb("scratch", [P, 9520])
        W1 = [region[:, 0:4096].rearrange("p (e f) -> p e f", e=8),
              region[:, 16384:24576].rearrange("p (e f) -> p e f", e=16)]
        W2 = [region[:, 4096:8192].rearrange("p (e c d) -> p e c d", e=8, c=FC),
              region[:, 0:8192].rearrange("p (e c d) -> p e c d", e=16, c=FC)]
        B1 = [region[:, 8192:12288].rearrange("p (e f) -> p e f", e=8),
              region[:, 8192:16384].rearrange("p (e f) -> p e f", e=16)]
        B2 = [region[:, 12288:13312].rearrange("p (e d) -> p e d", e=8), scratch[:, 7472:9520].rearrange("p (e d) -> p e d", e=16)]
        pixels = region[:, 8192:8192 + PATCHES * PIX * IMAGES].rearrange("p (n c b) -> p n c b", n=PATCHES, c=PIX)
        prods = region[:, 16384:16384 + SEQ * QHEADS * D].rearrange("p (w x) -> p w x", w=SEQ)

        R = sb("residual", [P, TILES[1], D])
        Z = sb("normed", [P, TILES[1], D])
        Y0 = scratch[:, 0:TILES[1] * D].rearrange("p (t d) -> p t d", t=TILES[1])
        Y1 = scratch[:, TILES[1] * D:2 * TILES[1] * D].rearrange("p (t d) -> p t d", t=TILES[1])
        qkv0 = scratch[:, 0:SEQ * QKV0].rearrange("p (t x) -> p t x", t=SEQ)
        s0 = scratch[:, 5168:5576].rearrange("p (w h g) -> p w h g", w=SEQ, h=QHEADS)
        p0 = scratch[:, 5576:5984].rearrange("p (w h g) -> p w h g", w=SEQ, h=QHEADS)
        mixed = scratch[:, 5984:5984 + QHEADS * 3 * D].rearrange("p (h x) -> p h x", h=QHEADS)
        mixedT = scratch[:, 7136:7136 + len(MIXED_ROWS) * P].rearrange("p (r b) -> p r b", b=P)
        Kbd = scratch[:, 0:3808].rearrange("p (g h t) -> p g h t", g=G, h=HEADS)
        Pf = scratch[0:TT, 3808:7616].rearrange("p (g h t) -> p g h t", g=G, h=HEADS)
        PT = scratch[0:TT, 7616:9520].rearrange("p (s h t) -> p s h t", s=2, h=HEADS)
        NK = G * HEADS * SEQ
        drop_key, drop_ge, drop_eq, drop_cum = (
            scratch[0:TT, k * NK:(k + 1) * NK].rearrange("p (r j) -> p r j", j=SEQ) for k in range(4))
        top8 = scratch[0:TT, 4 * NK:4 * NK + 8 * G * HEADS].rearrange("p (r k) -> p r k", k=8)
        drop_n = scratch[0:TT, 4 * NK + 256:4 * NK + 256 + G * HEADS]
        Y0_, Y1_ = (region[:, 8192 + k * TILES[1] * D:8192 + (k + 1) * TILES[1] * D].rearrange("p (t d) -> p t d", t=TILES[1])
                    for k in range(2))
        Y = [(Y0_, Y1_), (Y0, Y1)]

        def small(k, shape):
            n = 1
            for x in shape:
                n *= x
            v = scratch[:, 336 * k:336 * k + n]
            return v if len(shape) == 1 else v.rearrange("p (a b) -> p a b", b=shape[1])
        xs = scratch[:, 0:512].rearrange("p (g d) -> p g d", g=G)
        xsT = scratch[:, 512:1024].rearrange("p (g d) -> p g d", g=G)
        hid = scratch[:, 1024:3072].rearrange("p (g f) -> p g f", g=G)
        hidT = scratch[:, 3072:5120].rearrange("p (g f) -> p g f", g=G)
        ys = scratch[:, 5120:5632].rearrange("p (g d) -> p g d", g=G)
        heads = sb("heads", [P, 2452])
        qk = heads[:, 0:952].rearrange("p (g a t) -> p g a t", g=G, a=2)
        vs = heads[0:TT, 952:1464].rearrange("p (g d) -> p g d", g=G)
        osb = heads[0:TT, 1464:1976].rearrange("p (g d) -> p g d", g=G)
        oT = heads[:, 1976:2452].rearrange("p (g t) -> p g t", g=G)
        tokT = heads[:, 0:PIX * D].rearrange("p (c d) -> p c d", c=PIX)
        S = heads[:, 0:TILES[1] * D].rearrange("p (t d) -> p t d", t=TILES[1])
        packed_heads = sb("packed_heads", [P, 2, G * HEADS * SEQ])
        Sc, Pc = (packed_heads[0:TT, k, :].rearrange("p (r j) -> p r j", j=SEQ) for k in range(2))
        zeros = packed_heads[:].rearrange("p k x -> p (k x)")[:, 0:7 * P]
        fhid = scratch[:, 4864:6912].rearrange("p (g f) -> p g f", g=G)
        fhidT = scratch[:, 6912:8960].rearrange("p (g f) -> p g f", g=G)

        qkvT = [sb("qkv_T0", [P, QKV0])[:], sb("qkv_T1", [P, 3 * D])[:]]
        projT = [sb("proj_T0", [P, D])[:], sb("proj_T1", [P, D])[:]]
        ps1T, ps2T, ps3T = sb("ps1_T", [P, D]), sb("ps2_T", [P, 64]), sb("ps3_T", [64, 3])
        router_w = [sb("router_w0", [P, 8]), sb("router_w1", [P, 16])]
        sw1, sw2 = sb("shared_w1", [P, SHARED]), sb("shared_w2", [P, SC, D])
        fw1, fw2 = sb("ff_w1", [P, FF]), sb("ff_w2", [P, FC, D])
        rows = sb("bias_rows", [P, 2096])
        at, row = 0, {}
        for name, n in (("L0_tok_b", D), ("cls_tok", D), ("L0_attn_b_proj", D), ("L0_ffn_router_b", 8),
                        ("L1_attn_proj_b", D), ("L1_ffn_router_b", 16), ("L1_ffn_ln_in_g", D),
                        ("L1_ffn_ln_in_b", D), ("L1_attn_ps_b3", 3), ("L1_attn_pattern_bias", 3),
                        ("L1_attn_sparse_w", HEADS), ("L1_attn_sparse_b", HEADS), ("L1_ffn_sb1", SHARED),
                        ("L1_ffn_sb2", D), ("L1_ffn_ff_ln_g", D), ("L1_ffn_ff_ln_b", D),
                        ("L1_ffn_ff_b1", FF), ("L1_ffn_ff_b2", D)):
            row[name] = rows[:, at:at + n]
            at += n
        proj_b = [row["L0_attn_b_proj"], row["L1_attn_proj_b"]]
        router_b = [row["L0_ffn_router_b"], row["L1_ffn_router_b"]]
        cols = sb("bias_columns", [P, 2])
        pattern_b = sb("pattern_b", [P, 3])
        minus_sparse = sb("minus_sparse", [P, 2, HEADS])

        ident = sb("identity", [P, P])
        own = sb("own_image", [TT, IPT])
        own_rows_f = sb("own_rows_f", [IPT, TT])
        own_rows = sb("own_rows", [IPT, TT], BF16)
        other = sb("other_image", [IPT, 4, TT], BF16)
        head_rows = sb("head_rows", [P, HEADS])
        before = sb("before", [P, P], BF16)
        ones_b = sb("ones_b", [P, P], BF16)
        ones_f = sb("ones_f", [P, 16 * (TILES[1] + 1)])
        carry = sb("carry", [TT, G * HEADS, SEQ])
        is_last = sb("is_last", [P, 1])
        pool_mean = sb("pool_mean", [TT, TT])
        slot0 = sb("slot0", [P, G * SLOT_GROUPS[1]])
        slot0_i = sb("slot0_i", [P, G * SLOT_GROUPS[1]], I32)
        radix = sb("radix", [1, G])
        falling = sb("falling", [P, 16])
        falling_i = sb("falling_i", [P, 16], I32)
        mhalf = sb("mhalf", [P, G])
        eps = sb("eps", [P, G])
        carrier = sb("carrier", [1, 4])

        stats = sb("stats", [P, G, 6])
        mv = sb("mean_var", [P, G, 2])
        ve = sb("var_eps", [P, G])
        rs = sb("rstd", [P, G])
        xn = sb("xn", [P, G, D])
        xnT = sb("xnT", [P, G, D])
        Rb = sb("residual_bias", [P, G, D])
        mx = sb("row_max", [P, 52])
        sm = sb("row_sum", [P, 52])
        l3 = sb("pattern_logits", [TT, G, 3])
        e3 = sb("pattern_weights", [TT, G, 3])
        g1 = sb("gate_tmp", [TT, G])
        g2 = sb("gate", [TT, G])
        logits = sb("logits", [P, TILES[1], 16])
        choice = sb("choice", [P, TILES[1], 4])
        routed = sb("routed", [P, TILES[1], 16], BF16)
        count_i = sb("count_i", [P, 2, 16], I32)
        expert_of = sb("expert_of", [1, SLOT_GROUPS[1]], I32)

        M = ctx.enter_context(nc.psum_tensor("M", [P, 4, 512], F32))
        PS = ctx.enter_context(nc.psum_tensor("PS", [P, 2, 1024], F32))

        def sem(name):
            return ctx.enter_context(nc.semaphore(name))

        consts, pool_step, dve_step, tok_w_loaded, tok_rows_loaded = (
            sem(n) for n in ("consts", "pool_step", "dve_step", "tok_w_loaded", "tok_rows_loaded"))
        rows_loaded, l0_loaded, l1_loaded, zero_stored = (
            sem(n) for n in ("rows_loaded", "l0_loaded", "l1_loaded", "zero_stored"))
        own_ps, pool_ready, emb_ps, emb_sb, cls_set = (
            sem(n) for n in ("own_ps", "pool_ready", "emb_ps", "emb_sb", "cls_set"))
        mean_var_ready, rstd_ready, xn_ready, xnT_ps, xnT_sb = (
            sem(n) for n in ("mean_var_ready", "rstd_ready", "xn_ready", "xnT_ps", "xnT_sb"))
        qkv_ps, qkv0_sb, qk_sb, v_sb, kbd = (
            sem(n) for n in ("qkv_ps", "qkv0_sb", "qk_sb", "v_sb", "kbd"))
        rb_ready, scores_ps, packed, shifted = (
            sem(n) for n in ("rb_ready", "scores_ps", "packed", "shifted"))
        exp_done, probs, spread, pT_ps, pT_sb = (
            sem(n) for n in ("exp_done", "probs", "spread", "pT_ps", "pT_sb"))
        o_ps, o_sb, oT_ps, oT_sb, proj_ps = (
            sem(n) for n in ("o_ps", "o_sb", "oT_ps", "oT_sb", "proj_ps"))
        z_ready, zg_ready, zT_ps, zT_sb, logit_ps = (
            sem(n) for n in ("z_ready", "zg_ready", "zT_ps", "zT_sb", "logit_ps"))
        logits_ready = sem("logits_ready")
        products, s0_shifted, p0_exp, p0_ready, weighted = (
            sem(n) for n in ("products", "s0_shifted", "p0_exp", "p0_ready", "weighted"))
        mixed_ready, mixedT_ps, mixedT_sb, proj0_ps, attn0_done = (
            sem(n) for n in ("mixed_ready", "mixedT_ps", "mixedT_sb", "proj0_ps", "attn0_done"))
        rb0_ready, pl_sb, h1_ps, h1_sb, h2_ps = (
            sem(n) for n in ("rb0_ready", "pl_sb", "h1_ps", "h1_sb", "h2_ps"))
        h2_sb, l3_ps, l3_shifted, e3_done = (
            sem(n) for n in ("h2_sb", "l3_ps", "l3_shifted", "e3_done"))
        route_shifted, route_exp, routed_ready, rank_ps, routing_ready = (
            sem(n) for n in ("route_shifted", "route_exp", "routed_ready", "rank_ps", "routing_ready"))
        choice_stored, choice_loaded = (
            sem(n) for n in ("choice_stored", "choice_loaded"))
        residual_stored, residual_loaded, scattered, w0_loaded, w1a_loaded = (
            sem(n) for n in ("residual_stored", "residual_loaded", "scattered", "w0_loaded", "w1a_loaded"))
        w1b_loaded, b2_loaded = (
            sem(n) for n in ("w1b_loaded", "b2_loaded"))
        xs_in, xsT_ps, xsT_sb, up_ps, hid_biased = (
            sem(n) for n in ("xs_in", "xsT_ps", "xsT_sb", "up_ps", "hid_biased"))
        hid_ready, hT_ps, hT_sb, y_ps, y_sb = (
            sem(n) for n in ("hid_ready", "hT_ps", "hT_sb", "y_ps", "y_sb"))
        experts_added = sem("experts_added")
        y_stored, gathered, combined, shared_ready = (
            sem(n) for n in ("y_stored", "gathered", "combined", "shared_ready"))
        out_stored = sem("out_stored")
        pixels_in = [ctx.enter_context(nc.semaphore(f"pixels_in{g}")) for g in range(4)]

        block = ctx.enter_context(nc.Block())

        class Seq:
            def __init__(self, eng, sem):
                self.eng, self.sem, self.at, self.n = eng, sem, 0, 0

            def mark(self, ins):
                ins.then_inc(self.sem, 1)
                self.at = self.at + 1
                self.n += 1

            def sync(self):
                self.eng.wait_ge(self.sem, self.at)

            def step(self, ins):
                self.mark(ins)
                self.sync()

        def groups(eng, tiles, body, seq=None, steps=0, peel=False):
            whole, rest = divmod(tiles, G)
            start, n = (seq.at, seq.n) if seq else (0, 0)
            if peel:
                body(0, 0, G)
                n = seq.n if seq else 0
            with eng.Fori(1 if peel else 0, whole) as i:
                if seq:
                    seq.at = start + i * steps
                body(i * G, i, G)
            if seq:
                assert seq.n - n == steps, (seq.n - n, steps)
                seq.at = start + whole * steps
            if rest:
                body(whole * G, whole, rest)

        def pipelined(eng, tiles, body):
            whole, rest = divmod(tiles, G)
            body(0, 0, G, G)
            with eng.Fori(1, whole - 1) as i:
                body(i * G, i, G, G)
            body((whole - 1) * G, whole - 1, G, rest)
            if rest:
                body(whole * G, whole, rest, 0)

        def experts_of_group(eng, layer, grp, n):
            packed_ = eng.value_load(expert_of[0:1, bass.ds(grp, 1)], min_val=0, max_val=16 ** G - 1)
            return [(packed_ >> (4 * g)) & (EXPERTS[layer] - 1) for g in range(n)]

        hT_bank = [PS[:, b // 2, 512 * (b % 2):512 * (b % 2) + 512] for b in (0, 1, 2, 0)]
        xsT_bank = PS[:, 1, 512:1024].rearrange("p (g d) -> p g d", g=G)

        def is_zero(t0):
            return isinstance(t0, int) and t0 == 0

        def tile(T, t, rows):
            return T[0:rows, bass.ds(t, 1), :].rearrange("p a d -> p (a d)")

        LT = (0, TILES[0])
        LG = (0, GROUPS[0])
        LS = (0, SLOT_TILES[0])
        LSG = (0, SLOT_GROUPS[0])
        H = (0, SLOT_TILES[0] + TILES[1])
        HS, HF = SLOT_TILES[0], SLOT_TILES[0] + TILES[1] + SLOT_TILES[1]

        @block.sync
        def _(sp):
            def load(dst, name, sem):
                sp.dma_start(dst, a[name]).then_inc(sem, 16)

            def load_rows(*names, sem=rows_loaded):
                for name in names:
                    v = a[name] if len(a[name].shape) == 1 else a[name].rearrange("a b d -> (a b d)")
                    sp.dma_start(row[name], v.partition_broadcast(P)).then_inc(sem, 16)

            load(tokT, "L0_tok_W", tok_w_loaded)
            for g in range(4):
                sp.dma_start(pixels[:, 4 * g:4 * g + 4], a["x"][:, 4 * g:4 * g + 4]).then_inc(pixels_in[g], 16)
                if g == 0:
                    load_rows("L0_tok_b", "cls_tok", sem=tok_rows_loaded)
            load_rows("L0_attn_b_proj", "L0_ffn_router_b")
            load(qkvT[0], "L0_attn_w_qkv", l0_loaded)
            load(projT[0], "L0_attn_w_proj", l0_loaded)
            load(router_w[0][:], "L0_ffn_router_w", l0_loaded)
            load(W1[0], "L0_ffn_w1", w0_loaded)
            load(W2[0], "L0_ffn_w2", w0_loaded)
            sp.wait_ge(consts, 1)
            zrows = xs_dram.rearrange("(k p) d -> p k d", p=P)
            for k in range(0, MAX_SLOT_TILES, 7):
                sp.dma_start(zrows[:, k:k + 7, :], zeros.rearrange("p (k d) -> p k d", k=7)).then_inc(zero_stored, 16)
            sp.dma_start(residual_dram[TOKENS:PADDED, :], zeros[0:PADDED - TOKENS, 0:D]).then_inc(zero_stored, 16)
            sp.dma_start(choice_dram[TOKENS:PADDED, :], zeros[0:PADDED - TOKENS, 0:4]).then_inc(zero_stored, 16)
            load(qkvT[1], "L1_attn_qkv_w", l1_loaded)
            load(projT[1], "L1_attn_proj_w", l1_loaded)
            load(ps1T[:], "L1_attn_ps_w1", l1_loaded)
            load(ps2T[:], "L1_attn_ps_w2", l1_loaded)
            load(ps3T[:], "L1_attn_ps_w3", l1_loaded)
            load(router_w[1][:], "L1_ffn_router_w", l1_loaded)
            load(sw1[:], "L1_ffn_sw1", l1_loaded)
            load(sw2[:], "L1_ffn_sw2", l1_loaded)
            load(fw1[:], "L1_ffn_ff_w1", l1_loaded)
            load(fw2[:], "L1_ffn_ff_w2", l1_loaded)
            sp.dma_start(cols[:, 0:1], a["L1_attn_ps_b1"].unsqueeze(1)).then_inc(l1_loaded, 16)
            sp.dma_start(cols[0:64, 1:2], a["L1_attn_ps_b2"].unsqueeze(1)).then_inc(l1_loaded, 16)
            load_rows("L1_attn_proj_b", "L1_ffn_router_b", "L1_ffn_ln_in_g", "L1_ffn_ln_in_b", "L1_attn_ps_b3",
                      "L1_attn_pattern_bias", "L1_attn_sparse_w", "L1_attn_sparse_b", "L1_ffn_sb1", "L1_ffn_sb2",
                      "L1_ffn_ff_ln_g", "L1_ffn_ff_ln_b", "L1_ffn_ff_b1", "L1_ffn_ff_b2")
            sp.wait_ge(emb_ps, PATCHES)
            sp.dma_start(B1[0], a["L0_ffn_b1"].partition_broadcast(P)).then_inc(w0_loaded, 16)
            sp.dma_start(B2[0], a["L0_ffn_b2"].partition_broadcast(P)).then_inc(w0_loaded, 16)

            def experts(layer):
                tiles_of = lambda d, t0, n: d.rearrange("(k p) d -> p k d", p=P)[:, bass.ds(t0, n), :]

                def take(grp, n):
                    if layer or not is_zero(grp):
                        sp.wait_ge(xsT_ps, LSG[layer] + grp)
                    sp.dma_start(xs[:, 0:n, :], tiles_of(xs_dram, grp * G, n)).then_inc(xs_in, 16)

                def put(grp, n):
                    sp.wait_ge(y_sb, LS[layer] + grp * G + n)
                    sp.dma_start(tiles_of(ys_dram, grp * G, n), ys[:, 0:n, :]).then_inc(y_stored, 16)
                sp.wait_ge(scattered, 32 * (LT[layer] + TILES[layer]))
                sp.wait_ge(routing_ready, layer + 1)
                whole, rest = divmod(SLOT_TILES[layer], G)
                take(0, G)
                take(1, G)
                with sp.Fori(2, whole) as i:
                    take(i, G)
                    put(i - 2, G)
                if rest:
                    take(whole, rest)
                put(whole - 2, G)
                put(whole - 1, G)
                if rest:
                    put(whole, rest)

            sp.wait_ge(attn0_done, 1)
            sp.dma_start(residual_dram[0:TOKENS, :].rearrange("(b j) d -> b j d", j=SEQ), R[:, 0:SEQ, :])\
              .then_inc(residual_stored, 16)
            sp.dma_start(W1[1], a["L1_ffn_ew1"]).then_inc(w1a_loaded, 16)
            sp.wait_ge(routing_ready, 1)
            sp.dma_start(choice_dram[0:TOKENS, :].rearrange("(b j) c -> b (j c)", j=SEQ),
                         choice[:, 0:SEQ, :].rearrange("p t c -> p (t c)")).then_inc(choice_stored, 16)
            sp.wait_ge(residual_stored, 16)
            sp.wait_ge(zero_stored, 16 * (MAX_SLOT_TILES // 7 + 2))
            sp.wait_ge(logits_ready, TILES[0])
            sp.dma_start(R[0:TT, :, :], residual_dram.rearrange("(t p) d -> p t d", p=TT)).then_inc(residual_loaded, 16)
            experts(0)
            sp.wait_ge(choice_stored, 16)
            sp.dma_start(choice[0:TT, :, :], choice_dram.rearrange("(t p) c -> p t c", p=TT)).then_inc(choice_loaded, 16)
            sp.wait_ge(y_sb, SLOT_TILES[0])
            sp.dma_start(W2[1], a["L1_ffn_ew2"]).then_inc(w1b_loaded, 16)
            sp.wait_ge(experts_added, GROUPS[1])
            sp.dma_start(B1[1], a["L1_ffn_eb1"].partition_broadcast(P)).then_inc(w1b_loaded, 16)
            sp.wait_ge(logits_ready, TILES[0] + TILES[1])
            sp.dma_start(B2[1], a["L1_ffn_eb2"].partition_broadcast(P)).then_inc(b2_loaded, 16)
            experts(1)
            sp.wait_ge(combined, TILES[1])

            o = out.rearrange("b j d -> (b j) d")
            sp.dma_start(o[0:(TILES[1] - 1) * TT, :].rearrange("(t p) d -> p t d", p=TT),
                         Z[0:TT, 0:TILES[1] - 1, :]).then_inc(out_stored, 16)
            sp.dma_start(o[(TILES[1] - 1) * TT:TOKENS, :], Z[0:LAST, TILES[1] - 1, :]).then_inc(out_stored, 16)
            sp.wait_ge(out_stored, 32)

        @block.gpsimd
        def _(pool):
            seq = Seq(pool, pool_step)
            pool.memset(zeros, 0.0).then_inc(consts, 1)
            seq.mark(pool.memset(ident[:], 0.0))
            seq.mark(pool.memset(own[:], 1.0))
            seq.mark(pool.memset(own_rows_f[:], 1.0))
            seq.mark(pool.memset(head_rows[:], float(HDIM) ** -0.5))
            seq.mark(pool.memset(before[:], 1.0))
            seq.mark(pool.memset(is_last[:], 1.0))
            seq.mark(pool.memset(ones_b[:], 1.0))
            seq.mark(pool.memset(ones_f[:], 1.0))
            seq.mark(pool.memset(mhalf[:], -0.5))
            seq.mark(pool.memset(eps[:], EPS))
            seq.mark(pool.memset(carrier[:], 0.0))
            seq.mark(pool.memset(carry[:], 1.0))
            seq.mark(pool.memset(mixed, 0.0))
            seq.mark(pool.iota(slot0_i[:], pattern=[[P, G * SLOT_GROUPS[1]]], base=0, channel_multiplier=0))
            for g in range(G):
                seq.mark(pool.memset(radix[:, g:g + 1], 16.0 ** g))
            seq.mark(pool.iota(falling_i[:], pattern=[[-1, 16]], base=16, channel_multiplier=0))
            seq.sync()

            def keep(t, pattern, base, mult, op=ALU.is_ge, fill=0.0):
                seq.mark(pool.affine_select(out=t, in_=t, compare_op=op, fill=fill, base=base,
                                            pattern=pattern, channel_multiplier=mult))
            keep(ident[:], [[-1, P]], 0, 1, ALU.not_equal, 1.0)
            keep(own[:], [[-SEQ, IPT]], 0, 1)
            keep(own_rows_f[:], [[1, TT]], 0, -SEQ)
            keep(head_rows[:], [[-HDIM, HEADS]], 0, 1)
            keep(before[:], [[1, P]], -1, -1)
            keep(is_last[:], [[0, 1]], LAST - 1, -1)
            seq.mark(pool.memset(carry[:, :, 0:1], 0.0))
            seq.mark(pool.tensor_copy(slot0[:], slot0_i[:]))
            seq.mark(pool.tensor_copy(falling[:], falling_i[:]))
            seq.sync()
            keep(own[:], [[SEQ, IPT]], SEQ - 1, -1)
            keep(own_rows_f[:], [[-1, TT]], SEQ - 1, SEQ)
            keep(head_rows[:], [[HDIM, HEADS]], HDIM - 1, -1)
            seq.sync()
            seq.mark(pool.tensor_copy(own_rows[:], own_rows_f[:]))
            for h in range(4):
                seq.mark(pool.tensor_scalar(other[:, h, :], own_rows_f[:], -1.0, -NEG, ALU.add, ALU.mult))
            seq.sync()
            pool.memset(carrier[:], 0.0).then_inc(consts, 1)

            def norm_rstd(n, rws, at):
                pool.wait_ge(mean_var_ready, at)
                seq.step(pool.tensor_tensor(ve[0:rws, 0:n], mv[0:rws, 0:n, 1], eps[0:rws, 0:n], ALU.add))
                pool.tensor_tensor(rs[0:rws, 0:n], ve[0:rws, 0:n], mhalf[0:rws, 0:n], ALU.pow).then_inc(rstd_ready, 1)

            def attention0():
                pool.wait_ge(emb_sb, PATCHES)
                pool.wait_ge(cls_set, 1)
                groups(pool, TILES[0], lambda t0, grp, n: norm_rstd(n, P, grp + 1), seq, 1)
                pool.wait_ge(xn_ready, TILES[0])
                pool.wait_ge(rows_loaded, 16 * 16)
                pool.tensor_tensor(R[:, 0:SEQ, :], R[:, 0:SEQ, :],
                                   proj_b[0].unsqueeze(1).broadcast_to([P, SEQ, D]), ALU.add).then_inc(rb0_ready, 1)
                for w in range(SEQ):
                    t = position_of_window_row(w)
                    pool.wait_ge(qkv0_sb, t + 1)
                    q = qkv0[:, t, 0:QHEADS * HDIM].rearrange("p (h d) -> p h d", h=QHEADS)
                    k = qkv0[:, t, QHEADS * HDIM:QHEADS * HDIM + D].rearrange("p (g d) -> p g d", g=HEADS)
                    pool.tensor_tensor(prods[:, w, :].rearrange("p (h g d) -> p h g d", h=QHEADS, g=HEADS),
                                       q.unsqueeze(2).broadcast_to([P, QHEADS, HEADS, HDIM]),
                                       k.unsqueeze(1).broadcast_to([P, QHEADS, HEADS, HDIM]),
                                       ALU.mult).then_inc(products, 1)
                pool.wait_ge(p0_ready, 1)
                for w in range(SEQ):
                    t = position_of_window_row(w)
                    v = qkv0[:, t, QHEADS * HDIM + D:QKV0].rearrange("p (g d) -> p d g", g=HEADS)
                    pool.tensor_tensor(prods[:, w, :].rearrange("p (h d g) -> p h d g", h=QHEADS, g=HEADS),
                                       p0[:, w].unsqueeze(2).broadcast_to([P, QHEADS, HDIM, HEADS]),
                                       v.unsqueeze(1).broadcast_to([P, QHEADS, HDIM, HEADS]),
                                       ALU.mult).then_inc(weighted, 1)
                groups(pool, TILES[0], lambda t0, grp, n: norm_rstd(n, P, GROUPS[0] + grp + 1), seq, 1)

            def attention1():
                pool.wait_ge(l1_loaded, 16 * 12)
                for grp in range(GROUPS[1]):
                    t0, n = grp * G, min(G, TILES[1] - grp * G)
                    pool.wait_ge(experts_added, grp + 1)
                    norm_rstd(n, TT, 2 * GROUPS[0] + 3 * grp + 1)
                    for g in range(n):
                        ins = pool.tensor_tensor(Rb[0:TT, g, :], R[0:TT, t0 + g, :], proj_b[1][0:TT, :], ALU.add)
                    ins.then_inc(rb_ready, 1)
                    for g in range(n):
                        pool.wait_ge(qk_sb, t0 + g + 1)
                        pool.tensor_tensor(Kbd[:, g], qk[:, g, 1:2, :].broadcast_to([P, HEADS, TT]),
                                           head_rows[:].unsqueeze(2).broadcast_to([P, HEADS, TT]),
                                           ALU.mult).then_inc(kbd, 1)
                    if grp + 2 < GROUPS[1]:
                        gather(0, grp + 2)
                    for g in range(n):
                        pool.wait_ge(probs, t0 + g + 1)
                        pool.tensor_tensor(
                            Pf[:, g].rearrange("p h (i j) -> p h i j", i=IPT),
                            Pc[:, g * HEADS:(g + 1) * HEADS, :].unsqueeze(2).broadcast_to([TT, HEADS, IPT, SEQ]),
                            own[:].unsqueeze(1).unsqueeze(3).broadcast_to([TT, HEADS, IPT, SEQ]),
                            ALU.mult).then_inc(spread, 1)
                    norm_rstd(n, TT, 2 * GROUPS[0] + 3 * grp + 2)
                    norm_rstd(n, TT, 2 * GROUPS[0] + 3 * grp + 3)

            def rows_of(layer, t):
                return ROWS[layer] if layer == 0 or t < TILES[1] - 1 else LAST

            def scatter(layer):
                pool.wait_ge(routing_ready, layer + 1)
                pool.wait_ge(zero_stored, 16 * (MAX_SLOT_TILES // 7 + 2))
                for t in range(TILES[layer]):
                    n = rows_of(layer, t)
                    for k in range(2):
                        pool.indirect_dma_start(
                            out=xs_dram, out_offset=bass.IndirectOffsetOnAxis(ap=choice[0:n, t, k:k + 1].bitcast(U32), axis=0),
                            in_=Z[0:n, t, :], in_offset=None).then_inc(scattered, 16)

            def gather(layer, grp):
                if grp == 0:
                    pool.wait_ge(y_stored, 16 * (LSG[layer] + SLOT_GROUPS[layer]))
                    if layer == 0:
                        pool.wait_ge(choice_loaded, 16)
                else:
                    pool.wait_ge(gathered, 32 * (layer * TILES[1] + G * grp))
                for t in range(G * grp, min(G * (grp + 1), TILES[1])):
                    n = TT if layer == 0 else rows_of(1, t)
                    for k in range(2):
                        pool.indirect_dma_start(
                            out=Y[layer][k][0:n, t, :], out_offset=None, in_=ys_dram[0:SLOT_TILES[layer] * P, :],
                            in_offset=bass.IndirectOffsetOnAxis(ap=choice[0:n, t, k:k + 1].bitcast(U32), axis=0))\
                            .then_inc(gathered, 16)

            attention0()
            scatter(0)
            gather(0, 0)
            gather(0, 1)
            attention1()
            scatter(1)
            gather(1, 0)
            for grp in range(GROUPS[1]):
                if grp + 1 < GROUPS[1]:
                    gather(1, grp + 1)
                norm_rstd(min(G, TILES[1] - G * grp), TT, 2 * GROUPS[0] + 3 * GROUPS[1] + grp + 1)

        @block.tensor
        def _(pe):
            pe.wait_ge(consts, 2)
            pe.matmul(PS[0:TT, 1, 0:TT], own_rows[:], own_rows[:], start=True, stop=True).then_inc(own_ps, 1)
            pe.wait_ge(tok_w_loaded, 16)
            for n in range(PATCHES):
                if n % 4 == 0:
                    pe.wait_ge(pixels_in[n // 4], 16)
                if n >= 4:
                    pe.wait_ge(emb_sb, n - 3)
                for c in range(PIX):
                    ins = pe.matmul(M[:, n % 4, 0:D], pixels[:, n, c, :], tokT[:, c, :],
                                    start=(c == 0), stop=(c == PIX - 1))
                ins.then_inc(emb_ps, 1)
            pe.wait_ge(pool_ready, 1)

            def turn(src, dst, n, rws, ready, base, done):
                for g in range(n):
                    pe.wait_ge(ready, base + g + 1)
                    pe.transpose(dst(g)[:, 0:rws], src[0:rws, g, :], ident[0:rws, 0:rws]).then_inc(done, 1)

            def route_products(layer, n, base):
                E, rws = EXPERTS[layer], ROWS[layer]
                turn(xn, lambda g: M[:, g, :], n, rws, zg_ready, base, zT_ps)
                for g in range(n):
                    pe.wait_ge(zT_sb, base + g + 1)
                    pe.matmul(M[0:rws, g, 0:E], xnT[:, g, 0:rws], router_w[layer][:], start=True, stop=True)\
                        .then_inc(logit_ps, 1)

            def attention0():
                nq = QHEADS * HDIM
                pe.wait_ge(emb_sb, PATCHES)
                pe.wait_ge(l0_loaded, 16 * 3)

                def body(t0, grp, n):
                    if not is_zero(t0):
                        pe.wait_ge(qkv0_sb, t0)
                    turn(xn, lambda g: M[:, g, :], n, P, xn_ready, t0, xnT_ps)
                    for g in range(n):
                        pe.wait_ge(xnT_sb, t0 + g + 1)
                        pe.matmul(M[:, g, 0:QKV0], xnT[:, g, :], qkvT[0], start=True, stop=True).then_inc(qkv_ps, 1)
                groups(pe, TILES[0], body, peel=True)
                pe.wait_ge(mixed_ready, 1)
                for k, r in enumerate(MIXED_ROWS):
                    ins = pe.transpose(PS[:, k // 4, P * (k % 4):P * (k % 4 + 1)],
                                       mixed[:, r // 8, P * (r % 8):P * (r % 8 + 1)], ident[:])
                    if k % 4 == 3 or r == MIXED_ROWS[-1]:
                        ins.then_inc(mixedT_ps, 1)
                for k, r in enumerate(MIXED_ROWS):
                    if k % 4 == 0:
                        pe.wait_ge(mixedT_sb, k // 4 + 1)
                    ins = pe.matmul(M[:, k // 4, P * (k % 4):P * (k % 4 + 1)], mixedT[:, k, :], projT[0],
                                    start=True, stop=True)
                ins.then_inc(proj0_ps, 1)
                groups(pe, TILES[0], lambda t0, grp, n: route_products(0, n, t0))

            def attention1():
                L = LT[1]
                wq, wk, wv = (qkvT[1][:, k * D:(k + 1) * D] for k in range(3))
                pe.wait_ge(l1_loaded, 16 * 12)

                def body(t0, grp, n):
                    turn(xn, lambda g: M[:, g, :], n, TT, xn_ready, L + t0, xnT_ps)
                    for g in range(n):
                        pe.wait_ge(xnT_sb, L + t0 + g + 1)
                        pe.matmul(M[:, g, 0:TT], wq, xnT[:, g, 0:TT], start=True, stop=True)
                        pe.matmul(M[:, g, 120:120 + TT], wk, xnT[:, g, 0:TT], start=True, stop=True)
                        pe.matmul(M[0:TT, g, 256:384], xnT[:, g, 0:TT], wv, start=True, stop=True)
                        pe.matmul(M[:, g, 384:384 + TT], xn[0:TT, g, :], pool_mean[:], start=True, stop=True)\
                            .then_inc(qkv_ps, 1)
                    for g in range(n):
                        pe.wait_ge(pl_sb, t0 + g + 1)
                        pe.matmul(M[:, g, 0:TT], ps1T[:], oT[:, g, :], start=True, stop=True).then_inc(h1_ps, 1)
                    for g in range(n):
                        pe.wait_ge(kbd, t0 + g + 1)
                        if g >= 2:
                            pe.wait_ge(packed, t0 + g - 1)
                        for b in range(2):
                            bank = PS[0:TT, g % 2, 512 * b:512 * b + 4 * TT]
                            pe.matmul(bank, own_rows[:], other[:].rearrange("p h t -> p (h t)"),
                                      start=True, stop=False)
                            ins = pe.matmul(bank, qk[:, g, 0, :],
                                            Kbd[:, g, 4 * b:4 * b + 4, :].rearrange("p h t -> p (h t)"),
                                            start=False, stop=True)
                        ins.then_inc(scores_ps, 1)
                    for g in range(n):
                        pe.wait_ge(h1_sb, t0 + g + 1)
                        pe.matmul(M[0:64, g, 0:TT], ps2T[:], xnT[:, g, 0:TT], start=True, stop=True).then_inc(h2_ps, 1)
                    for g in range(n):
                        pe.wait_ge(h2_sb, t0 + g + 1)
                        pe.matmul(M[0:TT, g, 0:3], oT[0:64, g, :], ps3T[:], start=True, stop=True).then_inc(l3_ps, 1)

                    def turn_probs(g):
                        pe.wait_ge(spread, t0 + g + 1)
                        for h in range(HEADS):
                            o = 512 * (h // 4) + TT * (h % 4)
                            ins = pe.transpose(PS[0:TT, g % 2, o:o + TT], Pf[:, g, h, :], ident[0:TT, 0:TT])
                        ins.then_inc(pT_ps, 1)

                    def probs_values(g):
                        pe.wait_ge(pT_sb, t0 + g + 1)
                        pe.wait_ge(v_sb, t0 + g + 1)
                        for h in range(HEADS):
                            ins = pe.matmul(M[0:TT, g, h * HDIM:(h + 1) * HDIM], PT[:, g % 2, h, :],
                                            vs[:, g, h * HDIM:(h + 1) * HDIM], start=True, stop=True)
                        ins.then_inc(o_ps, 1)
                    for g in range(n):
                        turn_probs(g)
                        if g:
                            probs_values(g - 1)
                    probs_values(n - 1)
                    turn(osb, lambda g: M[:, g, :], n, TT, o_sb, t0, oT_ps)
                    for g in range(n):
                        pe.wait_ge(oT_sb, t0 + g + 1)
                        pe.matmul(M[0:TT, g, 0:D], oT[:, g, :], projT[1], start=True, stop=True).then_inc(proj_ps, 1)
                    route_products(1, n, L + t0)
                groups(pe, TILES[1], body)

            def rank(layer):
                rws, n = ROWS[layer], TILES[layer] * EXPERTS[layer]
                pe.wait_ge(routed_ready, layer + 1)
                chosen = routed[0:rws, 0:TILES[layer], 0:EXPERTS[layer]]
                pe.matmul(PS[0:rws, 0, 0:n], before[0:rws, 0:rws], chosen, start=True, stop=True)
                pe.matmul(PS[0:rws, 1, 0:n], ones_b[0:rws, 0:rws], chosen, start=True, stop=True).then_inc(rank_ps, 1)

            def hidden_down(n, at, hidT_, chunks, rhs, y_sem, ready, hid_, rws):
                def turn_hidden(g):
                    pe.wait_ge(ready, at(g))
                    for c in range(chunks):
                        ins = pe.transpose(hT_bank[g][:, P * c:P * c + rws],
                                           hid_[0:rws, g, P * c:P * (c + 1)], ident[0:rws, 0:rws])
                    ins.then_inc(hT_ps, 1)

                def down(g):
                    pe.wait_ge(hT_sb, at(g))
                    for c in range(chunks):
                        ins = pe.matmul(M[0:rws, g, 0:D], hidT_[:, g, P * c:P * c + rws], rhs(g, c),
                                        start=(c == 0), stop=(c == chunks - 1))
                    ins.then_inc(y_sem, 1)
                for g in range(n):
                    turn_hidden(g)
                    if g:
                        down(g - 1)
                down(n - 1)

            def experts(layer):
                L = LS[layer]

                def turn_inputs(grp, n):
                    pe.wait_ge(xs_in, 16 * (LSG[layer] + grp + 1))
                    for g in range(n):
                        ins = pe.transpose(xsT_bank[:, g, :], xs[:, g, :], ident[:])
                    ins.then_inc(xsT_ps, 1)

                def body(t0, grp, n, n_behind):
                    e = experts_of_group(pe, layer, grp, n)
                    pe.wait_ge(xsT_sb, LSG[layer] + grp + 1)
                    if layer or not is_zero(t0):
                        pe.wait_ge(y_sb, L + t0)
                    for g in range(n):
                        pe.matmul(M[:, g, :], xsT[:, g, :], W1[layer][:, bass.ds(e[g], 1), :].rearrange("p a f -> p (a f)"),
                                  start=True, stop=True).then_inc(up_ps, 1)
                    if n_behind:
                        turn_inputs(grp + 1, n_behind)
                    hidden_down(n, lambda g: H[layer] + t0 + g + 1, hidT, FC,
                                lambda g, c: W2[layer][:, bass.ds(e[g], 1), c, :].rearrange("p a d -> p (a d)"),
                                y_ps, hid_ready, hid, P)
                turn_inputs(0, G)
                pe.wait_ge(w0_loaded, 16 * 4)
                pe.wait_ge(routing_ready, layer + 1)
                if layer:
                    pe.wait_ge(w1a_loaded, 16)
                    pe.wait_ge(w1b_loaded, 32)
                pipelined(pe, SLOT_TILES[layer], body)

            attention0()
            rank(0)
            experts(0)
            attention1()
            rank(1)
            def shared(t0, grp, n):
                turn(xn, lambda g: M[:, g, :], n, TT, zg_ready, LT[1] + TILES[1] + t0, zT_ps)
                for g in range(n):
                    pe.wait_ge(zT_sb, LT[1] + TILES[1] + t0 + g + 1)
                    pe.matmul(M[0:TT, g, 0:SHARED], xnT[:, g, 0:TT], sw1[:], start=True, stop=True).then_inc(up_ps, 1)
                hidden_down(n, lambda g: HS + t0 + g + 1, hidT, SC, lambda g, c: sw2[:, c, :], y_ps,
                            hid_ready, hid, TT)
            groups(pe, TILES[1], shared)
            pe.wait_ge(shared_ready, TILES[1])
            experts(1)

            def last(t0, grp, n):
                turn(xn, lambda g: M[:, g, :], n, TT, zg_ready, LT[1] + 2 * TILES[1] + t0, zT_ps)
                for g in range(n):
                    pe.wait_ge(zT_sb, LT[1] + 2 * TILES[1] + t0 + g + 1)
                    pe.matmul(M[0:TT, g, :], xnT[:, g, 0:TT], fw1[:], start=True, stop=True).then_inc(up_ps, 1)
                hidden_down(n, lambda g: HF + t0 + g + 1, fhidT, FC, lambda g, c: fw2[:, c, :], y_ps,
                            hid_ready, fhid, TT)
            groups(pe, TILES[1], last)

        @block.scalar
        def _(act):
            act.wait_ge(own_ps, 1)
            act.activation(pool_mean[:], PS[0:TT, 1, 0:TT], ACT.Copy, scale=1.0 / SEQ).then_inc(pool_ready, 1)
            act.wait_ge(tok_rows_loaded, 32)
            act.activation(R[:, 0, :], row["cls_tok"], ACT.Copy).then_inc(cls_set, 1)

            def evacuate(n, base, wait, dst, src, sem):
                for g in range(n):
                    act.wait_ge(wait, base + g + 1)
                    act.activation(dst(g), src(g), ACT.Copy).then_inc(sem, 1)

            def turned(n, base, rws, wait, dst, sem):
                evacuate(n, base, wait, lambda g: dst[:, g, 0:rws], lambda g: M[:, g, 0:rws], sem)

            def attention0():
                def body(t0, grp, n):
                    turned(n, t0, P, xnT_ps, xnT, xnT_sb)
                    evacuate(n, t0, qkv_ps, lambda g: tile(qkv0, t0 + g, P), lambda g: M[:, g, 0:QKV0], qkv0_sb)
                groups(act, TILES[0], body)
                act.wait_ge(s0_shifted, 1)
                act.activation(p0, s0, ACT.Exp).then_inc(p0_exp, 1)
                for k in range(2):
                    act.wait_ge(mixedT_ps, k + 1)
                    m = min(4, len(MIXED_ROWS) - 4 * k)
                    act.activation(mixedT[:, 4 * k:4 * k + m, :].rearrange("p r b -> p (r b)"), PS[:, k, 0:m * P],
                                   ACT.Copy).then_inc(mixedT_sb, 1)
                groups(act, TILES[0], lambda t0, grp, n: turned(n, t0, P, zT_ps, xnT, zT_sb))

            def attention1():
                L = LT[1]
                act.wait_ge(l1_loaded, 16 * 12)

                def body(t0, grp, n):
                    turned(n, L + t0, TT, xnT_ps, xnT, xnT_sb)
                    for g in range(n):
                        act.wait_ge(qkv_ps, L + t0 + g + 1)
                        act.activation(qk[:, g], M[:, g, 0:240].rearrange("p (a t) -> p a t", a=2)[:, :, 0:TT],
                                       ACT.Copy).then_inc(qk_sb, 1)
                        act.activation(vs[:, g, :], M[0:TT, g, 256:384], ACT.Copy).then_inc(v_sb, 1)
                        act.activation(oT[:, g, :], M[:, g, 384:384 + TT], ACT.Copy).then_inc(pl_sb, 1)
                    for g in range(n):
                        act.wait_ge(h1_ps, t0 + g + 1)
                        act.activation(xnT[:, g, 0:TT], M[:, g, 0:TT], ACT.Relu, bias=cols[:, 0:1]).then_inc(h1_sb, 1)
                    for g in range(n):
                        act.wait_ge(h2_ps, t0 + g + 1)
                        act.activation(oT[0:64, g, :], M[0:64, g, 0:TT], ACT.Relu, bias=cols[0:64, 1:2]).then_inc(h2_sb, 1)
                    act.wait_ge(l3_shifted, grp + 1)
                    act.activation(e3[:, 0:n, :], l3[:, 0:n, :], ACT.Exp, scale=1.0 / PATTERN_TEMPERATURE).then_inc(e3_done, 1)
                    act.wait_ge(shifted, grp + 1)
                    act.activation(Pc[:, 0:n * HEADS, :], Sc[:, 0:n * HEADS, :], ACT.Exp).then_inc(exp_done, 1)

                    def pT(g):
                        act.wait_ge(pT_ps, t0 + g + 1)
                        act.activation(PT[:, g % 2].rearrange("p (b h) t -> p b (h t)", b=2),
                                       PS[0:TT, g % 2, :].rearrange("p (b x) -> p b x", b=2)[:, :, 0:4 * TT],
                                       ACT.Copy).then_inc(pT_sb, 1)

                    def o(g):
                        act.wait_ge(o_ps, t0 + g + 1)
                        act.activation(osb[:, g, :], M[0:TT, g, 0:D], ACT.Copy).then_inc(o_sb, 1)
                    for g in range(n):
                        pT(g)
                        if g:
                            o(g - 1)
                    o(n - 1)
                    turned(n, t0, TT, oT_ps, oT, oT_sb)
                    turned(n, L + t0, TT, zT_ps, xnT, zT_sb)
                groups(act, TILES[1], body)

            def route(layer):
                n = TILES[layer] * EXPERTS[layer]
                act.wait_ge(route_shifted, layer + 1)
                act.activation(small(1, [n])[0:ROWS[layer]], small(0, [n])[0:ROWS[layer]], ACT.Exp,
                               scale=1.0 / TEMPERATURE[layer]).then_inc(route_exp, 1)

            def hidden(n, func, base, hbase, rws, width, hid_, hidT_):
                for g in range(n):
                    act.wait_ge(hid_biased, hbase + g + 1)
                    act.activation(hid_[0:rws, g, 0:width], hid_[0:rws, g, 0:width], func).then_inc(hid_ready, 1)
                for g in range(n):
                    act.wait_ge(hT_ps, hbase + g + 1)
                    act.activation(hidT_[:, g, 0:width].rearrange("p (c r) -> p c r", r=P)[:, :, 0:rws],
                                   hT_bank[g][:, 0:width].rearrange("p (c r) -> p c r", r=P)[:, :, 0:rws],
                                   ACT.Copy).then_inc(hT_sb, 1)

            def experts(layer):
                def body(t0, grp, n):
                    hidden(n, (ACT.Gelu, ACT.Silu)[layer], LS[layer] + t0, H[layer] + t0, P, FF, hid, hidT)
                groups(act, SLOT_TILES[layer], body)

            attention0()
            route(0)
            experts(0)
            attention1()
            route(1)

            def shared(t0, grp, n):
                turned(n, LT[1] + TILES[1] + t0, TT, zT_ps, xnT, zT_sb)
                hidden(n, ACT.Silu, 0, HS + t0, TT, SHARED, hid, hidT)
            groups(act, TILES[1], shared)
            experts(1)

            def last(t0, grp, n):
                turned(n, LT[1] + 2 * TILES[1] + t0, TT, zT_ps, xnT, zT_sb)
                hidden(n, ACT.Silu, 0, HF + t0, TT, FF, fhid, fhidT)
            groups(act, TILES[1], last)

        @block.vector
        def _(dve):
            seq = Seq(dve, dve_step)
            dve.wait_ge(tok_rows_loaded, 32)
            for n in range(PATCHES):
                dve.wait_ge(emb_ps, n + 1)
                dve.tensor_tensor(R[:, n + 1, :], M[:, n % 4, 0:D], row["L0_tok_b"], ALU.add).then_inc(emb_sb, 1)
            dve.wait_ge(consts, 2)
            dve.wait_ge(emb_sb, PATCHES)
            dve.wait_ge(cls_set, 1)

            def carry_wait():
                dve.tensor_copy(carrier[:, 1:2], carrier[:, 0:1])

            def announce(sem):
                dve.tensor_copy(carrier[:, 2:3], carrier[:, 0:1]).then_inc(sem, 1)

            def mean_rstd(n, rws, src, at):
                carry_wait()
                for g in range(n):
                    seq.mark(dve.bn_stats(stats[0:rws, g, :], src(g)))
                seq.sync()
                carry_wait()
                for g in range(n):
                    ins = dve.bn_aggr(mv[0:rws, g, :], stats[0:rws, g, :])
                ins.then_inc(mean_var_ready, 1)
                dve.wait_ge(rstd_ready, at)

            def normalize(n, rws, src, dst, sem):
                for g in range(n):
                    dve.tensor_scalar(dst(g), src(g), mv[0:rws, g, 0:1], rs[0:rws, g:g + 1],
                                      ALU.subtract, ALU.mult).then_inc(sem, 1)

            def reduce(out_, in_, op):
                seq.mark(dve.tensor_reduce(out_, in_, AX.X, op))

            def norm_in(layer, t0, n, at):
                rws = ROWS[layer]
                mean_rstd(n, rws, lambda g: tile(R, t0 + g, rws), at)
                if not is_zero(t0):
                    dve.wait_ge(xnT_ps, LT[layer] + t0)
                normalize(n, rws, lambda g: tile(R, t0 + g, rws), lambda g: xn[0:rws, g, :], xn_ready)

            def keep_normed(layer, t0, n, ready):
                rws = ROWS[layer]
                dve.wait_ge(zg_ready, ready)
                for g in range(n):
                    dve.tensor_copy(tile(Z, t0 + g, rws), xn[0:rws, g, :]).then_inc(z_ready, 1)

            def take_logits(layer, t0, n):
                rws, E = ROWS[layer], EXPERTS[layer]
                for g in range(n):
                    dve.wait_ge(logit_ps, LT[layer] + t0 + g + 1)
                    dve.tensor_tensor(logits[0:rws, bass.ds(t0 + g, 1), 0:E].rearrange("p a d -> p (a d)"),
                                      M[0:rws, g, 0:E], router_b[layer][0:rws, :], ALU.add).then_inc(logits_ready, 1)

            def attention0():
                groups(dve, TILES[0], lambda t0, grp, n: norm_in(0, t0, n, grp + 1), seq, G, peel=True)
                for w in range(SEQ):
                    dve.wait_ge(products, w + 1)
                    reduce(s0[:, w], prods[:, w, :].rearrange("p (h g d) -> p h g d", h=QHEADS, g=HEADS), ALU.add)
                seq.sync()
                n = SEQ * QHEADS
                flat = lambda t: t.rearrange("p w h g -> p (w h) g")
                each = lambda t: t[:, 0:n].unsqueeze(2).broadcast_to([P, n, HEADS])
                seq.step(dve.tensor_scalar(s0, s0, float(HDIM) ** -0.5, None, ALU.mult))
                reduce(mx[:, 0:n], flat(s0), ALU.max)
                seq.sync()
                dve.tensor_tensor(flat(s0), flat(s0), each(mx), ALU.subtract).then_inc(s0_shifted, 1)
                dve.wait_ge(p0_exp, 1)
                reduce(sm[:, 0:n], flat(p0), ALU.add)
                seq.sync()
                seq.step(dve.reciprocal(mx[:, 0:n], sm[:, 0:n]))
                dve.tensor_tensor(flat(p0), flat(p0), each(mx), ALU.mult).then_inc(p0_ready, 1)
                for w in range(SEQ):
                    dve.wait_ge(weighted, w + 1)
                    reduce(mixed[:, :, w * HDIM:(w + 1) * HDIM],
                           prods[:, w, :].rearrange("p (h d g) -> p h d g", h=QHEADS, g=HEADS), ALU.add)
                seq.sync()
                announce(mixed_ready)
                dve.wait_ge(rb0_ready, 1)
                dve.wait_ge(proj0_ps, 1)
                for k, r in enumerate(MIXED_ROWS):
                    t = position_of_window_row(r)
                    seq.mark(dve.tensor_tensor(R[:, t, :], M[:, k // 4, P * (k % 4):P * (k % 4 + 1)], R[:, t, :], ALU.add))
                seq.sync()
                announce(attn0_done)

                def body(t0, grp, n):
                    mean_rstd(n, P, lambda g: tile(R, t0 + g, P), GROUPS[0] + grp + 1)
                    normalize(n, P, lambda g: tile(R, t0 + g, P), lambda g: xn[:, g, :], zg_ready)
                    keep_normed(0, t0, n, t0 + n)
                    take_logits(0, t0, n)
                groups(dve, TILES[0], body, seq, G)

            def combine(layer, t0, n, onto, to):
                for k in range(2):
                    for g in range(n):
                        weight = choice[0:TT, bass.ds(t0 + g, 1), 2 + k:3 + k].rearrange("p a b -> p (a b)")
                        seq.mark(dve.scalar_tensor_tensor(
                            to[0:TT, g, :] if k and to is Rb else tile(onto, t0 + g, TT),
                            tile(Y[layer][k], t0 + g, TT), weight, tile(onto, t0 + g, TT), ALU.mult, ALU.add))
                    seq.sync()

            def drop_keys(n):
                N = n * HEADS
                by_head = lambda k: minus_sparse[0:TT, k, :].unsqueeze(1).unsqueeze(3).broadcast_to([TT, n, HEADS, SEQ])
                g4 = lambda t: t[:, 0:N, :].rearrange("p (g h) j -> p g h j", g=n)
                seq.step(dve.tensor_tensor(g4(drop_key), g4(Sc), by_head(0), ALU.mult))
                seq.step(dve.tensor_tensor(g4(drop_key), g4(drop_key), by_head(1), ALU.add))
                carry_wait()
                for r in range(N):
                    ins = dve.max(top8[:, r, :], drop_key[:, r, :])
                seq.step(ins)
                least = top8[:, 0:N, DROP - 1:DROP].broadcast_to([TT, N, SEQ])
                seq.mark(dve.tensor_tensor(drop_ge[:, 0:N], drop_key[:, 0:N], least, ALU.is_ge))
                seq.step(dve.tensor_tensor(drop_eq[:, 0:N], drop_key[:, 0:N], least, ALU.is_equal))
                reduce(drop_n[:, 0:N], drop_ge[:, 0:N], ALU.add)
                flat = lambda t: t[:, 0:N, :].rearrange("p r j -> p (r j)")
                seq.step(dve.tensor_tensor_scan(flat(drop_cum), flat(carry), flat(drop_eq), 0.0, ALU.mult, ALU.add))
                seq.step(dve.tensor_scalar(drop_n[:, 0:N], drop_n[:, 0:N], float(DROP), None, ALU.subtract))
                seq.step(dve.tensor_tensor(drop_cum[:, 0:N], drop_cum[:, 0:N],
                                           drop_n[:, 0:N].unsqueeze(2).broadcast_to([TT, N, SEQ]), ALU.is_le))
                seq.step(dve.tensor_tensor(drop_eq[:, 0:N], drop_eq[:, 0:N], drop_cum[:, 0:N], ALU.mult))
                seq.step(dve.tensor_tensor(drop_ge[:, 0:N], drop_ge[:, 0:N], drop_eq[:, 0:N], ALU.subtract))

            def attention1():
                L = LT[1]
                dve.wait_ge(l1_loaded, 16 * 12)
                dve.wait_ge(rows_loaded, 16 * 16)
                seq.mark(dve.tensor_scalar(minus_sparse[:, 0, :], row["L1_attn_sparse_w"], -1.0, None, ALU.mult))
                seq.mark(dve.tensor_scalar(minus_sparse[:, 1, :], row["L1_attn_sparse_b"], -1.0, None, ALU.mult))
                seq.mark(dve.tensor_tensor(pattern_b[:], row["L1_attn_ps_b3"], row["L1_attn_pattern_bias"], ALU.add))
                seq.sync()

                def body(t0, grp, n):
                    dve.wait_ge(gathered, 32 * (t0 + n))
                    combine(0, t0, n, R, R)
                    announce(experts_added)
                    N = n * HEADS
                    each = lambda t: t[0:TT, 0:N].unsqueeze(2).broadcast_to([TT, N, SEQ])
                    norm_in(1, t0, n, 2 * GROUPS[0] + 3 * grp + 1)
                    for g in range(n):
                        dve.wait_ge(scores_ps, t0 + g + 1)
                        for b in range(2):
                            ins = dve.tensor_reduce(
                                Sc[:, g * HEADS + 4 * b:g * HEADS + 4 * b + 4, :],
                                PS[0:TT, g % 2, 512 * b:512 * b + 4 * TT].rearrange("p (h i j) -> p h j i", h=4, i=IPT),
                                AX.X, ALU.max)
                        ins.then_inc(packed, 1)
                    dve.wait_ge(packed, t0 + n)
                    drop_keys(n)
                    for g in range(n):
                        dve.wait_ge(l3_ps, t0 + g + 1)
                        seq.mark(dve.tensor_tensor(l3[:, g, :], M[0:TT, g, 0:3], pattern_b[0:TT, :], ALU.add))
                    seq.sync()
                    each3 = lambda t: t[0:TT, 0:n].unsqueeze(2).broadcast_to([TT, n, 3])
                    reduce(g1[:, 0:n], l3[:, 0:n], ALU.max)
                    seq.sync()
                    dve.tensor_tensor(l3[:, 0:n], l3[:, 0:n], each3(g1), ALU.subtract).then_inc(l3_shifted, 1)
                    dve.wait_ge(e3_done, grp + 1)
                    reduce(g1[:, 0:n], e3[:, 0:n], ALU.add)
                    seq.sync()
                    seq.step(dve.reciprocal(g2[:, 0:n], g1[:, 0:n]))
                    seq.step(dve.tensor_tensor(e3[:, 0:n], e3[:, 0:n], each3(g2), ALU.mult))
                    seq.step(dve.tensor_tensor(g1[:, 0:n], e3[:, 0:n, 0], e3[:, 0:n, 1], ALU.add))
                    seq.step(dve.tensor_scalar(g2[:, 0:n], g1[:, 0:n], 0.05, NEG, ALU.is_le, ALU.mult))
                    for g in range(n):
                        h = slice(g * HEADS, (g + 1) * HEADS)
                        seq.mark(dve.scalar_tensor_tensor(Sc[:, h, :], drop_ge[:, h, :], g2[:, g:g + 1], Sc[:, h, :],
                                                          ALU.mult, ALU.add))
                    seq.sync()
                    reduce(mx[0:TT, 0:N], Sc[:, 0:N, :], ALU.max)
                    seq.sync()
                    dve.tensor_tensor(Sc[:, 0:N, :], Sc[:, 0:N, :], each(mx), ALU.subtract).then_inc(shifted, 1)
                    dve.wait_ge(exp_done, grp + 1)
                    reduce(sm[0:TT, 0:N], Pc[:, 0:N, :], ALU.add)
                    seq.sync()
                    seq.step(dve.reciprocal(mx[0:TT, 0:N], sm[0:TT, 0:N]))
                    for g in range(n):
                        h = slice(g * HEADS, (g + 1) * HEADS)
                        dve.tensor_tensor(Pc[:, h, :], Pc[:, h, :],
                                          mx[0:TT, h].unsqueeze(2).broadcast_to([TT, HEADS, SEQ]),
                                          ALU.mult).then_inc(probs, 1)
                    dve.wait_ge(rb_ready, grp + 1)
                    for g in range(n):
                        dve.wait_ge(proj_ps, t0 + g + 1)
                        seq.mark(dve.tensor_tensor(tile(R, t0 + g, TT), M[0:TT, g, 0:D], Rb[0:TT, g, :], ALU.add))
                    seq.sync()
                    mean_rstd(n, TT, lambda g: tile(R, t0 + g, TT), 2 * GROUPS[0] + 3 * grp + 2)
                    for g in range(n):
                        seq.mark(dve.tensor_scalar(Rb[0:TT, g, :], tile(R, t0 + g, TT), mv[0:TT, g, 0:1],
                                                   rs[0:TT, g:g + 1], ALU.subtract, ALU.mult))
                    seq.sync()
                    for g in range(n):
                        seq.mark(dve.tensor_tensor(tile(R, t0 + g, TT), tile(R, t0 + g, TT), Rb[0:TT, g, :], ALU.add))
                    mean_rstd(n, TT, lambda g: Rb[0:TT, g, :], 2 * GROUPS[0] + 3 * grp + 3)
                    scaled_norm(n, Rb, row["L1_ffn_ln_in_g"], row["L1_ffn_ln_in_b"])
                    keep_normed(1, t0, n, L + t0 + n)
                    take_logits(1, t0, n)
                groups(dve, TILES[1], body, seq, 11 * G + 21)

            def scaled_norm(n, src, gain, shift):
                both = lambda v: v[0:TT, :].unsqueeze(1).broadcast_to([TT, n, D])
                for g in range(n):
                    seq.mark(dve.tensor_scalar(xn[0:TT, g, :], src[0:TT, g, :], mv[0:TT, g, 0:1], rs[0:TT, g:g + 1],
                                               ALU.subtract, ALU.mult))
                seq.sync()
                seq.step(dve.tensor_tensor(xn[0:TT, 0:n, :], xn[0:TT, 0:n, :], both(gain), ALU.mult))
                for g in range(n):
                    dve.tensor_tensor(xn[0:TT, g, :], xn[0:TT, g, :], shift[0:TT, :], ALU.add).then_inc(zg_ready, 1)

            def route(layer):
                rws, T, E = ROWS[layer], TILES[layer], EXPERTS[layer]

                def buf(k, shape=(T, E)):
                    return small(k, list(shape))[0:rws]

                def each(t):
                    return t.unsqueeze(2).broadcast_to([rws, T, E])
                lg = logits[0:rws, 0:T, 0:E]
                top, sum_, w0, w1, tmp = (small(12, [5, T])[0:rws, k, :] for k in range(5))
                fall = falling[0:rws, 16 - E:16].unsqueeze(1).broadcast_to([rws, T, E])
                dve.wait_ge(logits_ready, LT[layer] + T)
                reduce(top, lg, ALU.max)
                seq.sync()
                d, p, M0, M1, key = buf(0), buf(1), buf(2), buf(3), buf(4)
                dve.tensor_tensor(d, lg, each(top), ALU.subtract).then_inc(route_shifted, 1)
                dve.wait_ge(route_shifted, layer + 1)
                dve.wait_ge(route_exp, layer + 1)

                def first_largest(v, out_):
                    seq.step(dve.tensor_tensor(key, v, each(tmp), ALU.is_ge))
                    seq.step(dve.tensor_tensor(key, key, fall, ALU.mult))
                    reduce(tmp, key, ALU.max)
                    seq.sync()
                    seq.step(dve.tensor_tensor(out_, key, each(tmp), ALU.is_equal))
                reduce(tmp, d, ALU.max)
                seq.sync()
                first_largest(d, M0)
                seq.step(dve.scalar_tensor_tensor(d, M0, NEG, d, ALU.mult, ALU.add))
                reduce(tmp, d, ALU.max)
                seq.sync()
                first_largest(d, M1)
                reduce(sum_, p, ALU.add)
                for m, w in ((M0, w0), (M1, w1)):
                    seq.step(dve.tensor_tensor(key, p, m, ALU.mult))
                    reduce(w, key, ALU.add)
                    seq.sync()
                seq.step(dve.reciprocal(tmp, sum_))
                for k, w in enumerate((w0, w1)):
                    seq.mark(dve.tensor_tensor(w if layer == 0 else choice[0:rws, 0:T, 2 + k], w, tmp, ALU.mult))
                seq.sync()
                if layer == 0:
                    seq.step(dve.scalar_tensor_tensor(sum_, w0, 1e-9, w1, ALU.add, ALU.add))
                    seq.step(dve.reciprocal(tmp, sum_))
                    for k, w in enumerate((w0, w1)):
                        seq.mark(dve.tensor_tensor(choice[0:rws, 0:T, 2 + k], w, tmp, ALU.mult))
                seq.step(dve.tensor_tensor(routed[0:rws, 0:T, 0:E], M0, M1, ALU.add))
                if layer:
                    seq.step(dve.tensor_scalar(routed[0:rws, T - 1, 0:E], routed[0:rws, T - 1, 0:E],
                                               is_last[0:rws, 0:1], None, ALU.mult))
                announce(routed_ready)
                dve.wait_ge(rank_ps, layer + 1)
                per_tile, incl, excl = (buf(k, (E, T + 1)) for k in (5, 6, 7))
                totals, padded = small(13, [2, E])[0:rws, 0, :], small(13, [2, E])[0:rws, 1, :]
                n = T * E
                seq.step(dve.tensor_copy(per_tile[:, :, 0:T], PS[0:rws, 1, 0:n].rearrange("p (t e) -> p e t", e=E)))
                reduce(totals, per_tile[:, :, 0:T], ALU.add)
                seq.sync()
                seq.step(dve.tensor_scalar(count_i[0:rws, 0, 0:E], totals, float(P - 1), None, ALU.add))
                seq.step(dve.tensor_scalar(count_i[0:rws, 1, 0:E], count_i[0:rws, 0, 0:E], 7, 7,
                                           ALU.arith_shift_right, ALU.logical_shift_left))
                seq.step(dve.tensor_copy(padded, count_i[0:rws, 1, 0:E]))
                seq.step(dve.tensor_tensor(per_tile[:, :, T], padded, totals, ALU.subtract))
                flat = lambda t: t.rearrange("p e t -> p (e t)")
                seq.step(dve.tensor_tensor_scan(flat(incl), ones_f[0:rws, 0:E * (T + 1)], flat(per_tile), 0.0,
                                                ALU.mult, ALU.add))
                seq.step(dve.tensor_tensor(excl, incl, per_tile, ALU.subtract))
                slot = buf(8)
                seq.step(dve.tensor_tensor(slot, PS[0:rws, 0, 0:n].rearrange("p (t e) -> p t e", e=E),
                                           excl[:, :, 0:T].rearrange("p e t -> p t e"), ALU.add))
                for k, m in enumerate((M0, M1)):
                    seq.step(dve.tensor_tensor(key, slot, m, ALU.mult))
                    reduce(tmp, key, ALU.add)
                    seq.sync()
                    seq.step(dve.tensor_copy(choice[0:rws, 0:T, k].bitcast(I32), tmp))
                NT = G * SLOT_GROUPS[layer]
                ends = small(9, [NT * (E - 1)])[0:1].rearrange("p (i e) -> p i e", e=E - 1)
                seq.step(dve.tensor_tensor(ends, slot0[0:1, 0:NT].unsqueeze(2).broadcast_to([1, NT, E - 1]),
                                           incl[0:1, 0:E - 1, T].unsqueeze(1).broadcast_to([1, NT, E - 1]), ALU.is_ge))
                last_end, group_of = small(14, [SLOT_GROUPS[layer], G])[0:1], small(15, [SLOT_GROUPS[layer]])[0:1]
                reduce(last_end.rearrange("p i g -> p (i g)"), ends, ALU.add)
                seq.sync()
                seq.step(dve.tensor_tensor(last_end, last_end,
                                           radix[:].unsqueeze(1).broadcast_to([1, SLOT_GROUPS[layer], G]), ALU.mult))
                reduce(group_of, last_end, ALU.add)
                seq.sync()
                dve.tensor_copy(expert_of[0:1, 0:SLOT_GROUPS[layer]], group_of).then_inc(routing_ready, 1)

            def experts(layer):
                def inputs_turned(grp, n):
                    dve.wait_ge(xsT_ps, LSG[layer] + grp + 1)
                    dve.tensor_copy(xsT[:, 0:n, :], xsT_bank[:, 0:n, :]).then_inc(xsT_sb, 1)

                def body(t0, grp, n, n_behind):
                    e = experts_of_group(dve, layer, grp, n)
                    for g in range(n):
                        dve.wait_ge(up_ps, H[layer] + t0 + g + 1)
                        dve.tensor_tensor(hid[:, g, :], M[:, g, :], B1[layer][:, bass.ds(e[g], 1), :].rearrange("p a f -> p (a f)"),
                                          ALU.add).then_inc(hid_biased, 1)
                    if n_behind:
                        inputs_turned(grp + 1, n_behind)
                    if layer or not is_zero(t0):
                        dve.wait_ge(y_stored, 16 * (LSG[layer] + grp))
                    for g in range(n):
                        dve.wait_ge(y_ps, H[layer] + t0 + g + 1)
                        dve.tensor_tensor(ys[:, g, :], M[:, g, 0:D], B2[layer][:, bass.ds(e[g], 1), :].rearrange("p a f -> p (a f)"),
                                          ALU.add).then_inc(y_sb, 1)
                dve.wait_ge(routing_ready, layer + 1)
                inputs_turned(0, G)
                dve.wait_ge(w0_loaded, 16 * 4)
                if layer:
                    dve.wait_ge(w1b_loaded, 32)
                    dve.wait_ge(b2_loaded, 16)
                pipelined(dve, SLOT_TILES[layer], body)

            attention0()
            route(0)
            experts(0)
            dve.wait_ge(residual_loaded, 16)
            dve.wait_ge(choice_loaded, 16)
            attention1()
            route(1)

            def shared(t0, grp, n):
                for g in range(n):
                    dve.tensor_copy(xn[0:TT, g, :], tile(Z, t0 + g, TT)).then_inc(zg_ready, 1)
                for g in range(n):
                    dve.wait_ge(up_ps, HS + t0 + g + 1)
                    dve.tensor_tensor(hid[0:TT, g, 0:SHARED], M[0:TT, g, 0:SHARED], row["L1_ffn_sb1"][0:TT, :],
                                      ALU.add).then_inc(hid_biased, 1)
                for g in range(n):
                    dve.wait_ge(y_ps, HS + t0 + g + 1)
                    seq.mark(dve.tensor_tensor(Rb[0:TT, g, :], M[0:TT, g, 0:D], row["L1_ffn_sb2"][0:TT, :], ALU.add))
                seq.sync()
                for g in range(n):
                    dve.tensor_scalar(tile(S, t0 + g, TT), Rb[0:TT, g, :], 0.25, None, ALU.mult).then_inc(shared_ready, 1)
            groups(dve, TILES[1], shared, seq, G)
            experts(1)

            def last(t0, grp, n):
                dve.wait_ge(gathered, 32 * (TILES[1] + t0 + n))
                combine(1, t0, n, S, Rb)
                mean_rstd(n, TT, lambda g: Rb[0:TT, g, :], 2 * GROUPS[0] + 3 * GROUPS[1] + grp + 1)
                scaled_norm(n, Rb, row["L1_ffn_ff_ln_g"], row["L1_ffn_ff_ln_b"])
                for g in range(n):
                    seq.mark(dve.tensor_tensor(Rb[0:TT, g, :], Rb[0:TT, g, :], tile(R, t0 + g, TT), ALU.add))
                for g in range(n):
                    dve.wait_ge(up_ps, HF + t0 + g + 1)
                    dve.tensor_tensor(fhid[0:TT, g, :], M[0:TT, g, :], row["L1_ffn_ff_b1"][0:TT, :],
                                      ALU.add).then_inc(hid_biased, 1)
                seq.sync()
                for g in range(n):
                    seq.mark(dve.tensor_tensor(Rb[0:TT, g, :], Rb[0:TT, g, :], row["L1_ffn_ff_b2"][0:TT, :], ALU.add))
                seq.sync()
                for g in range(n):
                    dve.wait_ge(y_ps, HF + t0 + g + 1)
                    dve.tensor_tensor(tile(Z, t0 + g, TT), M[0:TT, g, 0:D], Rb[0:TT, g, :], ALU.add).then_inc(combined, 1)
            groups(dve, TILES[1], last, seq, 6 * G + 1)


def _laid_out(name, v):
    import numpy as np
    if name == "x":
        v = v.reshape(IMAGES, CHANNELS, GRID, 2, PATCH // 2, GRID, PATCH)
        return v.transpose(4, 6, 2, 5, 1, 3, 0).reshape(P, PATCHES, PIX, IMAGES)
    if name == "L0_tok_W":
        return v.reshape(D, CHANNELS, 2, P).transpose(3, 1, 2, 0).reshape(P, PIX, D)
    if name == "L0_attn_w_qkv":
        return np.concatenate([v[:QHEADS * HDIM], v[D:]]).T
    if name in ("L0_attn_w_proj", "L1_attn_qkv_w", "L1_attn_proj_w", "L1_attn_ps_w1",
                "L1_attn_ps_w2", "L1_attn_ps_w3"):
        return v.T
    if name in ("L0_ffn_w1", "L1_ffn_ew1"):
        return v.transpose(1, 0, 2)
    if name in ("L0_ffn_w2", "L1_ffn_ew2"):
        return v.reshape(v.shape[0], FC, P, D).transpose(2, 0, 1, 3)
    if name == "L1_ffn_sw2" or name == "L1_ffn_ff_w2":
        return v.reshape(-1, P, D).transpose(1, 0, 2)
    return v


def kernel(**inputs):
    import numpy as _np
    import concourse.bacc as _bacc
    from concourse import mybir as _mybir
    from concourse.bass_utils import run_bass_kernel_spmd as _run

    nc = _bacc.Bacc("TRN2", target_bir_lowering=False, num_devices=1)
    arrays, args = {}, {}
    for name, value in inputs.items():
        v = _laid_out(name, _np.asarray(value))
        v = _np.ascontiguousarray(v)
        arrays[f"in_{name}_dram"] = v
        args[name] = nc.dram_tensor(f"in_{name}_dram", v.shape, _mybir.dt.from_np(v.dtype), kind="ExternalInput").ap()
    out = nc.dram_tensor("out_0_dram", (IMAGES, SEQ, D), _mybir.dt.float32, kind="ExternalOutput").ap()
    vit_tower(nc, args, out)
    r = _run(nc, [arrays], core_ids=[0])
    return r.results[0]["out_0_dram"]
```

```python
from contextlib import ExitStack

import concourse.bass as bass
from concourse import mybir

F32 = mybir.dt.float32
BF16 = mybir.dt.bfloat16
I32 = mybir.dt.int32
U32 = mybir.dt.uint32
ALU = mybir.AluOpType
ACT = mybir.ActivationFunctionType
AX = mybir.AxisListType

P = 128
D = 128
IMAGES = 128
CHANNELS, SIDE, PATCH = 3, 64, 16
GRID = SIDE // PATCH
PATCHES = GRID * GRID
SEQ = PATCHES + 1
TOKENS = IMAGES * SEQ
HEADS = 8
HDIM = D // HEADS
IPT = P // SEQ
TT = IPT * SEQ
ROWS = (P, TT)
TILES = (SEQ, -(-TOKENS // TT))
LAST = TOKENS - (TILES[1] - 1) * TT
PADDED = TILES[1] * TT
G = 4
A = 2
A_GROUPS = -(-TILES[1] // A)
A_LAST = TILES[1] - A * (A_GROUPS - 1)
GROUPS = tuple(-(-t // G) for t in TILES)
PIX = PATCH * PATCH * CHANNELS // P
FF = 512
FC = FF // P
SHARED = 256
SC = SHARED // P
WINDOW = 64
HALF = WINDOW // 2
KEEP = max(1, min(SEQ, int(SEQ * (1.0 - 0.3))))
DROP = SEQ - KEEP
EXPERTS = (8, 16)
TEMPERATURE = (1.0, 0.7)
PATTERN_TEMPERATURE = 0.3
PAIRS = 2 * TOKENS
SLOT_TILES = tuple((PAIRS + E * (P - 1)) // P for E in EXPERTS)
MAX_SLOT_TILES = max(SLOT_TILES)
SLOT_GROUPS = tuple(-(-t // G) for t in SLOT_TILES)
NEG = -1e30
EPS = 1e-5

MIXED_ROWS = [r for r in range(SEQ) if 8 * (r % 8) < SEQ]
QHEADS = max(r // 8 for r in MIXED_ROWS) + 1
DVE_ROWS = [w for w in range(SEQ) if w % 4 == 3]
POOL_ROWS = [w for w in range(SEQ) if w % 4 != 3]
QKV0 = QHEADS * HDIM + 2 * D


def heads_of(w):
    return sum(r % 8 == w // 8 for r in MIXED_ROWS)


def position_of_window_row(w):
    return (w + HALF) % SEQ


def vit_tower(nc, a, out):
    with ExitStack() as ctx:
        def sb(name, shape, dt=F32):
            return ctx.enter_context(nc.sbuf_tensor(name, shape, dt))

        residual_dram = nc.dram_tensor("residual_tokens", [PADDED, D], F32).ap()
        choice_dram = nc.dram_tensor("choice_tokens", [PADDED, 4], F32).ap()
        xs_dram = nc.dram_tensor("expert_in", [MAX_SLOT_TILES * P, D], F32).ap()
        ys_dram = nc.dram_tensor("expert_out", [MAX_SLOT_TILES * P, D], F32).ap()

        region = sb("region", [P, 24576])
        scratch = sb("scratch", [P, 9520])
        W1 = [region[:, 0:4096].rearrange("p (e f) -> p e f", e=8),
              region[:, 16384:24576].rearrange("p (e f) -> p e f", e=16)]
        W2 = [region[:, 4096:8192].rearrange("p (e c d) -> p e c d", e=8, c=FC),
              region[:, 0:8192].rearrange("p (e c d) -> p e c d", e=16, c=FC)]
        B1 = [region[:, 8192:12288].rearrange("p (e f) -> p e f", e=8),
              region[:, 8192:16384].rearrange("p (e f) -> p e f", e=16)]
        B2 = [region[:, 12288:13312].rearrange("p (e d) -> p e d", e=8), scratch[:, 7472:9520].rearrange("p (e d) -> p e d", e=16)]
        pixels = region[:, 8192:8192 + PATCHES * PIX * IMAGES].rearrange("p (n c b) -> p n c b", n=PATCHES, c=PIX)
        prods = region[:, 16384:16384 + SEQ * QHEADS * D].rearrange("p (w x) -> p w x", w=SEQ)

        R = sb("residual", [P, TILES[1], D])
        Z = sb("normed", [P, TILES[1], D])
        Y0 = scratch[:, 0:TILES[1] * D].rearrange("p (t d) -> p t d", t=TILES[1])
        Y1 = scratch[:, TILES[1] * D:2 * TILES[1] * D].rearrange("p (t d) -> p t d", t=TILES[1])
        qkv0 = scratch[:, 0:SEQ * QKV0].rearrange("p (t x) -> p t x", t=SEQ)
        s0 = scratch[:, 5168:5576].rearrange("p (w h g) -> p w h g", w=SEQ, h=QHEADS)
        p0 = scratch[:, 5576:5984].rearrange("p (w h g) -> p w h g", w=SEQ, h=QHEADS)
        mixed = scratch[:, 5984:5984 + QHEADS * 3 * D].rearrange("p (h x) -> p h x", h=QHEADS)
        mixedT = scratch[:, 7136:7136 + len(MIXED_ROWS) * P].rearrange("p (r b) -> p r b", b=P)
        Kbd = scratch[:, 0:1904].rearrange("p (g h t) -> p g h t", g=A, h=HEADS)
        Pf = scratch[0:TT, 1904:3808].rearrange("p (g h t) -> p g h t", g=A, h=HEADS)
        PT = scratch[0:TT, 3808:5712].rearrange("p (g h t) -> p g h t", g=A, h=HEADS)
        NK = A * HEADS * SEQ
        drop_key, drop_ge, drop_eq, drop_cum = (
            scratch[0:TT, 5712 + k * NK:5712 + (k + 1) * NK].rearrange("p (r j) -> p r j", j=SEQ) for k in range(4))
        top8 = scratch[0:TT, 6800:6800 + 8 * A * HEADS].rearrange("p (r k) -> p r k", k=8)
        vs = scratch[0:TT, 6960:6960 + 4 * A * D].rearrange("p (g d) -> p g d", g=4 * A)
        drop_n = scratch[0:TT, 6928:6928 + A * HEADS]
        Y0_, Y1_ = (region[:, 8192 + k * TILES[1] * D:8192 + (k + 1) * TILES[1] * D].rearrange("p (t d) -> p t d", t=TILES[1])
                    for k in range(2))
        Y = [(Y0_, Y1_), (Y0, Y1)]

        def small(k, shape):
            n = 1
            for x in shape:
                n *= x
            v = scratch[:, 336 * k:336 * k + n]
            return v if len(shape) == 1 else v.rearrange("p (a b) -> p a b", b=shape[1])
        xs = scratch[:, 0:512].rearrange("p (g d) -> p g d", g=G)
        xsT = scratch[:, 512:1024].rearrange("p (g d) -> p g d", g=G)
        hid = scratch[:, 1024:3072].rearrange("p (g f) -> p g f", g=G)
        hidT = scratch[:, 3072:5120].rearrange("p (g f) -> p g f", g=G)
        ys = scratch[:, 5120:5632].rearrange("p (g d) -> p g d", g=G)
        heads = sb("heads", [P, 2452])
        qk = heads[:, 0:952].rearrange("p (g a t) -> p g a t", g=G, a=2)
        osb = heads[0:TT, 1464:1976].rearrange("p (g d) -> p g d", g=G)
        oT = heads[:, 1976:2452].rearrange("p (g t) -> p g t", g=G)
        tokT = heads[:, 0:PIX * D].rearrange("p (c d) -> p c d", c=PIX)
        S = heads[:, 0:TILES[1] * D].rearrange("p (t d) -> p t d", t=TILES[1])
        packed_heads = sb("packed_heads", [P, 2, G * HEADS * SEQ])
        Sc, Pc = (packed_heads[0:TT, k, :].rearrange("p (r j) -> p r j", j=SEQ) for k in range(2))
        zeros = packed_heads[:].rearrange("p k x -> p (k x)")[:, 0:7 * P]
        fhid = scratch[:, 4864:6912].rearrange("p (g f) -> p g f", g=G)
        fhidT = scratch[:, 6912:8960].rearrange("p (g f) -> p g f", g=G)

        qkvT = [sb("qkv_T0", [P, QKV0])[:], sb("qkv_T1", [P, 3 * D])[:]]
        projT = [sb("proj_T0", [P, D])[:], sb("proj_T1", [P, D])[:]]
        ps1T, ps2T, ps3T = sb("ps1_T", [P, D]), sb("ps2_T", [P, 64]), sb("ps3_T", [64, 3])
        router_w = [sb("router_w0", [P, 8]), sb("router_w1", [P, 16])]
        sw1, sw2 = sb("shared_w1", [P, SHARED]), sb("shared_w2", [P, SC, D])
        fw1, fw2 = sb("ff_w1", [P, FF]), sb("ff_w2", [P, FC, D])
        rows = sb("bias_rows", [P, 2096])
        at, row = 0, {}
        for name, n in (("L0_tok_b", D), ("cls_tok", D), ("L0_attn_b_proj", D), ("L0_ffn_router_b", 8),
                        ("L1_attn_proj_b", D), ("L1_ffn_router_b", 16), ("L1_ffn_ln_in_g", D),
                        ("L1_ffn_ln_in_b", D), ("L1_attn_ps_b3", 3), ("L1_attn_pattern_bias", 3),
                        ("L1_attn_sparse_w", HEADS), ("L1_attn_sparse_b", HEADS), ("L1_ffn_sb1", SHARED),
                        ("L1_ffn_sb2", D), ("L1_ffn_ff_ln_g", D), ("L1_ffn_ff_ln_b", D),
                        ("L1_ffn_ff_b1", FF), ("L1_ffn_ff_b2", D)):
            row[name] = rows[:, at:at + n]
            at += n
        proj_b = [row["L0_attn_b_proj"], row["L1_attn_proj_b"]]
        router_b = [row["L0_ffn_router_b"], row["L1_ffn_router_b"]]
        cols = sb("bias_columns", [P, 2])
        pattern_b = sb("pattern_b", [P, 3])
        minus_sparse = sb("minus_sparse", [P, 2, HEADS])

        ident = sb("identity", [P, P])
        own = sb("own_image", [TT, IPT])
        own_rows_f = sb("own_rows_f", [IPT, TT])
        own_rows = sb("own_rows", [IPT, TT], BF16)
        other = sb("other_image", [IPT, 4, TT], BF16)
        head_rows = sb("head_rows", [P, HEADS])
        before = sb("before", [P, P], BF16)
        ones_b = sb("ones_b", [P, P], BF16)
        ones_f = sb("ones_f", [P, 16 * (TILES[1] + 1)])
        carry = sb("carry", [TT, G * HEADS, SEQ])
        is_last = sb("is_last", [P, 1])
        pool_mean = sb("pool_mean", [TT, TT])
        slot0 = sb("slot0", [P, G * SLOT_GROUPS[1]])
        slot0_i = sb("slot0_i", [P, G * SLOT_GROUPS[1]], I32)
        radix = sb("radix", [1, G])
        falling = sb("falling", [P, 16])
        falling_i = sb("falling_i", [P, 16], I32)
        mhalf = sb("mhalf", [P, G])
        eps = sb("eps", [P, G])
        carrier = sb("carrier", [1, 4])

        stats = sb("stats", [P, G, 6])
        mv = sb("mean_var", [P, G, 2])
        ve = sb("var_eps", [P, G])
        rs = sb("rstd", [P, G])
        xn = sb("xn", [P, G, D])
        xnT = sb("xnT", [P, G, D])
        Rb = sb("residual_bias", [P, G, D])
        mx = sb("row_max", [P, 52])
        sm = sb("row_sum", [P, 52])
        l3 = sb("pattern_logits", [TT, G, 3])
        e3 = sb("pattern_weights", [TT, G, 3])
        g1 = sb("gate_tmp", [TT, G])
        g2 = sb("gate", [TT, G])
        logits = sb("logits", [P, TILES[1], 16])
        choice = sb("choice", [P, TILES[1], 4])
        routed = sb("routed", [P, TILES[1], 16], BF16)
        count_i = sb("count_i", [P, 2, 16], I32)
        expert_of = sb("expert_of", [1, SLOT_GROUPS[1]], I32)

        M = ctx.enter_context(nc.psum_tensor("M", [P, 4, 512], F32))
        PS = ctx.enter_context(nc.psum_tensor("PS", [P, 2, 1024], F32))

        def sem(name):
            return ctx.enter_context(nc.semaphore(name))

        consts, pool_step, dve_step, tok_w_loaded, tok_rows_loaded = (
            sem(n) for n in ("consts", "pool_step", "dve_step", "tok_w_loaded", "tok_rows_loaded"))
        rows_loaded, l0_loaded, l1_loaded, zero_stored = (
            sem(n) for n in ("rows_loaded", "l0_loaded", "l1_loaded", "zero_stored"))
        own_ps, pool_ready, emb_ps, emb_sb, cls_set = (
            sem(n) for n in ("own_ps", "pool_ready", "emb_ps", "emb_sb", "cls_set"))
        mean_var_ready, rstd_ready, xn_ready, xnT_ps, xnT_sb = (
            sem(n) for n in ("mean_var_ready", "rstd_ready", "xn_ready", "xnT_ps", "xnT_sb"))
        qkv_ps, qkv0_sb, qk_sb, v_sb, kbd = (
            sem(n) for n in ("qkv_ps", "qkv0_sb", "qk_sb", "v_sb", "kbd"))
        rb_ready, scores_ps, packed, shifted = (
            sem(n) for n in ("rb_ready", "scores_ps", "packed", "shifted"))
        exp_done, probs, spread, pT_ps, pT_sb = (
            sem(n) for n in ("exp_done", "probs", "spread", "pT_ps", "pT_sb"))
        o_ps, o_sb, oT_ps, oT_sb, proj_ps = (
            sem(n) for n in ("o_ps", "o_sb", "oT_ps", "oT_sb", "proj_ps"))
        z_ready, zg_ready, zT_ps, zT_sb, logit_ps = (
            sem(n) for n in ("z_ready", "zg_ready", "zT_ps", "zT_sb", "logit_ps"))
        logits_ready = sem("logits_ready")
        products, s0_shifted, p0_exp, p0_ready, weighted = (
            sem(n) for n in ("products", "s0_shifted", "p0_exp", "p0_ready", "weighted"))
        mixed_ready, mixedT_ps, mixedT_sb, proj0_ps, attn0_done = (
            sem(n) for n in ("mixed_ready", "mixedT_ps", "mixedT_sb", "proj0_ps", "attn0_done"))
        rb0_ready, pl_sb, h1_ps, h1_sb, h2_ps = (
            sem(n) for n in ("rb0_ready", "pl_sb", "h1_ps", "h1_sb", "h2_ps"))
        h2_sb, l3_ps, l3_shifted, e3_done = (
            sem(n) for n in ("h2_sb", "l3_ps", "l3_shifted", "e3_done"))
        route_shifted, route_exp, routed_ready, rank_ps, routing_ready = (
            sem(n) for n in ("route_shifted", "route_exp", "routed_ready", "rank_ps", "routing_ready"))
        choice_stored, choice_loaded = (
            sem(n) for n in ("choice_stored", "choice_loaded"))
        residual_stored, residual_loaded, scattered, w0_loaded, w1a_loaded = (
            sem(n) for n in ("residual_stored", "residual_loaded", "scattered", "w0_loaded", "w1a_loaded"))
        w1b_loaded, b2_loaded = (
            sem(n) for n in ("w1b_loaded", "b2_loaded"))
        xs_in, xsT_ps, xsT_sb, up_ps, hid_biased = (
            sem(n) for n in ("xs_in", "xsT_ps", "xsT_sb", "up_ps", "hid_biased"))
        hid_ready, hT_ps, hT_sb, y_ps, y_sb = (
            sem(n) for n in ("hid_ready", "hT_ps", "hT_sb", "y_ps", "y_sb"))
        experts_added = sem("experts_added")
        fT_ps, fT_sb = sem("fT_ps"), sem("fT_sb")
        y_stored, gathered, combined, shared_ready = (
            sem(n) for n in ("y_stored", "gathered", "combined", "shared_ready"))
        out_stored = sem("out_stored")
        pixels_in = [ctx.enter_context(nc.semaphore(f"pixels_in{g}")) for g in range(4)]

        block = ctx.enter_context(nc.Block())

        class Seq:
            def __init__(self, eng, sem):
                self.eng, self.sem, self.at, self.n = eng, sem, 0, 0

            def mark(self, ins):
                ins.then_inc(self.sem, 1)
                self.at = self.at + 1
                self.n += 1

            def sync(self):
                self.eng.wait_ge(self.sem, self.at)

            def step(self, ins):
                self.mark(ins)
                self.sync()

        def groups(eng, tiles, body, seq=None, steps=0, peel=False):
            whole, rest = divmod(tiles, G)
            start, n = (seq.at, seq.n) if seq else (0, 0)
            if peel:
                body(0, 0, G)
                n = seq.n if seq else 0
            with eng.Fori(1 if peel else 0, whole) as i:
                if seq:
                    seq.at = start + i * steps
                body(i * G, i, G)
            if seq:
                assert seq.n - n == steps, (seq.n - n, steps)
                seq.at = start + whole * steps
            if rest:
                body(whole * G, whole, rest)

        def pipelined(eng, tiles, body, seq=None, steps=0):
            whole, rest = divmod(tiles, G)
            body(0, 0, G, G)
            start, n = (seq.at, seq.n) if seq else (0, 0)
            with eng.Fori(1, whole - 1) as i:
                if seq:
                    seq.at = start + (i - 1) * steps
                body(i * G, i, G, G)
            if seq:
                assert seq.n - n == steps, (seq.n - n, steps)
                seq.at = start + (whole - 2) * steps
            body((whole - 1) * G, whole - 1, G, rest)
            if rest:
                body(whole * G, whole, rest, 0)

        def experts_of_group(eng, layer, grp, n):
            packed_ = eng.value_load(expert_of[0:1, bass.ds(grp, 1)], min_val=0, max_val=16 ** G - 1)
            return [(packed_ >> (4 * g)) & (EXPERTS[layer] - 1) for g in range(n)]

        def overlapped(eng, step, seq=None, steps=0):
            last = A_GROUPS - 1

            def tiles_of(i):
                return (i, A if i < last else A_LAST) if 0 <= i <= last else (None, 0)

            def static(i):
                step(*tiles_of(i), *tiles_of(i - 1), *tiles_of(i - 2), *tiles_of(i + 1))
            for i in range(-1, 2):
                static(i)
            start, n = (seq.at, seq.n) if seq else (0, 0)
            with eng.Fori(2, last - 1) as i:
                if seq:
                    seq.at = start + (i - 2) * steps
                step(i, A, i - 1, A, i - 2, A, i + 1, A)
            if seq:
                assert seq.n - n == steps, (seq.n - n, steps)
                seq.at = start + (last - 3) * steps
            for i in range(last - 1, last + 3):
                static(i)

        def tiles_before(*groups_):
            return [None if x is None else A * x for x in groups_]

        def prods_of(w, last_two):
            nh = heads_of(w)
            n = HEADS * HDIM
            v = prods[:, w, 0:nh * n]
            return v.rearrange("p (h x y) -> p h x y", h=nh, y=last_two)

        def query_key(eng, w):
            t, nh = position_of_window_row(w), heads_of(w)
            q = qkv0[:, t, 0:nh * HDIM].rearrange("p (h d) -> p h d", h=nh)
            k = qkv0[:, t, QHEADS * HDIM:QHEADS * HDIM + D].rearrange("p (g d) -> p g d", g=HEADS)
            return eng.tensor_tensor(prods_of(w, HDIM), q.unsqueeze(2).broadcast_to([P, nh, HEADS, HDIM]),
                                     k.unsqueeze(1).broadcast_to([P, nh, HEADS, HDIM]), ALU.mult)

        def prob_value(eng, w):
            t, nh = position_of_window_row(w), heads_of(w)
            v = qkv0[:, t, QHEADS * HDIM + D:QKV0].rearrange("p (g d) -> p d g", g=HEADS)
            return eng.tensor_tensor(prods_of(w, HEADS), p0[:, w, 0:nh].unsqueeze(2).broadcast_to([P, nh, HDIM, HEADS]),
                                     v.unsqueeze(1).broadcast_to([P, nh, HDIM, HEADS]), ALU.mult)

        NORMS = 2 * GROUPS[0]

        def norm_in_at(a):
            return NORMS + (a + 1 if isinstance(a, int) and a < 3 else 3 * a - 5)

        def norm_out_at(b, k):
            late = max(0, b - (A_GROUPS - 4)) if isinstance(b, int) else 0
            return NORMS + 3 * b + 5 + k - late

        hT_bank = [PS[:, b // 2, 512 * (b % 2):512 * (b % 2) + 512] for b in (0, 1, 2, 0)]
        xsT_bank = PS[:, 1, 512:1024].rearrange("p (g d) -> p g d", g=G)

        def is_zero(t0):
            return isinstance(t0, int) and t0 == 0

        def tile(T, t, rows):
            return T[0:rows, bass.ds(t, 1), :].rearrange("p a d -> p (a d)")

        LT = (0, TILES[0])
        LG = (0, GROUPS[0])
        LS = (0, SLOT_TILES[0])
        LSG = (0, SLOT_GROUPS[0])
        H = (0, SLOT_TILES[0] + TILES[1])
        HS, HF = SLOT_TILES[0], SLOT_TILES[0] + TILES[1] + SLOT_TILES[1]

        @block.sync
        def _(sp):
            def load(dst, name, sem):
                sp.dma_start(dst, a[name]).then_inc(sem, 16)

            def load_rows(*names, sem=rows_loaded):
                for name in names:
                    v = a[name] if len(a[name].shape) == 1 else a[name].rearrange("a b d -> (a b d)")
                    sp.dma_start(row[name], v.partition_broadcast(P)).then_inc(sem, 16)

            load(tokT, "L0_tok_W", tok_w_loaded)
            for g in range(4):
                sp.dma_start(pixels[:, 4 * g:4 * g + 4], a["x"][:, 4 * g:4 * g + 4]).then_inc(pixels_in[g], 16)
                if g == 0:
                    load_rows("L0_tok_b", "cls_tok", sem=tok_rows_loaded)
            load_rows("L0_attn_b_proj", "L0_ffn_router_b")
            load(qkvT[0], "L0_attn_w_qkv", l0_loaded)
            load(projT[0], "L0_attn_w_proj", l0_loaded)
            load(router_w[0][:], "L0_ffn_router_w", l0_loaded)
            load(W1[0], "L0_ffn_w1", w0_loaded)
            load(W2[0], "L0_ffn_w2", w0_loaded)
            sp.wait_ge(consts, 1)
            zrows = xs_dram.rearrange("(k p) d -> p k d", p=P)
            for k in range(0, MAX_SLOT_TILES, 7):
                sp.dma_start(zrows[:, k:k + 7, :], zeros.rearrange("p (k d) -> p k d", k=7)).then_inc(zero_stored, 16)
            sp.dma_start(residual_dram[TOKENS:PADDED, :], zeros[0:PADDED - TOKENS, 0:D]).then_inc(zero_stored, 16)
            sp.dma_start(choice_dram[TOKENS:PADDED, :], zeros[0:PADDED - TOKENS, 0:4]).then_inc(zero_stored, 16)
            load(qkvT[1], "L1_attn_qkv_w", l1_loaded)
            load(projT[1], "L1_attn_proj_w", l1_loaded)
            load(ps1T[:], "L1_attn_ps_w1", l1_loaded)
            load(ps2T[:], "L1_attn_ps_w2", l1_loaded)
            load(ps3T[:], "L1_attn_ps_w3", l1_loaded)
            load(router_w[1][:], "L1_ffn_router_w", l1_loaded)
            load(sw1[:], "L1_ffn_sw1", l1_loaded)
            load(sw2[:], "L1_ffn_sw2", l1_loaded)
            load(fw1[:], "L1_ffn_ff_w1", l1_loaded)
            load(fw2[:], "L1_ffn_ff_w2", l1_loaded)
            sp.dma_start(cols[:, 0:1], a["L1_attn_ps_b1"].unsqueeze(1)).then_inc(l1_loaded, 16)
            sp.dma_start(cols[0:64, 1:2], a["L1_attn_ps_b2"].unsqueeze(1)).then_inc(l1_loaded, 16)
            load_rows("L1_attn_proj_b", "L1_ffn_router_b", "L1_ffn_ln_in_g", "L1_ffn_ln_in_b", "L1_attn_ps_b3",
                      "L1_attn_pattern_bias", "L1_attn_sparse_w", "L1_attn_sparse_b", "L1_ffn_sb1", "L1_ffn_sb2",
                      "L1_ffn_ff_ln_g", "L1_ffn_ff_ln_b", "L1_ffn_ff_b1", "L1_ffn_ff_b2")
            sp.wait_ge(emb_ps, PATCHES)
            sp.dma_start(B1[0], a["L0_ffn_b1"].partition_broadcast(P)).then_inc(w0_loaded, 16)
            sp.dma_start(B2[0], a["L0_ffn_b2"].partition_broadcast(P)).then_inc(w0_loaded, 16)

            def experts(layer):
                tiles_of = lambda d, t0, n: d.rearrange("(k p) d -> p k d", p=P)[:, bass.ds(t0, n), :]

                def take(grp, n):
                    if layer or not is_zero(grp):
                        sp.wait_ge(xsT_ps, LSG[layer] + grp)
                    sp.dma_start(xs[:, 0:n, :], tiles_of(xs_dram, grp * G, n)).then_inc(xs_in, 16)

                def put(grp, n):
                    sp.wait_ge(y_sb, LS[layer] + grp * G + n)
                    sp.dma_start(tiles_of(ys_dram, grp * G, n), ys[:, 0:n, :]).then_inc(y_stored, 16)
                sp.wait_ge(scattered, 32 * (LT[layer] + TILES[layer]))
                sp.wait_ge(routing_ready, layer + 1)
                whole, rest = divmod(SLOT_TILES[layer], G)
                take(0, G)
                take(1, G)
                with sp.Fori(2, whole) as i:
                    take(i, G)
                    put(i - 2, G)
                if rest:
                    take(whole, rest)
                put(whole - 2, G)
                put(whole - 1, G)
                if rest:
                    put(whole, rest)

            sp.wait_ge(attn0_done, 1)
            sp.dma_start(residual_dram[0:TOKENS, :].rearrange("(b j) d -> b j d", j=SEQ), R[:, 0:SEQ, :])\
              .then_inc(residual_stored, 16)
            sp.dma_start(W1[1], a["L1_ffn_ew1"]).then_inc(w1a_loaded, 16)
            sp.wait_ge(routing_ready, 1)
            sp.dma_start(choice_dram[0:TOKENS, :].rearrange("(b j) c -> b (j c)", j=SEQ),
                         choice[:, 0:SEQ, :].rearrange("p t c -> p (t c)")).then_inc(choice_stored, 16)
            sp.wait_ge(residual_stored, 16)
            sp.wait_ge(zero_stored, 16 * (MAX_SLOT_TILES // 7 + 2))
            sp.wait_ge(logits_ready, TILES[0])
            sp.dma_start(R[0:TT, :, :], residual_dram.rearrange("(t p) d -> p t d", p=TT)).then_inc(residual_loaded, 16)
            experts(0)
            sp.wait_ge(choice_stored, 16)
            sp.dma_start(choice[0:TT, :, :], choice_dram.rearrange("(t p) c -> p t c", p=TT)).then_inc(choice_loaded, 16)
            sp.wait_ge(y_sb, SLOT_TILES[0])
            sp.dma_start(W2[1], a["L1_ffn_ew2"]).then_inc(w1b_loaded, 16)
            sp.wait_ge(experts_added, A_GROUPS)
            sp.dma_start(B1[1], a["L1_ffn_eb1"].partition_broadcast(P)).then_inc(w1b_loaded, 16)
            sp.wait_ge(logits_ready, TILES[0] + TILES[1])
            sp.dma_start(B2[1], a["L1_ffn_eb2"].partition_broadcast(P)).then_inc(b2_loaded, 16)
            experts(1)
            sp.wait_ge(combined, TILES[1])

            o = out.rearrange("b j d -> (b j) d")
            sp.dma_start(o[0:(TILES[1] - 1) * TT, :].rearrange("(t p) d -> p t d", p=TT),
                         Z[0:TT, 0:TILES[1] - 1, :]).then_inc(out_stored, 16)
            sp.dma_start(o[(TILES[1] - 1) * TT:TOKENS, :], Z[0:LAST, TILES[1] - 1, :]).then_inc(out_stored, 16)
            sp.wait_ge(out_stored, 32)

        @block.gpsimd
        def _(pool):
            seq = Seq(pool, pool_step)
            pool.memset(zeros, 0.0).then_inc(consts, 1)
            seq.mark(pool.memset(ident[:], 0.0))
            seq.mark(pool.memset(own[:], 1.0))
            seq.mark(pool.memset(own_rows_f[:], 1.0))
            seq.mark(pool.memset(head_rows[:], float(HDIM) ** -0.5))
            seq.mark(pool.memset(before[:], 1.0))
            seq.mark(pool.memset(is_last[:], 1.0))
            seq.mark(pool.memset(ones_b[:], 1.0))
            seq.mark(pool.memset(ones_f[:], 1.0))
            seq.mark(pool.memset(mhalf[:], -0.5))
            seq.mark(pool.memset(eps[:], EPS))
            seq.mark(pool.memset(carrier[:], 0.0))
            seq.mark(pool.memset(carry[:], 1.0))
            seq.mark(pool.memset(mixed, 0.0))
            seq.mark(pool.memset(s0, 0.0))
            seq.mark(pool.iota(slot0_i[:], pattern=[[P, G * SLOT_GROUPS[1]]], base=0, channel_multiplier=0))
            for g in range(G):
                seq.mark(pool.memset(radix[:, g:g + 1], 16.0 ** g))
            seq.mark(pool.iota(falling_i[:], pattern=[[-1, 16]], base=16, channel_multiplier=0))
            seq.sync()

            def keep(t, pattern, base, mult, op=ALU.is_ge, fill=0.0):
                seq.mark(pool.affine_select(out=t, in_=t, compare_op=op, fill=fill, base=base,
                                            pattern=pattern, channel_multiplier=mult))
            keep(ident[:], [[-1, P]], 0, 1, ALU.not_equal, 1.0)
            keep(own[:], [[-SEQ, IPT]], 0, 1)
            keep(own_rows_f[:], [[1, TT]], 0, -SEQ)
            keep(head_rows[:], [[-HDIM, HEADS]], 0, 1)
            keep(before[:], [[1, P]], -1, -1)
            keep(is_last[:], [[0, 1]], LAST - 1, -1)
            seq.mark(pool.memset(carry[:, :, 0:1], 0.0))
            seq.mark(pool.tensor_copy(slot0[:], slot0_i[:]))
            seq.mark(pool.tensor_copy(falling[:], falling_i[:]))
            seq.sync()
            keep(own[:], [[SEQ, IPT]], SEQ - 1, -1)
            keep(own_rows_f[:], [[-1, TT]], SEQ - 1, SEQ)
            keep(head_rows[:], [[HDIM, HEADS]], HDIM - 1, -1)
            seq.sync()
            seq.mark(pool.tensor_copy(own_rows[:], own_rows_f[:]))
            for h in range(4):
                seq.mark(pool.tensor_scalar(other[:, h, :], own_rows_f[:], -1.0, -NEG, ALU.add, ALU.mult))
            seq.sync()
            pool.memset(carrier[:], 0.0).then_inc(consts, 1)

            def norm_rstd(n, rws, at, slot=0):
                pool.wait_ge(mean_var_ready, at)
                v = ve[0:rws, slot:slot + n]
                seq.step(pool.tensor_tensor(v, mv[0:rws, slot:slot + n, 1], eps[0:rws, 0:n], ALU.add))
                pool.tensor_tensor(rs[0:rws, slot:slot + n], v, mhalf[0:rws, 0:n], ALU.pow).then_inc(rstd_ready, 1)

            def attention0():
                pool.wait_ge(emb_sb, PATCHES)
                pool.wait_ge(cls_set, 1)
                groups(pool, TILES[0], lambda t0, grp, n: norm_rstd(n, P, grp + 1), seq, 1)
                pool.wait_ge(xn_ready, TILES[0])
                pool.wait_ge(rows_loaded, 16 * 16)
                pool.tensor_tensor(R[:, 0:SEQ, :], R[:, 0:SEQ, :],
                                   proj_b[0].unsqueeze(1).broadcast_to([P, SEQ, D]), ALU.add).then_inc(rb0_ready, 1)
                for w in POOL_ROWS:
                    pool.wait_ge(qkv0_sb, position_of_window_row(w) + 1)
                    query_key(pool, w).then_inc(products, 1)
                pool.wait_ge(p0_ready, 1)
                for w in POOL_ROWS:
                    prob_value(pool, w).then_inc(weighted, 1)
                groups(pool, TILES[0], lambda t0, grp, n: norm_rstd(n, P, GROUPS[0] + grp + 1), seq, 1)

            def attention1():
                pool.wait_ge(l1_loaded, 16 * 12)

                def spread_probs(t0, g):
                    pool.wait_ge(probs, t0 + g + 1)
                    pool.tensor_tensor(
                        Pf[:, g].rearrange("p h (i j) -> p h i j", i=IPT),
                        Pc[:, g * HEADS:(g + 1) * HEADS, :].unsqueeze(2).broadcast_to([TT, HEADS, IPT, SEQ]),
                        own[:].unsqueeze(1).unsqueeze(3).broadcast_to([TT, HEADS, IPT, SEQ]),
                        ALU.mult).then_inc(spread, 1)

                for f in range(-1, A_GROUPS + 2):
                    m, b, ahead = f - 1, f - 2, f + 1
                    nm, nb, na = (min(A, TILES[1] - A * x) if 0 <= x < A_GROUPS else 0 for x in (m, b, ahead))
                    if nm:
                        if nb:
                            pool.wait_ge(pT_ps, A * b + nb)
                        spread_probs(A * m, 0)
                    if na:
                        norm_rstd(na, TT, norm_in_at(ahead))
                    for g in range(1, nm):
                        spread_probs(A * m, g)
                    if na:
                        a0 = A * ahead
                        pool.wait_ge(xn_ready, LT[1] + a0 + na)
                        for g in range(na):
                            ins = pool.tensor_tensor(R[0:TT, a0 + g, :], R[0:TT, a0 + g, :], proj_b[1][0:TT, :], ALU.add)
                        ins.then_inc(rb_ready, 1)
                    if nb:
                        norm_rstd(nb, TT, norm_out_at(b, 0), slot=A)
                        norm_rstd(nb, TT, norm_out_at(b, 1), slot=A)
                    if na:
                        for g in range(na):
                            pool.wait_ge(qk_sb, a0 + g + 1)
                            pool.tensor_tensor(Kbd[:, g], qk[:, g, 1:2, :].broadcast_to([P, HEADS, TT]),
                                               head_rows[:].unsqueeze(2).broadcast_to([P, HEADS, TT]),
                                               ALU.mult).then_inc(kbd, 1)
                        if ahead + 2 < A_GROUPS:
                            gather(0, A * (ahead + 2), min(A, TILES[1] - A * (ahead + 2)))

            def rows_of(layer, t):
                return ROWS[layer] if layer == 0 or t < TILES[1] - 1 else LAST

            def scatter(layer):
                pool.wait_ge(routing_ready, layer + 1)
                pool.wait_ge(zero_stored, 16 * (MAX_SLOT_TILES // 7 + 2))
                for t in range(TILES[layer]):
                    n = rows_of(layer, t)
                    for k in range(2):
                        pool.indirect_dma_start(
                            out=xs_dram, out_offset=bass.IndirectOffsetOnAxis(ap=choice[0:n, t, k:k + 1].bitcast(U32), axis=0),
                            in_=Z[0:n, t, :], in_offset=None).then_inc(scattered, 16)

            def gather(layer, first, tiles):
                if first == 0:
                    pool.wait_ge(y_stored, 16 * (LSG[layer] + SLOT_GROUPS[layer]))
                    if layer == 0:
                        pool.wait_ge(choice_loaded, 16)
                else:
                    pool.wait_ge(gathered, 32 * (layer * TILES[1] + first))
                for t in range(first, first + tiles):
                    n = TT if layer == 0 else rows_of(1, t)
                    for k in range(2):
                        pool.indirect_dma_start(
                            out=Y[layer][k][0:n, t, :], out_offset=None, in_=ys_dram[0:SLOT_TILES[layer] * P, :],
                            in_offset=bass.IndirectOffsetOnAxis(ap=choice[0:n, t, k:k + 1].bitcast(U32), axis=0))\
                            .then_inc(gathered, 16)

            attention0()
            scatter(0)
            gather(0, 0, A)
            gather(0, A, A)
            attention1()
            scatter(1)
            gather(1, 0, G)
            for grp in range(GROUPS[1]):
                if grp + 1 < GROUPS[1]:
                    gather(1, G * (grp + 1), min(G, TILES[1] - G * (grp + 1)))
                norm_rstd(min(G, TILES[1] - G * grp), TT, NORMS + 3 * A_GROUPS + grp + 1)

        @block.tensor
        def _(pe):
            pe.wait_ge(consts, 2)
            pe.matmul(PS[0:TT, 1, 0:TT], own_rows[:], own_rows[:], start=True, stop=True).then_inc(own_ps, 1)
            pe.wait_ge(tok_w_loaded, 16)
            for n in range(PATCHES):
                if n % 4 == 0:
                    pe.wait_ge(pixels_in[n // 4], 16)
                if n >= 4:
                    pe.wait_ge(emb_sb, n - 3)
                for c in range(PIX):
                    ins = pe.matmul(M[:, n % 4, 0:D], pixels[:, n, c, :], tokT[:, c, :],
                                    start=(c == 0), stop=(c == PIX - 1))
                ins.then_inc(emb_ps, 1)
            pe.wait_ge(pool_ready, 1)

            def turn(src, n, rws, ready, base, done, slot=0):
                for g in range(slot, slot + n):
                    pe.wait_ge(ready, base + g - slot + 1)
                    pe.transpose(M[:, g, 0:rws], src[0:rws, g, :], ident[0:rws, 0:rws]).then_inc(done, 1)

            def route_products(layer, n, base, slot=0):
                E, rws = EXPERTS[layer], ROWS[layer]
                turn(xn, n, rws, zg_ready, base, zT_ps, slot)
                for g in range(slot, slot + n):
                    pe.wait_ge(zT_sb, base + g - slot + 1)
                    pe.matmul(M[0:rws, g, 0:E], xnT[:, g, 0:rws], router_w[layer][:], start=True, stop=True)\
                        .then_inc(logit_ps, 1)

            def attention0():
                nq = QHEADS * HDIM
                pe.wait_ge(emb_sb, PATCHES)
                pe.wait_ge(l0_loaded, 16 * 3)

                def body(t0, grp, n):
                    if not is_zero(t0):
                        pe.wait_ge(qkv0_sb, t0)
                    turn(xn, n, P, xn_ready, t0, xnT_ps)
                    for g in range(n):
                        pe.wait_ge(xnT_sb, t0 + g + 1)
                        pe.matmul(M[:, g, 0:QKV0], xnT[:, g, :], qkvT[0], start=True, stop=True).then_inc(qkv_ps, 1)
                groups(pe, TILES[0], body, peel=True)
                pe.wait_ge(mixed_ready, 1)
                for k, r in enumerate(MIXED_ROWS):
                    ins = pe.transpose(PS[:, k // 4, P * (k % 4):P * (k % 4 + 1)],
                                       mixed[:, r // 8, P * (r % 8):P * (r % 8 + 1)], ident[:])
                    if k % 4 == 3 or r == MIXED_ROWS[-1]:
                        ins.then_inc(mixedT_ps, 1)
                for k, r in enumerate(MIXED_ROWS):
                    if k % 4 == 0:
                        pe.wait_ge(mixedT_sb, k // 4 + 1)
                    ins = pe.matmul(M[:, k // 4, P * (k % 4):P * (k % 4 + 1)], mixedT[:, k, :], projT[0],
                                    start=True, stop=True)
                ins.then_inc(proj0_ps, 1)
                groups(pe, TILES[0], lambda t0, grp, n: route_products(0, n, t0))

            def attention1():
                L = LT[1]
                wq, wk, wv = (qkvT[1][:, k * D:(k + 1) * D] for k in range(3))
                pe.wait_ge(l1_loaded, 16 * 12)

                def projections(t0, n):
                    turn(xn, n, TT, xn_ready, L + t0, xnT_ps)
                    for g in range(n):
                        pe.wait_ge(xnT_sb, L + t0 + g + 1)
                        pe.matmul(M[:, g, 0:TT], wq, xnT[:, g, 0:TT], start=True, stop=True)
                        pe.matmul(M[:, g, 120:120 + TT], wk, xnT[:, g, 0:TT], start=True, stop=True)
                        pe.matmul(M[0:TT, g, 256:384], xnT[:, g, 0:TT], wv, start=True, stop=True)
                        pe.matmul(M[:, g, 384:384 + TT], xn[0:TT, g, :], pool_mean[:], start=True, stop=True)\
                            .then_inc(qkv_ps, 1)

                def scores(t0, g):
                    pe.wait_ge(kbd, t0 + g + 1)
                    if g:
                        pe.wait_ge(packed, t0 + g)
                    for b in range(2):
                        bank = PS[0:TT, 0, 512 * b:512 * b + 4 * TT]
                        pe.matmul(bank, own_rows[:], other[:].rearrange("p h t -> p (h t)"), start=True, stop=False)
                        ins = pe.matmul(bank, qk[:, g, 0, :], Kbd[:, g, 4 * b:4 * b + 4, :].rearrange("p h t -> p (h t)"),
                                        start=False, stop=True)
                    ins.then_inc(scores_ps, 1)

                def pattern(t0, n, layer):
                    for g in range(n):
                        if layer == 1:
                            pe.wait_ge(pl_sb, t0 + g + 1)
                            pe.matmul(M[:, g, 0:TT], ps1T[:], oT[:, g, :], start=True, stop=True).then_inc(h1_ps, 1)
                        if layer == 2:
                            pe.wait_ge(h1_sb, t0 + g + 1)
                            pe.matmul(M[0:64, g, 0:TT], ps2T[:], xnT[:, g, 0:TT], start=True, stop=True).then_inc(h2_ps, 1)
                        if layer == 3:
                            pe.wait_ge(h2_sb, t0 + g + 1)
                            pe.matmul(M[0:TT, g, 0:3], oT[0:64, g, :], ps3T[:], start=True, stop=True).then_inc(l3_ps, 1)

                def turn_probs(t0, g):
                    pe.wait_ge(spread, t0 + g + 1)
                    for h in range(HEADS):
                        o = 512 * (h // 4) + TT * (h % 4)
                        ins = pe.transpose(PS[0:TT, 1, o:o + TT], Pf[:, g, h, :], ident[0:TT, 0:TT])
                    ins.then_inc(pT_ps, 1)

                def probs_values(t0, grp, g):
                    pe.wait_ge(pT_sb, t0 + g + 1)
                    pe.wait_ge(v_sb, t0 + g + 1)
                    if g == 0:
                        pe.wait_ge(logits_ready, L + t0)
                    v = vs[:, bass.ds((grp & 3) * A + g, 1), :].rearrange("p a d -> p (a d)")
                    for h in range(HEADS):
                        ins = pe.matmul(M[0:TT, A + g, h * HDIM:(h + 1) * HDIM], PT[:, g, h, :],
                                        v[:, h * HDIM:(h + 1) * HDIM], start=True, stop=True)
                    ins.then_inc(o_ps, 1)

                def step(f, nf, m, nm, b, nb, ahead, na):
                    f0, b0, a0 = tiles_before(f, b, ahead)
                    if nb:
                        turn_probs(b0, 0)
                    pattern(f0, nf, 1)
                    if nb:
                        probs_values(b0, b, 0)
                    if nb > 1:
                        turn_probs(b0, 1)
                    pattern(f0, nf, 2)
                    if nb > 1:
                        probs_values(b0, b, 1)
                    pattern(f0, nf, 3)
                    if nf:
                        scores(f0, 0)
                    if nb:
                        turn(osb, nb, TT, o_sb, b0, oT_ps, slot=A)
                        for g in range(nb):
                            pe.wait_ge(oT_sb, b0 + g + 1)
                            pe.matmul(M[0:TT, A + g, 0:D], oT[:, A + g, :], projT[1], start=True, stop=True)\
                                .then_inc(proj_ps, 1)
                    if nf > 1:
                        scores(f0, 1)
                    if na:
                        projections(a0, na)
                    if nb:
                        route_products(1, nb, L + b0, slot=A)
                overlapped(pe, step)

            def rank(layer):
                rws, n = ROWS[layer], TILES[layer] * EXPERTS[layer]
                pe.wait_ge(routed_ready, layer + 1)
                chosen = routed[0:rws, 0:TILES[layer], 0:EXPERTS[layer]]
                pe.matmul(PS[0:rws, 0, 0:n], before[0:rws, 0:rws], chosen, start=True, stop=True)
                pe.matmul(PS[0:rws, 1, 0:n], ones_b[0:rws, 0:rws], chosen, start=True, stop=True).then_inc(rank_ps, 1)

            def hidden_down(n, at, hidT_, chunks, rhs, y_sem, ready, hid_, rws):
                def turn_hidden(g):
                    pe.wait_ge(ready, at(g))
                    for c in range(chunks):
                        ins = pe.transpose(hT_bank[g][:, P * c:P * c + rws],
                                           hid_[0:rws, g, P * c:P * (c + 1)], ident[0:rws, 0:rws])
                    ins.then_inc(hT_ps, 1)

                def down(g):
                    pe.wait_ge(hT_sb, at(g))
                    for c in range(chunks):
                        ins = pe.matmul(M[0:rws, g, 0:D], hidT_[:, g, P * c:P * c + rws], rhs(g, c),
                                        start=(c == 0), stop=(c == chunks - 1))
                    ins.then_inc(y_sem, 1)
                for g in range(n):
                    turn_hidden(g)
                    if g:
                        down(g - 1)
                down(n - 1)

            def experts(layer):
                L = LS[layer]

                def turn_inputs(grp, n):
                    pe.wait_ge(xs_in, 16 * (LSG[layer] + grp + 1))
                    for g in range(n):
                        ins = pe.transpose(xsT_bank[:, g, :], xs[:, g, :], ident[:])
                    ins.then_inc(xsT_ps, 1)

                def body(t0, grp, n, n_behind):
                    e = experts_of_group(pe, layer, grp, n)
                    pe.wait_ge(xsT_sb, LSG[layer] + grp + 1)
                    if layer or not is_zero(t0):
                        pe.wait_ge(y_sb, L + t0)
                    for g in range(n):
                        pe.matmul(M[:, g, :], xsT[:, g, :], W1[layer][:, bass.ds(e[g], 1), :].rearrange("p a f -> p (a f)"),
                                  start=True, stop=True).then_inc(up_ps, 1)
                    if n_behind:
                        turn_inputs(grp + 1, n_behind)
                    hidden_down(n, lambda g: H[layer] + t0 + g + 1, hidT, FC,
                                lambda g, c: W2[layer][:, bass.ds(e[g], 1), c, :].rearrange("p a d -> p (a d)"),
                                y_ps, hid_ready, hid, P)
                turn_inputs(0, G)
                pe.wait_ge(w0_loaded, 16 * 4)
                pe.wait_ge(routing_ready, layer + 1)
                if layer:
                    pe.wait_ge(w1a_loaded, 16)
                    pe.wait_ge(w1b_loaded, 32)
                pipelined(pe, SLOT_TILES[layer], body)

            attention0()
            rank(0)
            experts(0)
            attention1()
            rank(1)
            def shared(t0, grp, n):
                turn(xn, n, TT, zg_ready, LT[1] + TILES[1] + t0, zT_ps)
                for g in range(n):
                    pe.wait_ge(zT_sb, LT[1] + TILES[1] + t0 + g + 1)
                    pe.matmul(M[0:TT, g, 0:SHARED], xnT[:, g, 0:TT], sw1[:], start=True, stop=True).then_inc(up_ps, 1)
                hidden_down(n, lambda g: HS + t0 + g + 1, hidT, SC, lambda g, c: sw2[:, c, :], y_ps,
                            hid_ready, hid, TT)
            groups(pe, TILES[1], shared)
            pe.wait_ge(shared_ready, TILES[1])
            experts(1)

            def turn_normed(t0, n):
                for g in range(n):
                    pe.wait_ge(zg_ready, LT[1] + 2 * TILES[1] + t0 + g + 1)
                    ins = pe.transpose(xsT_bank[:, g, 0:TT], xn[0:TT, g, :], ident[0:TT, 0:TT])
                ins.then_inc(fT_ps, 1)

            def last(t0, grp, n, n_behind):
                pe.wait_ge(fT_sb, grp + 1)
                if not is_zero(t0):
                    pe.wait_ge(combined, t0)
                for g in range(n):
                    pe.matmul(M[0:TT, g, :], xnT[:, g, 0:TT], fw1[:], start=True, stop=True).then_inc(up_ps, 1)
                hidden_down(n, lambda g: HF + t0 + g + 1, fhidT, FC, lambda g, c: fw2[:, c, :], y_ps,
                            hid_ready, fhid, TT)
                if n_behind:
                    turn_normed(t0 + G, n_behind)
            turn_normed(0, G)
            pipelined(pe, TILES[1], last)

        @block.scalar
        def _(act):
            act.wait_ge(own_ps, 1)
            act.activation(pool_mean[:], PS[0:TT, 1, 0:TT], ACT.Copy, scale=1.0 / SEQ).then_inc(pool_ready, 1)
            act.wait_ge(tok_rows_loaded, 32)
            act.activation(R[:, 0, :], row["cls_tok"], ACT.Copy).then_inc(cls_set, 1)

            def evacuate(n, base, wait, dst, src, sem):
                for g in range(n):
                    act.wait_ge(wait, base + g + 1)
                    act.activation(dst(g), src(g), ACT.Copy).then_inc(sem, 1)

            def turned(n, base, rws, wait, dst, sem, slot=0):
                evacuate(n, base, wait, lambda g: dst[:, slot + g, 0:rws], lambda g: M[:, slot + g, 0:rws], sem)

            def attention0():
                def body(t0, grp, n):
                    turned(n, t0, P, xnT_ps, xnT, xnT_sb)
                    evacuate(n, t0, qkv_ps, lambda g: tile(qkv0, t0 + g, P), lambda g: M[:, g, 0:QKV0], qkv0_sb)
                groups(act, TILES[0], body)
                act.wait_ge(s0_shifted, 1)
                act.activation(p0, s0, ACT.Exp).then_inc(p0_exp, 1)
                for k in range(2):
                    act.wait_ge(mixedT_ps, k + 1)
                    m = min(4, len(MIXED_ROWS) - 4 * k)
                    act.activation(mixedT[:, 4 * k:4 * k + m, :].rearrange("p r b -> p (r b)"), PS[:, k, 0:m * P],
                                   ACT.Copy).then_inc(mixedT_sb, 1)
                groups(act, TILES[0], lambda t0, grp, n: turned(n, t0, P, zT_ps, xnT, zT_sb))

            def attention1():
                L = LT[1]
                act.wait_ge(l1_loaded, 16 * 12)

                def projections(t0, grp, n):
                    turned(n, L + t0, TT, xnT_ps, xnT, xnT_sb)
                    for g in range(n):
                        act.wait_ge(qkv_ps, L + t0 + g + 1)
                        act.activation(qk[:, g], M[:, g, 0:240].rearrange("p (a t) -> p a t", a=2)[:, :, 0:TT],
                                       ACT.Copy).then_inc(qk_sb, 1)
                        act.activation(vs[:, bass.ds((grp & 3) * A + g, 1), :].rearrange("p a d -> p (a d)"),
                                       M[0:TT, g, 256:384], ACT.Copy).then_inc(v_sb, 1)
                        act.activation(oT[:, g, :], M[:, g, 384:384 + TT], ACT.Copy).then_inc(pl_sb, 1)

                def pT(t0, g):
                    act.wait_ge(pT_ps, t0 + g + 1)
                    act.activation(PT[:, g].rearrange("p (b h) t -> p b (h t)", b=2),
                                   PS[0:TT, 1, :].rearrange("p (b x) -> p b x", b=2)[:, :, 0:4 * TT],
                                   ACT.Copy).then_inc(pT_sb, 1)

                def o(t0, g):
                    act.wait_ge(o_ps, t0 + g + 1)
                    act.activation(osb[:, A + g, :], M[0:TT, A + g, 0:D], ACT.Copy).then_inc(o_sb, 1)

                def step(f, nf, m, nm, b, nb, ahead, na):
                    f0, b0, a0 = tiles_before(f, b, ahead)
                    if nb:
                        pT(b0, 0)
                    for g in range(nf):
                        act.wait_ge(h1_ps, f0 + g + 1)
                        act.activation(xnT[:, g, 0:TT], M[:, g, 0:TT], ACT.Relu, bias=cols[:, 0:1]).then_inc(h1_sb, 1)
                    if nb:
                        o(b0, 0)
                    if nm:
                        if nb:
                            act.wait_ge(spread, b0 + nb)
                        act.wait_ge(shifted, m + 1)
                        act.activation(Pc[:, 0:nm * HEADS, :], Sc[:, 0:nm * HEADS, :], ACT.Exp).then_inc(exp_done, 1)
                    if nb > 1:
                        pT(b0, 1)
                    for g in range(nf):
                        act.wait_ge(h2_ps, f0 + g + 1)
                        act.activation(oT[0:64, g, :], M[0:64, g, 0:TT], ACT.Relu, bias=cols[0:64, 1:2]).then_inc(h2_sb, 1)
                    if nb > 1:
                        o(b0, 1)
                    if nf:
                        act.wait_ge(l3_shifted, f + 1)
                        act.activation(e3[:, 0:nf, :], l3[:, 0:nf, :], ACT.Exp, scale=1.0 / PATTERN_TEMPERATURE)\
                            .then_inc(e3_done, 1)
                    if nb:
                        turned(nb, b0, TT, oT_ps, oT, oT_sb, slot=A)
                    if na:
                        projections(a0, ahead, na)
                    if nb:
                        turned(nb, L + b0, TT, zT_ps, xnT, zT_sb, slot=A)
                overlapped(act, step)

            def route(layer):
                n = TILES[layer] * EXPERTS[layer]
                act.wait_ge(route_shifted, layer + 1)
                act.activation(small(1, [n])[0:ROWS[layer]], small(0, [n])[0:ROWS[layer]], ACT.Exp,
                               scale=1.0 / TEMPERATURE[layer]).then_inc(route_exp, 1)

            def hidden(n, func, base, hbase, rws, width, hid_, hidT_):
                for g in range(n):
                    act.wait_ge(hid_biased, hbase + g + 1)
                    act.activation(hid_[0:rws, g, 0:width], hid_[0:rws, g, 0:width], func).then_inc(hid_ready, 1)
                for g in range(n):
                    act.wait_ge(hT_ps, hbase + g + 1)
                    act.activation(hidT_[:, g, 0:width].rearrange("p (c r) -> p c r", r=P)[:, :, 0:rws],
                                   hT_bank[g][:, 0:width].rearrange("p (c r) -> p c r", r=P)[:, :, 0:rws],
                                   ACT.Copy).then_inc(hT_sb, 1)

            def experts(layer):
                def body(t0, grp, n):
                    hidden(n, (ACT.Gelu, ACT.Silu)[layer], LS[layer] + t0, H[layer] + t0, P, FF, hid, hidT)
                groups(act, SLOT_TILES[layer], body)

            attention0()
            route(0)
            experts(0)
            attention1()
            route(1)

            def shared(t0, grp, n):
                turned(n, LT[1] + TILES[1] + t0, TT, zT_ps, xnT, zT_sb)
                hidden(n, ACT.Silu, 0, HS + t0, TT, SHARED, hid, hidT)
            groups(act, TILES[1], shared)
            experts(1)

            def take_normed(grp, n):
                act.wait_ge(fT_ps, grp + 1)
                act.activation(xnT[:, 0:n, 0:TT], xsT_bank[:, 0:n, 0:TT], ACT.Copy).then_inc(fT_sb, 1)

            def last(t0, grp, n, n_behind):
                hidden(n, ACT.Silu, 0, HF + t0, TT, FF, fhid, fhidT)
                if n_behind:
                    take_normed(grp + 1, n_behind)
            take_normed(0, G)
            pipelined(act, TILES[1], last)

        @block.vector
        def _(dve):
            seq = Seq(dve, dve_step)
            dve.wait_ge(tok_rows_loaded, 32)
            for n in range(PATCHES):
                dve.wait_ge(emb_ps, n + 1)
                dve.tensor_tensor(R[:, n + 1, :], M[:, n % 4, 0:D], row["L0_tok_b"], ALU.add).then_inc(emb_sb, 1)
            dve.wait_ge(consts, 2)
            dve.wait_ge(emb_sb, PATCHES)
            dve.wait_ge(cls_set, 1)

            def carry_wait():
                dve.tensor_copy(carrier[:, 1:2], carrier[:, 0:1])

            def announce(sem):
                dve.tensor_copy(carrier[:, 2:3], carrier[:, 0:1]).then_inc(sem, 1)

            def mean_var(n, rws, src, slot=0):
                carry_wait()
                for g in range(n):
                    seq.mark(dve.bn_stats(stats[0:rws, slot + g, :], src(g)))
                seq.sync()
                carry_wait()
                for g in range(n):
                    ins = dve.bn_aggr(mv[0:rws, slot + g, :], stats[0:rws, slot + g, :])
                ins.then_inc(mean_var_ready, 1)

            def mean_rstd(n, rws, src, at):
                mean_var(n, rws, src)
                dve.wait_ge(rstd_ready, at)

            def normalize(n, rws, src, dst, sem):
                for g in range(n):
                    dve.tensor_scalar(dst(g), src(g), mv[0:rws, g, 0:1], rs[0:rws, g:g + 1],
                                      ALU.subtract, ALU.mult).then_inc(sem, 1)

            def reduce(out_, in_, op):
                seq.mark(dve.tensor_reduce(out_, in_, AX.X, op))

            def norm_in(t0, n, at):
                mean_rstd(n, P, lambda g: tile(R, t0 + g, P), at)
                if not is_zero(t0):
                    dve.wait_ge(xnT_ps, t0)
                normalize(n, P, lambda g: tile(R, t0 + g, P), lambda g: xn[:, g, :], xn_ready)

            def keep_normed(layer, t0, n, ready, slot=0):
                rws = ROWS[layer]
                dve.wait_ge(zg_ready, ready)
                for g in range(n):
                    dve.tensor_copy(tile(Z, t0 + g, rws), xn[0:rws, slot + g, :]).then_inc(z_ready, 1)

            def take_logits(layer, t0, n, slot=0):
                rws, E = ROWS[layer], EXPERTS[layer]
                for g in range(n):
                    dve.wait_ge(logit_ps, LT[layer] + t0 + g + 1)
                    dve.tensor_tensor(logits[0:rws, bass.ds(t0 + g, 1), 0:E].rearrange("p a d -> p (a d)"),
                                      M[0:rws, slot + g, 0:E], router_b[layer][0:rws, :], ALU.add).then_inc(logits_ready, 1)

            def attention0():
                groups(dve, TILES[0], lambda t0, grp, n: norm_in(t0, n, grp + 1), seq, G, peel=True)
                for w in range(SEQ):
                    if w in DVE_ROWS:
                        dve.wait_ge(qkv0_sb, position_of_window_row(w) + 1)
                        seq.step(query_key(dve, w))
                    else:
                        dve.wait_ge(products, POOL_ROWS.index(w) + 1)
                    reduce(s0[:, w, 0:heads_of(w)], prods_of(w, HDIM), ALU.add)
                seq.sync()
                n = SEQ * QHEADS
                flat = lambda t: t.rearrange("p w h g -> p (w h) g")
                each = lambda t: t[:, 0:n].unsqueeze(2).broadcast_to([P, n, HEADS])
                seq.step(dve.tensor_scalar(s0, s0, float(HDIM) ** -0.5, None, ALU.mult))
                reduce(mx[:, 0:n], flat(s0), ALU.max)
                seq.sync()
                dve.tensor_tensor(flat(s0), flat(s0), each(mx), ALU.subtract).then_inc(s0_shifted, 1)
                dve.wait_ge(p0_exp, 1)
                reduce(sm[:, 0:n], flat(p0), ALU.add)
                seq.sync()
                seq.step(dve.reciprocal(mx[:, 0:n], sm[:, 0:n]))
                dve.tensor_tensor(flat(p0), flat(p0), each(mx), ALU.mult).then_inc(p0_ready, 1)
                dve.wait_ge(p0_ready, 1)
                for w in range(SEQ):
                    if w in DVE_ROWS:
                        seq.sync()
                        seq.step(prob_value(dve, w))
                    else:
                        dve.wait_ge(weighted, POOL_ROWS.index(w) + 1)
                    reduce(mixed[:, 0:heads_of(w), w * HDIM:(w + 1) * HDIM], prods_of(w, HEADS), ALU.add)
                seq.sync()
                announce(mixed_ready)
                dve.wait_ge(rb0_ready, 1)
                dve.wait_ge(proj0_ps, 1)
                for k, r in enumerate(MIXED_ROWS):
                    t = position_of_window_row(r)
                    seq.mark(dve.tensor_tensor(R[:, t, :], M[:, k // 4, P * (k % 4):P * (k % 4 + 1)], R[:, t, :], ALU.add))
                seq.sync()
                announce(attn0_done)

                def body(t0, grp, n):
                    mean_rstd(n, P, lambda g: tile(R, t0 + g, P), GROUPS[0] + grp + 1)
                    normalize(n, P, lambda g: tile(R, t0 + g, P), lambda g: xn[:, g, :], zg_ready)
                    keep_normed(0, t0, n, t0 + n)
                    take_logits(0, t0, n)
                groups(dve, TILES[0], body, seq, G)

            def combine(layer, t0, n, onto, to):
                for k in range(2):
                    for g in range(n):
                        weight = choice[0:TT, bass.ds(t0 + g, 1), 2 + k:3 + k].rearrange("p a b -> p (a b)")
                        seq.mark(dve.scalar_tensor_tensor(
                            to[0:TT, g, :] if k and to is Rb else tile(onto, t0 + g, TT),
                            tile(Y[layer][k], t0 + g, TT), weight, tile(onto, t0 + g, TT), ALU.mult, ALU.add))
                    seq.sync()

            def sparse_keys(n):
                N = n * HEADS
                by_head = lambda k: minus_sparse[0:TT, k, :].unsqueeze(1).unsqueeze(3).broadcast_to([TT, n, HEADS, SEQ])
                g4 = lambda t: t[:, 0:N, :].rearrange("p (g h) j -> p g h j", g=n)
                seq.step(dve.tensor_tensor(g4(drop_key), g4(Sc), by_head(0), ALU.mult))
                seq.step(dve.tensor_tensor(g4(drop_key), g4(drop_key), by_head(1), ALU.add))

            def drop_keys(n):
                N = n * HEADS
                carry_wait()
                for r in range(N):
                    ins = dve.max(top8[:, r, :], drop_key[:, r, :])
                seq.step(ins)
                least = top8[:, 0:N, DROP - 1:DROP].broadcast_to([TT, N, SEQ])
                seq.mark(dve.tensor_tensor(drop_ge[:, 0:N], drop_key[:, 0:N], least, ALU.is_ge))
                seq.step(dve.tensor_tensor(drop_eq[:, 0:N], drop_key[:, 0:N], least, ALU.is_equal))
                reduce(drop_n[:, 0:N], drop_ge[:, 0:N], ALU.add)
                flat = lambda t: t[:, 0:N, :].rearrange("p r j -> p (r j)")
                seq.step(dve.tensor_tensor_scan(flat(drop_cum), flat(carry), flat(drop_eq), 0.0, ALU.mult, ALU.add))
                seq.step(dve.tensor_scalar(drop_n[:, 0:N], drop_n[:, 0:N], float(DROP), None, ALU.subtract))
                seq.step(dve.tensor_tensor(drop_cum[:, 0:N], drop_cum[:, 0:N],
                                           drop_n[:, 0:N].unsqueeze(2).broadcast_to([TT, N, SEQ]), ALU.is_le))
                seq.step(dve.tensor_tensor(drop_eq[:, 0:N], drop_eq[:, 0:N], drop_cum[:, 0:N], ALU.mult))
                seq.step(dve.tensor_tensor(drop_ge[:, 0:N], drop_ge[:, 0:N], drop_eq[:, 0:N], ALU.subtract))

            def attention1():
                L = LT[1]
                dve.wait_ge(l1_loaded, 16 * 12)
                dve.wait_ge(rows_loaded, 16 * 16)
                seq.mark(dve.tensor_scalar(minus_sparse[:, 0, :], row["L1_attn_sparse_w"], -1.0, None, ALU.mult))
                seq.mark(dve.tensor_scalar(minus_sparse[:, 1, :], row["L1_attn_sparse_b"], -1.0, None, ALU.mult))
                seq.mark(dve.tensor_tensor(pattern_b[:], row["L1_attn_ps_b3"], row["L1_attn_pattern_bias"], ALU.add))
                seq.sync()

                def front_in(j, n):
                    t0 = A * j
                    dve.wait_ge(gathered, 32 * (t0 + n))
                    combine(0, t0, n, R, R)
                    mean_var(n, TT, lambda g: tile(R, t0 + g, TT))

                def front_normed(j, n):
                    dve.wait_ge(rstd_ready, norm_in_at(j))
                    normalize(n, TT, lambda g: tile(R, A * j + g, TT), lambda g: xn[0:TT, g, :], xn_ready)
                    announce(experts_added)

                def pack(t0, g):
                    dve.wait_ge(scores_ps, t0 + g + 1)
                    for b in range(2):
                        ins = dve.tensor_reduce(
                            Sc[:, g * HEADS + 4 * b:g * HEADS + 4 * b + 4, :],
                            PS[0:TT, 0, 512 * b:512 * b + 4 * TT].rearrange("p (h i j) -> p h j i", h=4, i=IPT),
                            AX.X, ALU.max)
                    ins.then_inc(packed, 1)

                def pattern_logits(t0, n):
                    for g in range(n):
                        dve.wait_ge(l3_ps, t0 + g + 1)
                        seq.mark(dve.tensor_tensor(l3[:, g, :], M[0:TT, g, 0:3], pattern_b[0:TT, :], ALU.add))
                    seq.sync()
                    reduce(g1[:, 0:n], l3[:, 0:n], ALU.max)
                    seq.sync()
                    dve.tensor_tensor(l3[:, 0:n], l3[:, 0:n], g1[:, 0:n].unsqueeze(2).broadcast_to([TT, n, 3]),
                                      ALU.subtract).then_inc(l3_shifted, 1)

                def gate_keys(j, n):
                    dve.wait_ge(e3_done, j + 1)
                    reduce(g1[:, 0:n], e3[:, 0:n], ALU.add)
                    seq.sync()
                    seq.step(dve.reciprocal(g2[:, 0:n], g1[:, 0:n]))
                    seq.step(dve.tensor_tensor(e3[:, 0:n], e3[:, 0:n], g2[:, 0:n].unsqueeze(2).broadcast_to([TT, n, 3]),
                                               ALU.mult))
                    seq.step(dve.tensor_tensor(g1[:, 0:n], e3[:, 0:n, 0], e3[:, 0:n, 1], ALU.add))
                    seq.step(dve.tensor_scalar(g2[:, 0:n], g1[:, 0:n], 0.05, NEG, ALU.is_le, ALU.mult))
                    for g in range(n):
                        h = slice(g * HEADS, (g + 1) * HEADS)
                        seq.mark(dve.scalar_tensor_tensor(Sc[:, h, :], drop_ge[:, h, :], g2[:, g:g + 1], Sc[:, h, :],
                                                          ALU.mult, ALU.add))
                    seq.sync()

                def softmax(j, n):
                    N = n * HEADS
                    reduce(mx[0:TT, 0:N], Sc[:, 0:N, :], ALU.max)
                    seq.sync()
                    dve.tensor_tensor(Sc[:, 0:N, :], Sc[:, 0:N, :], mx[0:TT, 0:N].unsqueeze(2).broadcast_to([TT, N, SEQ]),
                                      ALU.subtract).then_inc(shifted, 1)
                    dve.wait_ge(exp_done, j + 1)
                    reduce(sm[0:TT, 0:N], Pc[:, 0:N, :], ALU.add)
                    seq.sync()
                    seq.step(dve.reciprocal(mx[0:TT, 0:N], sm[0:TT, 0:N]))
                    for g in range(n):
                        h = slice(g * HEADS, (g + 1) * HEADS)
                        dve.tensor_tensor(Pc[:, h, :], Pc[:, h, :],
                                          mx[0:TT, h].unsqueeze(2).broadcast_to([TT, HEADS, SEQ]),
                                          ALU.mult).then_inc(probs, 1)

                def residual(i, t0, n):
                    dve.wait_ge(rb_ready, i + 1)
                    for g in range(n):
                        dve.wait_ge(proj_ps, t0 + g + 1)
                        seq.mark(dve.tensor_tensor(tile(R, t0 + g, TT), M[0:TT, A + g, 0:D], tile(R, t0 + g, TT), ALU.add))
                    seq.sync()
                    mean_var(n, TT, lambda g: tile(R, t0 + g, TT), slot=A)

                def add_norm(i, t0, n):
                    dve.wait_ge(rstd_ready, norm_out_at(i, 0))
                    for g in range(n):
                        seq.mark(dve.tensor_scalar(Rb[0:TT, g, :], tile(R, t0 + g, TT), mv[0:TT, A + g, 0:1],
                                                   rs[0:TT, A + g:A + g + 1], ALU.subtract, ALU.mult))
                    seq.sync()
                    for g in range(n):
                        seq.mark(dve.tensor_tensor(tile(R, t0 + g, TT), tile(R, t0 + g, TT), Rb[0:TT, g, :], ALU.add))
                    mean_var(n, TT, lambda g: Rb[0:TT, g, :], slot=A)

                def step(f, nf, m, nm, b, nb, ahead, na):
                    f0, b0 = tiles_before(f, b)
                    if nm:
                        drop_keys(nm)
                        gate_keys(m, nm)
                        softmax(m, nm)
                    if na:
                        front_in(ahead, na)
                    if nf:
                        pattern_logits(f0, nf)
                    if na:
                        front_normed(ahead, na)
                    if nf:
                        pack(f0, 0)
                    if nb:
                        residual(b, b0, nb)
                    if nf > 1:
                        pack(f0, 1)
                    if nb:
                        add_norm(b, b0, nb)
                    if nf:
                        dve.wait_ge(packed, f0 + nf)
                        sparse_keys(nf)
                    if nb:
                        dve.wait_ge(rstd_ready, norm_out_at(b, 1))
                        scaled_norm(nb, Rb, row["L1_ffn_ln_in_g"], row["L1_ffn_ln_in_b"], slot=A)
                        keep_normed(1, b0, nb, L + b0 + nb, slot=A)
                        take_logits(1, b0, nb, slot=A)
                overlapped(dve, step, seq, 11 * A + 21)

            def scaled_norm(n, src, gain, shift, slot=0):
                both = lambda v: v[0:TT, :].unsqueeze(1).broadcast_to([TT, n, D])
                for g in range(n):
                    seq.mark(dve.tensor_scalar(xn[0:TT, slot + g, :], src[0:TT, g, :], mv[0:TT, slot + g, 0:1],
                                               rs[0:TT, slot + g:slot + g + 1],
                                               ALU.subtract, ALU.mult))
                seq.sync()
                seq.step(dve.tensor_tensor(xn[0:TT, slot:slot + n, :], xn[0:TT, slot:slot + n, :], both(gain), ALU.mult))
                for g in range(n):
                    dve.tensor_tensor(xn[0:TT, slot + g, :], xn[0:TT, slot + g, :], shift[0:TT, :], ALU.add).then_inc(zg_ready, 1)

            def route(layer):
                rws, T, E = ROWS[layer], TILES[layer], EXPERTS[layer]

                def buf(k, shape=(T, E)):
                    return small(k, list(shape))[0:rws]

                def each(t):
                    return t.unsqueeze(2).broadcast_to([rws, T, E])
                lg = logits[0:rws, 0:T, 0:E]
                top, sum_, w0, w1, tmp = (small(12, [5, T])[0:rws, k, :] for k in range(5))
                fall = falling[0:rws, 16 - E:16].unsqueeze(1).broadcast_to([rws, T, E])
                dve.wait_ge(logits_ready, LT[layer] + T)
                reduce(top, lg, ALU.max)
                seq.sync()
                d, p, M0, M1, key = buf(0), buf(1), buf(2), buf(3), buf(4)
                dve.tensor_tensor(d, lg, each(top), ALU.subtract).then_inc(route_shifted, 1)
                dve.wait_ge(route_shifted, layer + 1)
                dve.wait_ge(route_exp, layer + 1)

                def first_largest(v, out_):
                    seq.step(dve.tensor_tensor(key, v, each(tmp), ALU.is_ge))
                    seq.step(dve.tensor_tensor(key, key, fall, ALU.mult))
                    reduce(tmp, key, ALU.max)
                    seq.sync()
                    seq.step(dve.tensor_tensor(out_, key, each(tmp), ALU.is_equal))
                reduce(tmp, d, ALU.max)
                seq.sync()
                first_largest(d, M0)
                seq.step(dve.scalar_tensor_tensor(d, M0, NEG, d, ALU.mult, ALU.add))
                reduce(tmp, d, ALU.max)
                seq.sync()
                first_largest(d, M1)
                reduce(sum_, p, ALU.add)
                for m, w in ((M0, w0), (M1, w1)):
                    seq.step(dve.tensor_tensor(key, p, m, ALU.mult))
                    reduce(w, key, ALU.add)
                    seq.sync()
                seq.step(dve.reciprocal(tmp, sum_))
                for k, w in enumerate((w0, w1)):
                    seq.mark(dve.tensor_tensor(w if layer == 0 else choice[0:rws, 0:T, 2 + k], w, tmp, ALU.mult))
                seq.sync()
                if layer == 0:
                    seq.step(dve.scalar_tensor_tensor(sum_, w0, 1e-9, w1, ALU.add, ALU.add))
                    seq.step(dve.reciprocal(tmp, sum_))
                    for k, w in enumerate((w0, w1)):
                        seq.mark(dve.tensor_tensor(choice[0:rws, 0:T, 2 + k], w, tmp, ALU.mult))
                seq.step(dve.tensor_tensor(routed[0:rws, 0:T, 0:E], M0, M1, ALU.add))
                if layer:
                    seq.step(dve.tensor_scalar(routed[0:rws, T - 1, 0:E], routed[0:rws, T - 1, 0:E],
                                               is_last[0:rws, 0:1], None, ALU.mult))
                announce(routed_ready)
                dve.wait_ge(rank_ps, layer + 1)
                per_tile, incl, excl = (buf(k, (E, T + 1)) for k in (5, 6, 7))
                totals, padded = small(13, [2, E])[0:rws, 0, :], small(13, [2, E])[0:rws, 1, :]
                n = T * E
                seq.step(dve.tensor_copy(per_tile[:, :, 0:T], PS[0:rws, 1, 0:n].rearrange("p (t e) -> p e t", e=E)))
                reduce(totals, per_tile[:, :, 0:T], ALU.add)
                seq.sync()
                seq.step(dve.tensor_scalar(count_i[0:rws, 0, 0:E], totals, float(P - 1), None, ALU.add))
                seq.step(dve.tensor_scalar(count_i[0:rws, 1, 0:E], count_i[0:rws, 0, 0:E], 7, 7,
                                           ALU.arith_shift_right, ALU.logical_shift_left))
                seq.step(dve.tensor_copy(padded, count_i[0:rws, 1, 0:E]))
                seq.step(dve.tensor_tensor(per_tile[:, :, T], padded, totals, ALU.subtract))
                flat = lambda t: t.rearrange("p e t -> p (e t)")
                seq.step(dve.tensor_tensor_scan(flat(incl), ones_f[0:rws, 0:E * (T + 1)], flat(per_tile), 0.0,
                                                ALU.mult, ALU.add))
                seq.step(dve.tensor_tensor(excl, incl, per_tile, ALU.subtract))
                slot = buf(8)
                seq.step(dve.tensor_tensor(slot, PS[0:rws, 0, 0:n].rearrange("p (t e) -> p t e", e=E),
                                           excl[:, :, 0:T].rearrange("p e t -> p t e"), ALU.add))
                for k, m in enumerate((M0, M1)):
                    seq.step(dve.tensor_tensor(key, slot, m, ALU.mult))
                    reduce(tmp, key, ALU.add)
                    seq.sync()
                    seq.step(dve.tensor_copy(choice[0:rws, 0:T, k].bitcast(I32), tmp))
                NT = G * SLOT_GROUPS[layer]
                ends = small(9, [NT * (E - 1)])[0:1].rearrange("p (i e) -> p i e", e=E - 1)
                seq.step(dve.tensor_tensor(ends, slot0[0:1, 0:NT].unsqueeze(2).broadcast_to([1, NT, E - 1]),
                                           incl[0:1, 0:E - 1, T].unsqueeze(1).broadcast_to([1, NT, E - 1]), ALU.is_ge))
                last_end, group_of = small(14, [SLOT_GROUPS[layer], G])[0:1], small(15, [SLOT_GROUPS[layer]])[0:1]
                reduce(last_end.rearrange("p i g -> p (i g)"), ends, ALU.add)
                seq.sync()
                seq.step(dve.tensor_tensor(last_end, last_end,
                                           radix[:].unsqueeze(1).broadcast_to([1, SLOT_GROUPS[layer], G]), ALU.mult))
                reduce(group_of, last_end, ALU.add)
                seq.sync()
                dve.tensor_copy(expert_of[0:1, 0:SLOT_GROUPS[layer]], group_of).then_inc(routing_ready, 1)

            def experts(layer):
                def inputs_turned(grp, n):
                    dve.wait_ge(xsT_ps, LSG[layer] + grp + 1)
                    dve.tensor_copy(xsT[:, 0:n, :], xsT_bank[:, 0:n, :]).then_inc(xsT_sb, 1)

                def body(t0, grp, n, n_behind):
                    e = experts_of_group(dve, layer, grp, n)
                    for g in range(n):
                        dve.wait_ge(up_ps, H[layer] + t0 + g + 1)
                        dve.tensor_tensor(hid[:, g, :], M[:, g, :], B1[layer][:, bass.ds(e[g], 1), :].rearrange("p a f -> p (a f)"),
                                          ALU.add).then_inc(hid_biased, 1)
                    if n_behind:
                        inputs_turned(grp + 1, n_behind)
                    if layer or not is_zero(t0):
                        dve.wait_ge(y_stored, 16 * (LSG[layer] + grp))
                    for g in range(n):
                        dve.wait_ge(y_ps, H[layer] + t0 + g + 1)
                        dve.tensor_tensor(ys[:, g, :], M[:, g, 0:D], B2[layer][:, bass.ds(e[g], 1), :].rearrange("p a f -> p (a f)"),
                                          ALU.add).then_inc(y_sb, 1)
                dve.wait_ge(routing_ready, layer + 1)
                inputs_turned(0, G)
                dve.wait_ge(w0_loaded, 16 * 4)
                if layer:
                    dve.wait_ge(w1b_loaded, 32)
                    dve.wait_ge(b2_loaded, 16)
                pipelined(dve, SLOT_TILES[layer], body)

            attention0()
            route(0)
            experts(0)
            dve.wait_ge(residual_loaded, 16)
            dve.wait_ge(choice_loaded, 16)
            attention1()
            route(1)

            def shared(t0, grp, n):
                for g in range(n):
                    dve.tensor_copy(xn[0:TT, g, :], tile(Z, t0 + g, TT)).then_inc(zg_ready, 1)
                for g in range(n):
                    dve.wait_ge(up_ps, HS + t0 + g + 1)
                    dve.tensor_tensor(hid[0:TT, g, 0:SHARED], M[0:TT, g, 0:SHARED], row["L1_ffn_sb1"][0:TT, :],
                                      ALU.add).then_inc(hid_biased, 1)
                for g in range(n):
                    dve.wait_ge(y_ps, HS + t0 + g + 1)
                    seq.mark(dve.tensor_tensor(Rb[0:TT, g, :], M[0:TT, g, 0:D], row["L1_ffn_sb2"][0:TT, :], ALU.add))
                seq.sync()
                for g in range(n):
                    dve.tensor_scalar(tile(S, t0 + g, TT), Rb[0:TT, g, :], 0.25, None, ALU.mult).then_inc(shared_ready, 1)
            groups(dve, TILES[1], shared, seq, G)
            experts(1)

            def mix_and_norm(t0, grp, n):
                dve.wait_ge(gathered, 32 * (TILES[1] + t0 + n))
                combine(1, t0, n, S, Rb)
                mean_rstd(n, TT, lambda g: Rb[0:TT, g, :], NORMS + 3 * A_GROUPS + grp + 1)
                scaled_norm(n, Rb, row["L1_ffn_ff_ln_g"], row["L1_ffn_ff_ln_b"])
                for g in range(n):
                    seq.mark(dve.tensor_tensor(tile(Z, t0 + g, TT), Rb[0:TT, g, :], tile(R, t0 + g, TT), ALU.add))
                seq.sync()
                for g in range(n):
                    seq.mark(dve.tensor_tensor(tile(Z, t0 + g, TT), tile(Z, t0 + g, TT), row["L1_ffn_ff_b2"][0:TT, :], ALU.add))

            def last(t0, grp, n, n_behind):
                for g in range(n):
                    dve.wait_ge(up_ps, HF + t0 + g + 1)
                    dve.tensor_tensor(fhid[0:TT, g, :], M[0:TT, g, :], row["L1_ffn_ff_b1"][0:TT, :],
                                      ALU.add).then_inc(hid_biased, 1)
                if n_behind:
                    mix_and_norm(t0 + G, grp + 1, n_behind)
                    seq.sync()
                for g in range(n):
                    dve.wait_ge(y_ps, HF + t0 + g + 1)
                    dve.tensor_tensor(tile(Z, t0 + g, TT), M[0:TT, g, 0:D], tile(Z, t0 + g, TT), ALU.add).then_inc(combined, 1)
            mix_and_norm(0, 0, G)
            pipelined(dve, TILES[1], last, seq, 6 * G + 1)


def _laid_out(name, v):
    import numpy as np
    if name == "x":
        v = v.reshape(IMAGES, CHANNELS, GRID, 2, PATCH // 2, GRID, PATCH)
        return v.transpose(4, 6, 2, 5, 1, 3, 0).reshape(P, PATCHES, PIX, IMAGES)
    if name == "L0_tok_W":
        return v.reshape(D, CHANNELS, 2, P).transpose(3, 1, 2, 0).reshape(P, PIX, D)
    if name == "L0_attn_w_qkv":
        return np.concatenate([v[:QHEADS * HDIM], v[D:]]).T
    if name in ("L0_attn_w_proj", "L1_attn_qkv_w", "L1_attn_proj_w", "L1_attn_ps_w1",
                "L1_attn_ps_w2", "L1_attn_ps_w3"):
        return v.T
    if name in ("L0_ffn_w1", "L1_ffn_ew1"):
        return v.transpose(1, 0, 2)
    if name in ("L0_ffn_w2", "L1_ffn_ew2"):
        return v.reshape(v.shape[0], FC, P, D).transpose(2, 0, 1, 3)
    if name == "L1_ffn_sw2" or name == "L1_ffn_ff_w2":
        return v.reshape(-1, P, D).transpose(1, 0, 2)
    return v


def kernel(**inputs):
    import numpy as _np
    import concourse.bacc as _bacc
    from concourse import mybir as _mybir
    from concourse.bass_utils import run_bass_kernel_spmd as _run

    nc = _bacc.Bacc("TRN2", target_bir_lowering=False, num_devices=1)
    arrays, args = {}, {}
    for name, value in inputs.items():
        v = _laid_out(name, _np.asarray(value))
        v = _np.ascontiguousarray(v)
        arrays[f"in_{name}_dram"] = v
        args[name] = nc.dram_tensor(f"in_{name}_dram", v.shape, _mybir.dt.from_np(v.dtype), kind="ExternalInput").ap()
    out = nc.dram_tensor("out_0_dram", (IMAGES, SEQ, D), _mybir.dt.float32, kind="ExternalOutput").ap()
    vit_tower(nc, args, out)
    r = _run(nc, [arrays], core_ids=[0])
    return r.results[0]["out_0_dram"]
```

```python
from contextlib import ExitStack

import concourse.bass as bass
from concourse import mybir

F32 = mybir.dt.float32
BF16 = mybir.dt.bfloat16
I32 = mybir.dt.int32
U32 = mybir.dt.uint32
ALU = mybir.AluOpType
ACT = mybir.ActivationFunctionType
AX = mybir.AxisListType

P = 128
D = 128
IMAGES = 128
CHANNELS, SIDE, PATCH = 3, 64, 16
GRID = SIDE // PATCH
PATCHES = GRID * GRID
SEQ = PATCHES + 1
TOKENS = IMAGES * SEQ
HEADS = 8
HDIM = D // HEADS
IPT = P // SEQ
TT = IPT * SEQ
ROWS = (P, TT)
TILES = (SEQ, -(-TOKENS // TT))
LAST = TOKENS - (TILES[1] - 1) * TT
PADDED = TILES[1] * TT
G = 4
A = 2
A_GROUPS = -(-TILES[1] // A)
A_LAST = TILES[1] - A * (A_GROUPS - 1)
GROUPS = tuple(-(-t // G) for t in TILES)
PIX = PATCH * PATCH * CHANNELS // P
PIXEL_LOADS = ((0, 1), (1, 3), (3, 6), (6, 11), (11, PATCHES))
FF = 512
FC = FF // P
SHARED = 256
SC = SHARED // P
WINDOW = 64
HALF = WINDOW // 2
KEEP = max(1, min(SEQ, int(SEQ * (1.0 - 0.3))))
DROP = SEQ - KEEP
EXPERTS = (8, 16)
TEMPERATURE = (1.0, 0.7)
PATTERN_TEMPERATURE = 0.3
PAIRS = 2 * TOKENS
SLOT_TILES = tuple((PAIRS + E * (P - 1)) // P for E in EXPERTS)
MAX_SLOT_TILES = max(SLOT_TILES)
SLOT_GROUPS = tuple(-(-t // G) for t in SLOT_TILES)
NEG = -1e30
EPS = 1e-5

MIXED_ROWS = [r for r in range(SEQ) if 8 * (r % 8) < SEQ]
QHEADS = max(r // 8 for r in MIXED_ROWS) + 1
QKV0 = QHEADS * HDIM + 2 * D


def heads_of(w):
    return sum(r % 8 == w // 8 for r in MIXED_ROWS)


def position_of_window_row(w):
    return (w + HALF) % SEQ


WINDOW_ROWS = sorted(range(SEQ), key=position_of_window_row)
DVE_ROWS = WINDOW_ROWS[2::3]
POOL_ROWS = [w for w in WINDOW_ROWS if w not in DVE_ROWS]


def runs(tiles):
    out = []
    for x in tiles:
        if out and out[-1][1] == x:
            out[-1] = (out[-1][0], x + 1)
        else:
            out.append((x, x + 1))
    return out


EMBEDDED = [(0, 5)] + [(k, k + 4) for k in range(5, SEQ, 4)]
MIXED_TILES = sorted(position_of_window_row(r) for r in MIXED_ROWS)
BIASED = runs([t for t in range(SEQ) if t not in MIXED_TILES])
MIXED = runs(MIXED_TILES)
ROUTED_ORDER = [t for lo, hi in BIASED + MIXED for t in range(lo, hi)]
NORMS = len(EMBEDDED) + len(BIASED) + len(MIXED)


def vit_tower(nc, a, out):
    with ExitStack() as ctx:
        def sb(name, shape, dt=F32):
            return ctx.enter_context(nc.sbuf_tensor(name, shape, dt))

        residual_dram = nc.dram_tensor("residual_tokens", [PADDED, D], F32).ap()
        choice_dram = nc.dram_tensor("choice_tokens", [PADDED, 4], F32).ap()
        xs_dram = nc.dram_tensor("expert_in", [MAX_SLOT_TILES * P, D], F32).ap()
        ys_dram = nc.dram_tensor("expert_out", [MAX_SLOT_TILES * P, D], F32).ap()

        region = sb("region", [P, 24576])
        scratch = sb("scratch", [P, 9520])
        W1 = [region[:, 0:4096].rearrange("p (e f) -> p e f", e=8),
              region[:, 16384:24576].rearrange("p (e f) -> p e f", e=16)]
        W2 = [region[:, 4096:8192].rearrange("p (e c d) -> p e c d", e=8, c=FC),
              region[:, 0:8192].rearrange("p (e c d) -> p e c d", e=16, c=FC)]
        B1 = [region[:, 8192:12288].rearrange("p (e f) -> p e f", e=8),
              region[:, 8192:16384].rearrange("p (e f) -> p e f", e=16)]
        B2 = [region[:, 12288:13312].rearrange("p (e d) -> p e d", e=8), scratch[:, 7472:9520].rearrange("p (e d) -> p e d", e=16)]
        pixels = region[:, 8192:8192 + PATCHES * PIX * IMAGES].rearrange("p (n c b) -> p n c b", n=PATCHES, c=PIX)
        prods = region[:, 16384:16384 + SEQ * QHEADS * D].rearrange("p (w x) -> p w x", w=SEQ)

        R = sb("residual", [P, TILES[1], D])
        Z = sb("normed", [P, TILES[1], D])
        Y0 = scratch[:, 0:TILES[1] * D].rearrange("p (t d) -> p t d", t=TILES[1])
        Y1 = scratch[:, TILES[1] * D:2 * TILES[1] * D].rearrange("p (t d) -> p t d", t=TILES[1])
        qkv0 = scratch[:, 0:SEQ * QKV0].rearrange("p (t x) -> p t x", t=SEQ)
        s0 = scratch[:, 5168:5576].rearrange("p (w h g) -> p w h g", w=SEQ, h=QHEADS)
        p0 = scratch[:, 5576:5984].rearrange("p (w h g) -> p w h g", w=SEQ, h=QHEADS)
        mixed = scratch[:, 5984:5984 + QHEADS * 3 * D].rearrange("p (h x) -> p h x", h=QHEADS)
        mixedT = scratch[:, 7136:7136 + len(MIXED_ROWS) * P].rearrange("p (r b) -> p r b", b=P)
        Kbd = scratch[:, 0:1904].rearrange("p (g h t) -> p g h t", g=A, h=HEADS)
        Pf = scratch[0:TT, 1904:3808].rearrange("p (g h t) -> p g h t", g=A, h=HEADS)
        PT = scratch[0:TT, 3808:5712].rearrange("p (g h t) -> p g h t", g=A, h=HEADS)
        NK = A * HEADS * SEQ
        drop_key, drop_ge, drop_eq, drop_cum = (
            scratch[0:TT, 5712 + k * NK:5712 + (k + 1) * NK].rearrange("p (r j) -> p r j", j=SEQ) for k in range(4))
        top8 = scratch[0:TT, 6800:6800 + 8 * A * HEADS].rearrange("p (r k) -> p r k", k=8)
        vs = scratch[0:TT, 6960:6960 + 4 * A * D].rearrange("p (g d) -> p g d", g=4 * A)
        drop_n = scratch[0:TT, 6928:6928 + A * HEADS]
        Y0_, Y1_ = (region[:, 8192 + k * TILES[1] * D:8192 + (k + 1) * TILES[1] * D].rearrange("p (t d) -> p t d", t=TILES[1])
                    for k in range(2))
        Y = [(Y0_, Y1_), (Y0, Y1)]

        def small(k, shape):
            n = 1
            for x in shape:
                n *= x
            v = scratch[:, 336 * k:336 * k + n]
            return v if len(shape) == 1 else v.rearrange("p (a b) -> p a b", b=shape[1])
        xs = scratch[:, 0:512].rearrange("p (g d) -> p g d", g=G)
        xsT = scratch[:, 512:1024].rearrange("p (g d) -> p g d", g=G)
        hid = scratch[:, 1024:3072].rearrange("p (g f) -> p g f", g=G)
        hidT = scratch[:, 3072:5120].rearrange("p (g f) -> p g f", g=G)
        ys = scratch[:, 5120:5632].rearrange("p (g d) -> p g d", g=G)
        heads = sb("heads", [P, 2452])
        qk = heads[:, 0:952].rearrange("p (g a t) -> p g a t", g=G, a=2)
        osb = heads[0:TT, 1464:1976].rearrange("p (g d) -> p g d", g=G)
        oT = heads[:, 1976:2452].rearrange("p (g t) -> p g t", g=G)
        tokT = heads[:, 0:PIX * D].rearrange("p (c d) -> p c d", c=PIX)
        S = heads[:, 0:TILES[1] * D].rearrange("p (t d) -> p t d", t=TILES[1])
        packed_heads = sb("packed_heads", [P, 2, G * HEADS * SEQ])
        Sc, Pc = (packed_heads[0:TT, k, :].rearrange("p (r j) -> p r j", j=SEQ) for k in range(2))
        zeros = packed_heads[:].rearrange("p k x -> p (k x)")[:, 0:7 * P]
        fhid = scratch[:, 4864:6912].rearrange("p (g f) -> p g f", g=G)
        fhidT = scratch[:, 6912:8960].rearrange("p (g f) -> p g f", g=G)

        qkvT = [sb("qkv_T0", [P, QKV0])[:], sb("qkv_T1", [P, 3 * D])[:]]
        projT = [sb("proj_T0", [P, D])[:], sb("proj_T1", [P, D])[:]]
        ps1T, ps2T, ps3T = sb("ps1_T", [P, D]), sb("ps2_T", [P, 64]), sb("ps3_T", [64, 3])
        router_w = [sb("router_w0", [P, 8]), sb("router_w1", [P, 16])]
        sw1, sw2 = sb("shared_w1", [P, SHARED]), sb("shared_w2", [P, SC, D])
        fw1, fw2 = sb("ff_w1", [P, FF]), sb("ff_w2", [P, FC, D])
        rows = sb("bias_rows", [P, 2096])
        at, row = 0, {}
        for name, n in (("L0_tok_b", D), ("cls_tok", D), ("L0_attn_b_proj", D), ("L0_ffn_router_b", 8),
                        ("L1_attn_proj_b", D), ("L1_ffn_router_b", 16), ("L1_ffn_ln_in_g", D),
                        ("L1_ffn_ln_in_b", D), ("L1_attn_ps_b3", 3), ("L1_attn_pattern_bias", 3),
                        ("L1_attn_sparse_w", HEADS), ("L1_attn_sparse_b", HEADS), ("L1_ffn_sb1", SHARED),
                        ("L1_ffn_sb2", D), ("L1_ffn_ff_ln_g", D), ("L1_ffn_ff_ln_b", D),
                        ("L1_ffn_ff_b1", FF), ("L1_ffn_ff_b2", D)):
            row[name] = rows[:, at:at + n]
            at += n
        proj_b = [row["L0_attn_b_proj"], row["L1_attn_proj_b"]]
        router_b = [row["L0_ffn_router_b"], row["L1_ffn_router_b"]]
        cols = sb("bias_columns", [P, 2])
        pattern_b = sb("pattern_b", [P, 3])
        minus_sparse = sb("minus_sparse", [P, 2, HEADS])

        ident = sb("identity", [P, P])
        own = sb("own_image", [TT, IPT])
        own_rows_f = sb("own_rows_f", [IPT, TT])
        own_rows = sb("own_rows", [IPT, TT], BF16)
        other = sb("other_image", [IPT, 4, TT], BF16)
        head_rows = sb("head_rows", [P, HEADS])
        before = sb("before", [P, P], BF16)
        ones_b = sb("ones_b", [P, P], BF16)
        ones_f = sb("ones_f", [P, 16 * (TILES[1] + 1)])
        carry = sb("carry", [TT, G * HEADS, SEQ])
        is_last = sb("is_last", [P, 1])
        own_mean = sb("own_mean", [TT, IPT])
        slot0 = sb("slot0", [P, G * SLOT_GROUPS[1]])
        slot0_i = sb("slot0_i", [P, G * SLOT_GROUPS[1]], I32)
        radix = sb("radix", [1, G])
        falling = sb("falling", [P, 16])
        falling_i = sb("falling_i", [P, 16], I32)
        mhalf = sb("mhalf", [P, 5])
        eps = sb("eps", [P, 5])
        carrier = sb("carrier", [1, 4])

        stats = sb("stats", [P, SEQ, 6])
        mv = sb("mean_var", [P, SEQ, 2])
        ve = sb("var_eps", [P, SEQ])
        rs = sb("rstd", [P, SEQ])
        xn = sb("xn", [P, G, D])
        xnT = sb("xnT", [P, G, D])
        Rb = sb("residual_bias", [P, G, D])
        mx = sb("row_max", [P, 52])
        sm = sb("row_sum", [P, 52])
        l3 = sb("pattern_logits", [TT, G, 3])
        e3 = sb("pattern_weights", [TT, G, 3])
        g1 = sb("gate_tmp", [TT, G])
        g2 = sb("gate", [TT, G])
        logits = sb("logits", [P, TILES[1], 16])
        choice = sb("choice", [P, TILES[1], 4])
        routed = sb("routed", [P, TILES[1], 16], BF16)
        count_i = sb("count_i", [P, 2, 16], I32)
        expert_of = sb("expert_of", [1, SLOT_GROUPS[1]], I32)

        M = ctx.enter_context(nc.psum_tensor("M", [P, 4, 512], F32))
        PS = ctx.enter_context(nc.psum_tensor("PS", [P, 2, 1024], F32))

        def sem(name):
            return ctx.enter_context(nc.semaphore(name))

        consts, pool_step, dve_step, tok_w_loaded, tok_rows_loaded = (
            sem(n) for n in ("consts", "pool_step", "dve_step", "tok_w_loaded", "tok_rows_loaded"))
        rows_loaded, l0_loaded, l1_loaded, zero_stored = (
            sem(n) for n in ("rows_loaded", "l0_loaded", "l1_loaded", "zero_stored"))
        emb_ps, emb_sb, cls_set = (
            sem(n) for n in ("emb_ps", "emb_sb", "cls_set"))
        mean_var_ready, rstd_ready, xn_ready, xnT_ps, xnT_sb = (
            sem(n) for n in ("mean_var_ready", "rstd_ready", "xn_ready", "xnT_ps", "xnT_sb"))
        qkv_ps, qkv0_sb, qk_sb, v_sb, kbd = (
            sem(n) for n in ("qkv_ps", "qkv0_sb", "qk_sb", "v_sb", "kbd"))
        rb_ready, scores_ps, packed, shifted = (
            sem(n) for n in ("rb_ready", "scores_ps", "packed", "shifted"))
        exp_done, probs, spread, pT_ps, pT_sb = (
            sem(n) for n in ("exp_done", "probs", "spread", "pT_ps", "pT_sb"))
        o_ps, o_sb, oT_ps, oT_sb, proj_ps = (
            sem(n) for n in ("o_ps", "o_sb", "oT_ps", "oT_sb", "proj_ps"))
        z_ready, zg_ready, zT_ps, zT_sb, logit_ps = (
            sem(n) for n in ("z_ready", "zg_ready", "zT_ps", "zT_sb", "logit_ps"))
        logits_ready = sem("logits_ready")
        products, s0_shifted, p0_exp, p0_ready, weighted = (
            sem(n) for n in ("products", "s0_shifted", "p0_exp", "p0_ready", "weighted"))
        mixed_ready, mixedT_ps, mixedT_sb, proj0_ps, attn0_done = (
            sem(n) for n in ("mixed_ready", "mixedT_ps", "mixedT_sb", "proj0_ps", "attn0_done"))
        rb0_ready, pl_sb, h1_ps, h1_sb, h2_ps = (
            sem(n) for n in ("rb0_ready", "pl_sb", "h1_ps", "h1_sb", "h2_ps"))
        h2_sb, l3_ps, l3_shifted, e3_done = (
            sem(n) for n in ("h2_sb", "l3_ps", "l3_shifted", "e3_done"))
        route_shifted, route_exp, routed_ready, rank_ps, routing_ready = (
            sem(n) for n in ("route_shifted", "route_exp", "routed_ready", "rank_ps", "routing_ready"))
        choice_stored, choice_loaded = (
            sem(n) for n in ("choice_stored", "choice_loaded"))
        residual_stored, residual_loaded, scattered, w0_loaded, w1a_loaded = (
            sem(n) for n in ("residual_stored", "residual_loaded", "scattered", "w0_loaded", "w1a_loaded"))
        w1b_loaded, b2_loaded = (
            sem(n) for n in ("w1b_loaded", "b2_loaded"))
        xs_in, xsT_ps, xsT_sb, up_ps, hid_biased = (
            sem(n) for n in ("xs_in", "xsT_ps", "xsT_sb", "up_ps", "hid_biased"))
        hid_ready, hT_ps, hT_sb, y_ps, y_sb = (
            sem(n) for n in ("hid_ready", "hT_ps", "hT_sb", "y_ps", "y_sb"))
        l0_rows_loaded = sem("l0_rows_loaded")
        slots_ready, weights_ready = sem("slots_ready"), sem("weights_ready")
        experts_added = sem("experts_added")
        fT_ps, fT_sb = sem("fT_ps"), sem("fT_sb")
        y_stored, gathered, combined, shared_ready = (
            sem(n) for n in ("y_stored", "gathered", "combined", "shared_ready"))
        out_stored = sem("out_stored")
        pixels_in = [ctx.enter_context(nc.semaphore(f"pixels_in{g}")) for g in range(len(PIXEL_LOADS))]

        block = ctx.enter_context(nc.Block())

        class Seq:
            def __init__(self, eng, sem):
                self.eng, self.sem, self.at, self.n = eng, sem, 0, 0

            def mark(self, ins):
                ins.then_inc(self.sem, 1)
                self.at = self.at + 1
                self.n += 1

            def sync(self):
                self.eng.wait_ge(self.sem, self.at)

            def step(self, ins):
                self.mark(ins)
                self.sync()

        def groups(eng, tiles, body, seq=None, steps=0, peel=False):
            whole, rest = divmod(tiles, G)
            start, n = (seq.at, seq.n) if seq else (0, 0)
            if peel:
                body(0, 0, G)
                n = seq.n if seq else 0
            with eng.Fori(1 if peel else 0, whole) as i:
                if seq:
                    seq.at = start + i * steps
                body(i * G, i, G)
            if seq:
                assert seq.n - n == steps, (seq.n - n, steps)
                seq.at = start + whole * steps
            if rest:
                body(whole * G, whole, rest)

        def pipelined(eng, tiles, body, seq=None, steps=0):
            whole, rest = divmod(tiles, G)
            body(0, 0, G, G)
            start, n = (seq.at, seq.n) if seq else (0, 0)
            with eng.Fori(1, whole - 1) as i:
                if seq:
                    seq.at = start + (i - 1) * steps
                body(i * G, i, G, G)
            if seq:
                assert seq.n - n == steps, (seq.n - n, steps)
                seq.at = start + (whole - 2) * steps
            body((whole - 1) * G, whole - 1, G, rest)
            if rest:
                body(whole * G, whole, rest, 0)

        def experts_of_group(eng, layer, grp, n):
            packed_ = eng.value_load(expert_of[0:1, bass.ds(grp, 1)], min_val=0, max_val=16 ** G - 1)
            return [(packed_ >> (4 * g)) & (EXPERTS[layer] - 1) for g in range(n)]

        def overlapped(eng, step, seq=None, steps=0):
            last = A_GROUPS - 1

            def tiles_of(i):
                return (i, A if i < last else A_LAST) if 0 <= i <= last else (None, 0)

            def static(i):
                step(*tiles_of(i), *tiles_of(i - 1), *tiles_of(i - 2), *tiles_of(i - 3), *tiles_of(i + 1))
            for i in range(-1, 3):
                static(i)
            start, n = (seq.at, seq.n) if seq else (0, 0)
            with eng.Fori(3, last - 1) as i:
                if seq:
                    seq.at = start + (i - 3) * steps
                step(i, A, i - 1, A, i - 2, A, i - 3, A, i + 1, A)
            if seq:
                assert seq.n - n == steps, (seq.n - n, steps)
                seq.at = start + (last - 4) * steps
            for i in range(last - 1, last + 4):
                static(i)

        def tiles_before(*groups_):
            return [None if x is None else A * x for x in groups_]

        def prods_of(w, last_two):
            nh = heads_of(w)
            n = HEADS * HDIM
            v = prods[:, w, 0:nh * n]
            return v.rearrange("p (h x y) -> p h x y", h=nh, y=last_two)

        def query_key(eng, w):
            t, nh = position_of_window_row(w), heads_of(w)
            q = qkv0[:, t, 0:nh * HDIM].rearrange("p (h d) -> p h d", h=nh)
            k = qkv0[:, t, QHEADS * HDIM:QHEADS * HDIM + D].rearrange("p (g d) -> p g d", g=HEADS)
            return eng.tensor_tensor(prods_of(w, HDIM), q.unsqueeze(2).broadcast_to([P, nh, HEADS, HDIM]),
                                     k.unsqueeze(1).broadcast_to([P, nh, HEADS, HDIM]), ALU.mult)

        def prob_value(eng, w):
            t, nh = position_of_window_row(w), heads_of(w)
            v = qkv0[:, t, QHEADS * HDIM + D:QKV0].rearrange("p (g d) -> p d g", g=HEADS)
            return eng.tensor_tensor(prods_of(w, HEADS), p0[:, w, 0:nh].unsqueeze(2).broadcast_to([P, nh, HDIM, HEADS]),
                                     v.unsqueeze(1).broadcast_to([P, nh, HDIM, HEADS]), ALU.mult)

        def norm_in_at(a):
            return NORMS + (a + 1 if isinstance(a, int) and a < 3 else 3 * a - 5)

        def norm_out_at(b, k):
            late = max(0, b - (A_GROUPS - 4)) if isinstance(b, int) else 0
            return NORMS + 3 * b + 5 + k - late

        hT_bank = [PS[:, b // 2, 512 * (b % 2):512 * (b % 2) + 512] for b in (0, 1, 2, 0)]
        xsT_bank = PS[:, 1, 512:1024].rearrange("p (g d) -> p g d", g=G)

        def is_zero(t0):
            return isinstance(t0, int) and t0 == 0

        def tile(T, t, rows):
            return T[0:rows, bass.ds(t, 1), :].rearrange("p a d -> p (a d)")

        LT = (0, TILES[0])
        LG = (0, GROUPS[0])
        LS = (0, SLOT_TILES[0])
        LSG = (0, SLOT_GROUPS[0])
        H = (0, SLOT_TILES[0] + TILES[1])
        HS, HF = SLOT_TILES[0], SLOT_TILES[0] + TILES[1] + SLOT_TILES[1]

        @block.sync
        def _(sp):
            def load(dst, name, sem):
                sp.dma_start(dst, a[name]).then_inc(sem, 16)

            def load_rows(*names, sem=rows_loaded):
                for name in names:
                    v = a[name] if len(a[name].shape) == 1 else a[name].rearrange("a b d -> (a b d)")
                    sp.dma_start(row[name], v.partition_broadcast(P)).then_inc(sem, 16)

            load(tokT, "L0_tok_W", tok_w_loaded)
            for g, (lo, hi) in enumerate(PIXEL_LOADS):
                sp.dma_start(pixels[:, lo:hi], a["x"][:, lo:hi]).then_inc(pixels_in[g], 16)
                if g == 0:
                    load_rows("L0_tok_b", "cls_tok", sem=tok_rows_loaded)
            load_rows("L0_attn_b_proj", "L0_ffn_router_b", sem=l0_rows_loaded)
            load(qkvT[0], "L0_attn_w_qkv", l0_loaded)
            load(projT[0], "L0_attn_w_proj", l0_loaded)
            load(router_w[0][:], "L0_ffn_router_w", l0_loaded)
            load(W1[0], "L0_ffn_w1", w0_loaded)
            load(W2[0], "L0_ffn_w2", w0_loaded)
            sp.wait_ge(consts, 1)
            zrows = xs_dram.rearrange("(k p) d -> p k d", p=P)
            for k in range(0, MAX_SLOT_TILES, 7):
                sp.dma_start(zrows[:, k:k + 7, :], zeros.rearrange("p (k d) -> p k d", k=7)).then_inc(zero_stored, 16)
            sp.dma_start(residual_dram[TOKENS:PADDED, :], zeros[0:PADDED - TOKENS, 0:D]).then_inc(zero_stored, 16)
            sp.dma_start(choice_dram[TOKENS:PADDED, :], zeros[0:PADDED - TOKENS, 0:4]).then_inc(zero_stored, 16)
            load(qkvT[1], "L1_attn_qkv_w", l1_loaded)
            load(projT[1], "L1_attn_proj_w", l1_loaded)
            load(ps1T[:], "L1_attn_ps_w1", l1_loaded)
            load(ps2T[:], "L1_attn_ps_w2", l1_loaded)
            load(ps3T[:], "L1_attn_ps_w3", l1_loaded)
            load(router_w[1][:], "L1_ffn_router_w", l1_loaded)
            load(sw1[:], "L1_ffn_sw1", l1_loaded)
            load(sw2[:], "L1_ffn_sw2", l1_loaded)
            load(fw1[:], "L1_ffn_ff_w1", l1_loaded)
            load(fw2[:], "L1_ffn_ff_w2", l1_loaded)
            sp.dma_start(cols[:, 0:1], a["L1_attn_ps_b1"].unsqueeze(1)).then_inc(l1_loaded, 16)
            sp.dma_start(cols[0:64, 1:2], a["L1_attn_ps_b2"].unsqueeze(1)).then_inc(l1_loaded, 16)
            load_rows("L1_attn_proj_b", "L1_ffn_router_b", "L1_ffn_ln_in_g", "L1_ffn_ln_in_b", "L1_attn_ps_b3",
                      "L1_attn_pattern_bias", "L1_attn_sparse_w", "L1_attn_sparse_b", "L1_ffn_sb1", "L1_ffn_sb2",
                      "L1_ffn_ff_ln_g", "L1_ffn_ff_ln_b", "L1_ffn_ff_b1", "L1_ffn_ff_b2")
            sp.wait_ge(emb_ps, PATCHES)
            sp.dma_start(B1[0], a["L0_ffn_b1"].partition_broadcast(P)).then_inc(w0_loaded, 16)
            sp.dma_start(B2[0], a["L0_ffn_b2"].partition_broadcast(P)).then_inc(w0_loaded, 16)

            def experts(layer):
                tiles_of = lambda d, t0, n: d.rearrange("(k p) d -> p k d", p=P)[:, bass.ds(t0, n), :]

                def take(grp, n):
                    if layer or not is_zero(grp):
                        sp.wait_ge(xsT_ps, LSG[layer] + grp)
                    sp.dma_start(xs[:, 0:n, :], tiles_of(xs_dram, grp * G, n)).then_inc(xs_in, 16)

                def put(grp, n):
                    sp.wait_ge(y_sb, LS[layer] + grp * G + n)
                    sp.dma_start(tiles_of(ys_dram, grp * G, n), ys[:, 0:n, :]).then_inc(y_stored, 16)
                sp.wait_ge(scattered, 32 * (LT[layer] + TILES[layer]))
                sp.wait_ge(weights_ready, layer + 1)
                whole, rest = divmod(SLOT_TILES[layer], G)
                take(0, G)
                take(1, G)
                with sp.Fori(2, whole) as i:
                    take(i, G)
                    put(i - 2, G)
                if rest:
                    take(whole, rest)
                put(whole - 2, G)
                put(whole - 1, G)
                if rest:
                    put(whole, rest)

            sp.wait_ge(attn0_done, 1)
            sp.dma_start(residual_dram[0:TOKENS, :].rearrange("(b j) d -> b j d", j=SEQ), R[:, 0:SEQ, :])\
              .then_inc(residual_stored, 16)
            sp.dma_start(W1[1], a["L1_ffn_ew1"]).then_inc(w1a_loaded, 16)
            sp.wait_ge(weights_ready, 1)
            sp.dma_start(choice_dram[0:TOKENS, :].rearrange("(b j) c -> b (j c)", j=SEQ),
                         choice[:, 0:SEQ, :].rearrange("p t c -> p (t c)")).then_inc(choice_stored, 16)
            sp.wait_ge(residual_stored, 16)
            sp.wait_ge(zero_stored, 16 * (MAX_SLOT_TILES // 7 + 2))
            sp.wait_ge(logits_ready, 1)
            sp.dma_start(R[0:TT, :, :], residual_dram.rearrange("(t p) d -> p t d", p=TT)).then_inc(residual_loaded, 16)
            experts(0)
            sp.wait_ge(choice_stored, 16)
            sp.dma_start(choice[0:TT, :, :], choice_dram.rearrange("(t p) c -> p t c", p=TT)).then_inc(choice_loaded, 16)
            sp.wait_ge(experts_added, A_GROUPS)
            sp.dma_start(W2[1], a["L1_ffn_ew2"]).then_inc(w1b_loaded, 16)
            sp.dma_start(B1[1], a["L1_ffn_eb1"].partition_broadcast(P)).then_inc(w1b_loaded, 16)
            sp.wait_ge(logits_ready, 1 + TILES[1])
            sp.dma_start(B2[1], a["L1_ffn_eb2"].partition_broadcast(P)).then_inc(b2_loaded, 16)
            experts(1)

            o = out.rearrange("b j d -> (b j) d")
            early = G * (GROUPS[1] - 1)
            for lo, hi in ((0, early // 2), (early // 2, early), (early, TILES[1] - 1)):
                sp.wait_ge(combined, hi)
                sp.dma_start(o[lo * TT:hi * TT, :].rearrange("(t p) d -> p t d", p=TT),
                             Z[0:TT, lo:hi, :]).then_inc(out_stored, 16)
            sp.wait_ge(combined, TILES[1])
            sp.dma_start(o[(TILES[1] - 1) * TT:TOKENS, :], Z[0:LAST, TILES[1] - 1, :]).then_inc(out_stored, 16)
            sp.wait_ge(out_stored, 4 * 16)

        @block.gpsimd
        def _(pool):
            seq = Seq(pool, pool_step)
            pool.memset(zeros, 0.0).then_inc(consts, 1)
            seq.mark(pool.memset(ident[:], 0.0))
            seq.mark(pool.memset(own[:], 1.0))
            seq.mark(pool.memset(own_rows_f[:], 1.0))
            seq.mark(pool.memset(head_rows[:], float(HDIM) ** -0.5))
            seq.mark(pool.memset(before[:], 1.0))
            seq.mark(pool.memset(is_last[:], 1.0))
            seq.mark(pool.memset(ones_b[:], 1.0))
            seq.mark(pool.memset(ones_f[:], 1.0))
            seq.mark(pool.memset(mhalf[:], -0.5))
            seq.mark(pool.memset(eps[:], EPS))
            seq.mark(pool.memset(carrier[:], 0.0))
            seq.mark(pool.memset(carry[:], 1.0))
            seq.mark(pool.memset(mixed, 0.0))
            seq.mark(pool.memset(s0, 0.0))
            seq.mark(pool.iota(slot0_i[:], pattern=[[P, G * SLOT_GROUPS[1]]], base=0, channel_multiplier=0))
            for g in range(G):
                seq.mark(pool.memset(radix[:, g:g + 1], 16.0 ** g))
            seq.mark(pool.iota(falling_i[:], pattern=[[-1, 16]], base=16, channel_multiplier=0))
            seq.sync()

            def keep(t, pattern, base, mult, op=ALU.is_ge, fill=0.0):
                seq.mark(pool.affine_select(out=t, in_=t, compare_op=op, fill=fill, base=base,
                                            pattern=pattern, channel_multiplier=mult))
            keep(ident[:], [[-1, P]], 0, 1, ALU.not_equal, 1.0)
            keep(own[:], [[-SEQ, IPT]], 0, 1)
            keep(own_rows_f[:], [[1, TT]], 0, -SEQ)
            keep(head_rows[:], [[-HDIM, HEADS]], 0, 1)
            keep(before[:], [[1, P]], -1, -1)
            keep(is_last[:], [[0, 1]], LAST - 1, -1)
            seq.mark(pool.memset(carry[:, :, 0:1], 0.0))
            seq.mark(pool.tensor_copy(slot0[:], slot0_i[:]))
            seq.mark(pool.tensor_copy(falling[:], falling_i[:]))
            seq.sync()
            keep(own[:], [[SEQ, IPT]], SEQ - 1, -1)
            keep(own_rows_f[:], [[-1, TT]], SEQ - 1, SEQ)
            keep(head_rows[:], [[HDIM, HEADS]], HDIM - 1, -1)
            seq.sync()
            seq.mark(pool.tensor_copy(own_rows[:], own_rows_f[:]))
            seq.mark(pool.tensor_scalar(own_mean[:], own[:], 1.0 / SEQ, None, ALU.mult))
            for h in range(4):
                seq.mark(pool.tensor_scalar(other[:, h, :], own_rows_f[:], -1.0, -NEG, ALU.add, ALU.mult))
            seq.sync()
            pool.memset(carrier[:], 0.0).then_inc(consts, 1)

            def norm_rstd(n, rws, at, slot=0):
                pool.wait_ge(mean_var_ready, at)
                v = ve[0:rws, slot:slot + n]
                seq.step(pool.tensor_tensor(v, mv[0:rws, slot:slot + n, 1], eps[0:rws, 0:n], ALU.add))
                pool.tensor_tensor(rs[0:rws, slot:slot + n], v, mhalf[0:rws, 0:n], ALU.pow).then_inc(rstd_ready, 1)

            def attention0():
                for k, (lo, hi) in enumerate(EMBEDDED):
                    norm_rstd(hi - lo, P, k + 1, slot=lo)
                for w in POOL_ROWS:
                    pool.wait_ge(qkv0_sb, position_of_window_row(w) + 1)
                    query_key(pool, w).then_inc(products, 1)
                pool.wait_ge(xn_ready, TILES[0])
                pool.wait_ge(l0_rows_loaded, 32)
                pool.tensor_tensor(R[:, 0:SEQ, :], R[:, 0:SEQ, :],
                                   proj_b[0].unsqueeze(1).broadcast_to([P, SEQ, D]), ALU.add).then_inc(rb0_ready, 1)
                pool.wait_ge(p0_ready, 1)
                for w in POOL_ROWS:
                    prob_value(pool, w).then_inc(weighted, 1)
                for k, (lo, hi) in enumerate(BIASED + MIXED):
                    norm_rstd(hi - lo, P, len(EMBEDDED) + k + 1, slot=lo)

            def attention1():
                pool.wait_ge(l1_loaded, 16 * 12)
                pool.wait_ge(rows_loaded, 16 * 14)

                def spread_probs(t0, g):
                    pool.wait_ge(probs, t0 + g + 1)
                    pool.tensor_tensor(
                        Pf[:, g].rearrange("p h (i j) -> p h i j", i=IPT),
                        Pc[:, g * HEADS:(g + 1) * HEADS, :].unsqueeze(2).broadcast_to([TT, HEADS, IPT, SEQ]),
                        own[:].unsqueeze(1).unsqueeze(3).broadcast_to([TT, HEADS, IPT, SEQ]),
                        ALU.mult).then_inc(spread, 1)

                for f in range(-1, A_GROUPS + 2):
                    m, b, ahead = f - 1, f - 2, f + 1
                    nm, nb, na = (min(A, TILES[1] - A * x) if 0 <= x < A_GROUPS else 0 for x in (m, b, ahead))
                    if nm:
                        if nb:
                            pool.wait_ge(pT_ps, A * b + nb)
                        spread_probs(A * m, 0)
                    if na:
                        norm_rstd(na, TT, norm_in_at(ahead))
                    for g in range(1, nm):
                        spread_probs(A * m, g)
                    if na:
                        a0 = A * ahead
                        pool.wait_ge(xn_ready, LT[1] + a0 + na)
                        for g in range(na):
                            ins = pool.tensor_tensor(R[0:TT, a0 + g, :], R[0:TT, a0 + g, :], proj_b[1][0:TT, :], ALU.add)
                        ins.then_inc(rb_ready, 1)
                    if f == 0:
                        gather(0, 2 * A, A)
                    if nb:
                        norm_rstd(nb, TT, norm_out_at(b, 0), slot=A)
                        norm_rstd(nb, TT, norm_out_at(b, 1), slot=A)
                    if na:
                        for g in range(na):
                            pool.wait_ge(qk_sb, a0 + g + 1)
                            pool.tensor_tensor(Kbd[:, g], qk[:, g, 1:2, :].broadcast_to([P, HEADS, TT]),
                                               head_rows[:].unsqueeze(2).broadcast_to([P, HEADS, TT]),
                                               ALU.mult).then_inc(kbd, 1)
                        if f >= 0 and ahead + 2 < A_GROUPS:
                            gather(0, A * (ahead + 2), min(A, TILES[1] - A * (ahead + 2)))

            def rows_of(layer, t):
                return ROWS[layer] if layer == 0 or t < TILES[1] - 1 else LAST

            def scatter(layer):
                pool.wait_ge(slots_ready, layer + 1)
                pool.wait_ge(zero_stored, 16 * (MAX_SLOT_TILES // 7 + 2))
                for t in range(TILES[layer]):
                    n = rows_of(layer, t)
                    for k in range(2):
                        pool.indirect_dma_start(
                            out=xs_dram, out_offset=bass.IndirectOffsetOnAxis(ap=choice[0:n, t, k:k + 1].bitcast(U32), axis=0),
                            in_=Z[0:n, t, :], in_offset=None).then_inc(scattered, 16)

            def gather(layer, first, tiles):
                if first == 0:
                    pool.wait_ge(y_stored, 16 * (LSG[layer] + SLOT_GROUPS[layer]))
                    if layer == 0:
                        pool.wait_ge(choice_loaded, 16)
                else:
                    pool.wait_ge(gathered, 32 * (layer * TILES[1] + first))
                for t in range(first, first + tiles):
                    n = TT if layer == 0 else rows_of(1, t)
                    for k in range(2):
                        pool.indirect_dma_start(
                            out=Y[layer][k][0:n, t, :], out_offset=None, in_=ys_dram[0:SLOT_TILES[layer] * P, :],
                            in_offset=bass.IndirectOffsetOnAxis(ap=choice[0:n, t, k:k + 1].bitcast(U32), axis=0))\
                            .then_inc(gathered, 16)

            attention0()
            scatter(0)
            gather(0, 0, A)
            gather(0, A, A)
            attention1()
            scatter(1)
            gather(1, 0, G)
            for grp in range(GROUPS[1]):
                norm_rstd(min(G, TILES[1] - G * grp), TT, NORMS + 3 * A_GROUPS + grp + 1)
                if grp + 1 < GROUPS[1]:
                    gather(1, G * (grp + 1), min(G, TILES[1] - G * (grp + 1)))

        @block.tensor
        def _(pe):
            pe.wait_ge(tok_w_loaded, 16)
            for n in range(PATCHES):
                for g, (lo, hi) in enumerate(PIXEL_LOADS):
                    if n == lo:
                        pe.wait_ge(pixels_in[g], 16)
                if n >= 4:
                    pe.wait_ge(emb_sb, n - 3)
                for c in range(PIX):
                    ins = pe.matmul(M[:, n % 4, 0:D], pixels[:, n, c, :], tokT[:, c, :],
                                    start=(c == 0), stop=(c == PIX - 1))
                ins.then_inc(emb_ps, 1)
            pe.wait_ge(consts, 2)

            def turn(src, n, rws, ready, base, done, slot=0):
                for g in range(slot, slot + n):
                    pe.wait_ge(ready, base + g - slot + 1)
                    pe.transpose(M[:, g, 0:rws], src[0:rws, g, :], ident[0:rws, 0:rws]).then_inc(done, 1)

            def route_products(layer, n, base, slot=0):
                E, rws = EXPERTS[layer], ROWS[layer]
                turn(xn, n, rws, zg_ready, base, zT_ps, slot)
                for g in range(slot, slot + n):
                    pe.wait_ge(zT_sb, base + g - slot + 1)
                    pe.matmul(M[0:rws, g, 0:E], xnT[:, g, 0:rws], router_w[layer][:], start=True, stop=True)\
                        .then_inc(logit_ps, 1)

            def normed_products(order, ready, turned_ps, turned_sb, product):
                def turn_tile(k):
                    pe.wait_ge(ready, k + 1)
                    pe.transpose(PS[:, 1, 512 * (k % 2):512 * (k % 2) + P], Z[:, order[k], :], ident[:]).then_inc(turned_ps, 1)
                turn_tile(0)
                for k in range(len(order)):
                    if k + 1 < len(order):
                        turn_tile(k + 1)
                    pe.wait_ge(turned_sb, k + 1)
                    product(k, order[k])

            def attention0():
                pe.wait_ge(emb_sb, PATCHES)
                pe.wait_ge(l0_loaded, 16 * 3)

                def qkv(k, tile_):
                    if k >= 4:
                        pe.wait_ge(qkv0_sb, k - 3)
                    pe.matmul(M[:, k % 4, 0:QKV0], xnT[:, k % 4, :], qkvT[0], start=True, stop=True).then_inc(qkv_ps, 1)
                normed_products(list(range(SEQ)), xn_ready, xnT_ps, xnT_sb, qkv)
                pe.wait_ge(mixed_ready, 1)
                for k, r in enumerate(MIXED_ROWS):
                    ins = pe.transpose(PS[:, k // 4, P * (k % 4):P * (k % 4 + 1)],
                                       mixed[:, r // 8, P * (r % 8):P * (r % 8 + 1)], ident[:])
                    if k % 4 == 3 or r == MIXED_ROWS[-1]:
                        ins.then_inc(mixedT_ps, 1)
                for k, r in enumerate(MIXED_ROWS):
                    if k % 4 == 0:
                        pe.wait_ge(mixedT_sb, k // 4 + 1)
                    ins = pe.matmul(M[:, k // 4, P * (k % 4):P * (k % 4 + 1)], mixedT[:, k, :], projT[0],
                                    start=True, stop=True)
                ins.then_inc(proj0_ps, 1)

                def route_product(k, tile_):
                    pe.matmul(PS[:, 0, 8 * tile_:8 * tile_ + 8], xnT[:, k % 4, :], router_w[0][:], start=True, stop=True)\
                        .then_inc(logit_ps, 1)
                normed_products(ROUTED_ORDER, zg_ready, zT_ps, zT_sb, route_product)

            def attention1():
                L = LT[1]
                wq, wk, wv = (qkvT[1][:, k * D:(k + 1) * D] for k in range(3))
                pe.wait_ge(l1_loaded, 16 * 12)

                def projections(t0, n):
                    turn(xn, n, TT, xn_ready, L + t0, xnT_ps)
                    for g in range(n):
                        pe.wait_ge(xnT_sb, L + t0 + g + 1)
                        pe.matmul(M[:, g, 0:TT], wq, xnT[:, g, 0:TT], start=True, stop=True)
                        pe.matmul(M[:, g, 120:120 + TT], wk, xnT[:, g, 0:TT], start=True, stop=True)
                        pe.matmul(M[0:TT, g, 256:384], xnT[:, g, 0:TT], wv, start=True, stop=True)
                        pe.matmul(M[:, g, 384:384 + IPT], xn[0:TT, g, :], own_mean[:], start=True, stop=True)\
                            .then_inc(qkv_ps, 1)

                def scores(t0, g):
                    pe.wait_ge(kbd, t0 + g + 1)
                    if g or not is_zero(t0):
                        pe.wait_ge(packed, t0 + g)
                    for b in range(2):
                        bank = PS[0:TT, 0, 512 * b:512 * b + 4 * TT]
                        pe.matmul(bank, own_rows[:], other[:].rearrange("p h t -> p (h t)"), start=True, stop=False)
                        ins = pe.matmul(bank, qk[:, g, 0, :], Kbd[:, g, 4 * b:4 * b + 4, :].rearrange("p h t -> p (h t)"),
                                        start=False, stop=True)
                    ins.then_inc(scores_ps, 1)

                def pattern(f, t0, n, layer):
                    if layer == 1:
                        pe.wait_ge(pl_sb, t0 + n)
                        pe.matmul(M[:, 0, 0:n * IPT], ps1T[:], oT[:, 0:n, 0:IPT], start=True, stop=True).then_inc(h1_ps, 1)
                    if layer == 2:
                        pe.wait_ge(h1_sb, f + 1)
                        pe.matmul(M[0:64, 0, 0:n * IPT], ps2T[:], xnT[:, 0, 0:n * IPT], start=True, stop=True)\
                            .then_inc(h2_ps, 1)
                    if layer == 3:
                        pe.wait_ge(h2_sb, f + 1)
                        for g in range(n):
                            pe.matmul(M[0:TT, g, 0:3], oT[0:64, g, :], ps3T[:], start=True, stop=True).then_inc(l3_ps, 1)

                def turn_probs(t0, g):
                    pe.wait_ge(spread, t0 + g + 1)
                    for h in range(HEADS):
                        o = 512 * (h // 4) + TT * (h % 4)
                        ins = pe.transpose(PS[0:TT, 1, o:o + TT], Pf[:, g, h, :], ident[0:TT, 0:TT])
                    ins.then_inc(pT_ps, 1)

                def probs_values(t0, grp, g):
                    pe.wait_ge(pT_sb, t0 + g + 1)
                    pe.wait_ge(v_sb, t0 + g + 1)
                    if g == 0:
                        pe.wait_ge(logits_ready, 1 + t0)
                    v = vs[:, bass.ds((grp & 3) * A + g, 1), :].rearrange("p a d -> p (a d)")
                    for h in range(HEADS):
                        ins = pe.matmul(M[0:TT, A + g, h * HDIM:(h + 1) * HDIM], PT[:, g, h, :],
                                        v[:, h * HDIM:(h + 1) * HDIM], start=True, stop=True)
                    ins.then_inc(o_ps, 1)

                def step(f, nf, m, nm, b, nb, c, nc, ahead, na):
                    f0, b0, c0, a0 = tiles_before(f, b, c, ahead)
                    if nb:
                        turn_probs(b0, 0)
                    if nc:
                        route_products(1, nc, L + c0, slot=A)
                    if nf:
                        pattern(f, f0, nf, 1)
                    if nf:
                        pattern(f, f0, nf, 2)
                    if nf:
                        scores(f0, 0)
                    if nb:
                        probs_values(b0, b, 0)
                    if nb > 1:
                        turn_probs(b0, 1)
                    if nf:
                        pattern(f, f0, nf, 3)
                    if nb > 1:
                        probs_values(b0, b, 1)
                    if nb:
                        turn(osb, nb, TT, o_sb, b0, oT_ps, slot=A)
                        for g in range(nb):
                            pe.wait_ge(oT_sb, b0 + g + 1)
                            pe.matmul(M[0:TT, A + g, 0:D], oT[:, A + g, :], projT[1], start=True, stop=True)\
                                .then_inc(proj_ps, 1)
                    if nf > 1:
                        scores(f0, 1)
                    if na:
                        projections(a0, na)
                overlapped(pe, step)

            def rank(layer):
                rws, n = ROWS[layer], TILES[layer] * EXPERTS[layer]
                pe.wait_ge(routed_ready, layer + 1)
                chosen = routed[0:rws, 0:TILES[layer], 0:EXPERTS[layer]]
                pe.matmul(PS[0:rws, 0, 0:n], before[0:rws, 0:rws], chosen, start=True, stop=True)
                pe.matmul(PS[0:rws, 1, 0:n], ones_b[0:rws, 0:rws], chosen, start=True, stop=True).then_inc(rank_ps, 1)

            def hidden_down(n, at, hidT_, chunks, rhs, y_sem, ready, hid_, rws):
                def turn_hidden(g):
                    pe.wait_ge(ready, at(g))
                    for c in range(chunks):
                        ins = pe.transpose(hT_bank[g][:, P * c:P * c + rws],
                                           hid_[0:rws, g, P * c:P * (c + 1)], ident[0:rws, 0:rws])
                    ins.then_inc(hT_ps, 1)

                def down(g):
                    pe.wait_ge(hT_sb, at(g))
                    for c in range(chunks):
                        ins = pe.matmul(M[0:rws, g, 0:D], hidT_[:, g, P * c:P * c + rws], rhs(g, c),
                                        start=(c == 0), stop=(c == chunks - 1))
                    ins.then_inc(y_sem, 1)
                for g in range(n):
                    turn_hidden(g)
                    if g:
                        down(g - 1)
                down(n - 1)

            def experts(layer):
                L = LS[layer]

                def turn_inputs(grp, n):
                    pe.wait_ge(xs_in, 16 * (LSG[layer] + grp + 1))
                    for g in range(n):
                        ins = pe.transpose(xsT_bank[:, g, :], xs[:, g, :], ident[:])
                    ins.then_inc(xsT_ps, 1)

                def body(t0, grp, n, n_behind):
                    e = experts_of_group(pe, layer, grp, n)
                    pe.wait_ge(xsT_sb, LSG[layer] + grp + 1)
                    if layer or not is_zero(t0):
                        pe.wait_ge(y_sb, L + t0)
                    for g in range(n):
                        pe.matmul(M[:, g, :], xsT[:, g, :], W1[layer][:, bass.ds(e[g], 1), :].rearrange("p a f -> p (a f)"),
                                  start=True, stop=True).then_inc(up_ps, 1)
                    if n_behind:
                        turn_inputs(grp + 1, n_behind)
                    hidden_down(n, lambda g: H[layer] + t0 + g + 1, hidT, FC,
                                lambda g, c: W2[layer][:, bass.ds(e[g], 1), c, :].rearrange("p a d -> p (a d)"),
                                y_ps, hid_ready, hid, P)
                turn_inputs(0, G)
                pe.wait_ge(w0_loaded, 16 * 4)
                pe.wait_ge(routing_ready, layer + 1)
                if layer:
                    pe.wait_ge(w1a_loaded, 16)
                    pe.wait_ge(w1b_loaded, 32)
                pipelined(pe, SLOT_TILES[layer], body)

            attention0()
            rank(0)
            experts(0)
            attention1()
            rank(1)
            def shared(t0, grp, n):
                turn(xn, n, TT, zg_ready, LT[1] + TILES[1] + t0, zT_ps)
                for g in range(n):
                    pe.wait_ge(zT_sb, LT[1] + TILES[1] + t0 + g + 1)
                    pe.matmul(M[0:TT, g, 0:SHARED], xnT[:, g, 0:TT], sw1[:], start=True, stop=True).then_inc(up_ps, 1)
                hidden_down(n, lambda g: HS + t0 + g + 1, hidT, SC, lambda g, c: sw2[:, c, :], y_ps,
                            hid_ready, hid, TT)
            groups(pe, TILES[1], shared)
            pe.wait_ge(shared_ready, TILES[1])
            experts(1)

            def turn_normed(t0, n):
                for g in range(n):
                    pe.wait_ge(zg_ready, LT[1] + 2 * TILES[1] + t0 + g + 1)
                    ins = pe.transpose(xsT_bank[:, g, 0:TT], xn[0:TT, g, :], ident[0:TT, 0:TT])
                ins.then_inc(fT_ps, 1)

            def last(t0, grp, n, n_behind):
                pe.wait_ge(fT_sb, grp + 1)
                if not is_zero(t0):
                    pe.wait_ge(combined, t0)
                for g in range(n):
                    pe.matmul(M[0:TT, g, :], xnT[:, g, 0:TT], fw1[:], start=True, stop=True).then_inc(up_ps, 1)
                hidden_down(n, lambda g: HF + t0 + g + 1, fhidT, FC, lambda g, c: fw2[:, c, :], y_ps,
                            hid_ready, fhid, TT)
                if n_behind:
                    turn_normed(t0 + G, n_behind)
            turn_normed(0, G)
            pipelined(pe, TILES[1], last)

        @block.scalar
        def _(act):
            act.wait_ge(tok_rows_loaded, 32)
            act.activation(R[:, 0, :], row["cls_tok"], ACT.Copy).then_inc(cls_set, 1)

            def evacuate(n, base, wait, dst, src, sem):
                for g in range(n):
                    act.wait_ge(wait, base + g + 1)
                    act.activation(dst(g), src(g), ACT.Copy).then_inc(sem, 1)

            def turned(n, base, rws, wait, dst, sem, slot=0):
                evacuate(n, base, wait, lambda g: dst[:, slot + g, 0:rws], lambda g: M[:, slot + g, 0:rws], sem)

            def attention0():
                def turned_tile(k, ps, sb_):
                    act.wait_ge(ps, k + 1)
                    act.activation(xnT[:, k % 4, :], PS[:, 1, 512 * (k % 2):512 * (k % 2) + P], ACT.Copy).then_inc(sb_, 1)
                for k in range(SEQ):
                    turned_tile(k, xnT_ps, xnT_sb)
                    if k:
                        act.wait_ge(qkv_ps, k)
                        act.activation(qkv0[:, k - 1, :], M[:, (k - 1) % 4, 0:QKV0], ACT.Copy).then_inc(qkv0_sb, 1)
                act.wait_ge(qkv_ps, SEQ)
                act.activation(qkv0[:, SEQ - 1, :], M[:, (SEQ - 1) % 4, 0:QKV0], ACT.Copy).then_inc(qkv0_sb, 1)
                act.wait_ge(s0_shifted, 1)
                act.activation(p0, s0, ACT.Exp).then_inc(p0_exp, 1)
                for k in range(2):
                    act.wait_ge(mixedT_ps, k + 1)
                    m = min(4, len(MIXED_ROWS) - 4 * k)
                    act.activation(mixedT[:, 4 * k:4 * k + m, :].rearrange("p r b -> p (r b)"), PS[:, k, 0:m * P],
                                   ACT.Copy).then_inc(mixedT_sb, 1)
                for k in range(SEQ):
                    if k >= 4:
                        act.wait_ge(logit_ps, k - 3)
                    turned_tile(k, zT_ps, zT_sb)

            def attention1():
                L = LT[1]
                act.wait_ge(l1_loaded, 16 * 12)

                def projections(t0, grp, n):
                    turned(n, L + t0, TT, xnT_ps, xnT, xnT_sb)
                    for g in range(n):
                        act.wait_ge(qkv_ps, L + t0 + g + 1)
                        act.activation(qk[:, g], M[:, g, 0:240].rearrange("p (a t) -> p a t", a=2)[:, :, 0:TT],
                                       ACT.Copy).then_inc(qk_sb, 1)
                        act.activation(vs[:, bass.ds((grp & 3) * A + g, 1), :].rearrange("p a d -> p (a d)"),
                                       M[0:TT, g, 256:384], ACT.Copy).then_inc(v_sb, 1)
                        act.activation(oT[:, g, 0:IPT], M[:, g, 384:384 + IPT], ACT.Copy).then_inc(pl_sb, 1)

                def pT(t0, g):
                    act.wait_ge(pT_ps, t0 + g + 1)
                    act.activation(PT[:, g].rearrange("p (b h) t -> p b (h t)", b=2),
                                   PS[0:TT, 1, :].rearrange("p (b x) -> p b x", b=2)[:, :, 0:4 * TT],
                                   ACT.Copy).then_inc(pT_sb, 1)

                def o(t0, g):
                    act.wait_ge(o_ps, t0 + g + 1)
                    act.activation(osb[:, A + g, :], M[0:TT, A + g, 0:D], ACT.Copy).then_inc(o_sb, 1)

                def step(f, nf, m, nm, b, nb, c, nc, ahead, na):
                    f0, b0, c0, a0 = tiles_before(f, b, c, ahead)
                    if nb:
                        pT(b0, 0)
                    if nc:
                        turned(nc, L + c0, TT, zT_ps, xnT, zT_sb, slot=A)
                    if nf:
                        act.wait_ge(h1_ps, f + 1)
                        act.activation(xnT[:, 0, 0:nf * IPT], M[:, 0, 0:nf * IPT], ACT.Relu, bias=cols[:, 0:1])\
                            .then_inc(h1_sb, 1)
                    if nf:
                        act.wait_ge(h2_ps, f + 1)
                        act.activation(oT[0:64, 0:nf, :].rearrange("p g (i j) -> p g i j", j=SEQ),
                                       M[0:64, 0, 0:nf * IPT].rearrange("p (g i) -> p g i", i=IPT).unsqueeze(3)
                                       .broadcast_to([64, nf, IPT, SEQ]),
                                       ACT.Relu, bias=cols[0:64, 1:2]).then_inc(h2_sb, 1)
                    if nm:
                        if nb:
                            act.wait_ge(spread, b0 + nb)
                        act.wait_ge(shifted, m + 1)
                        act.activation(Pc[:, 0:nm * HEADS, :], Sc[:, 0:nm * HEADS, :], ACT.Exp).then_inc(exp_done, 1)
                    if nb:
                        o(b0, 0)
                    if nb > 1:
                        pT(b0, 1)
                        o(b0, 1)
                    if nf:
                        act.wait_ge(l3_shifted, f + 1)
                        act.activation(e3[:, 0:nf, :], l3[:, 0:nf, :], ACT.Exp, scale=1.0 / PATTERN_TEMPERATURE)\
                            .then_inc(e3_done, 1)
                    if nb:
                        turned(nb, b0, TT, oT_ps, oT, oT_sb, slot=A)
                    if na:
                        projections(a0, ahead, na)
                overlapped(act, step)

            def route(layer):
                n = TILES[layer] * EXPERTS[layer]
                act.wait_ge(route_shifted, layer + 1)
                act.activation(small(1, [n])[0:ROWS[layer]], small(0, [n])[0:ROWS[layer]], ACT.Exp,
                               scale=1.0 / TEMPERATURE[layer]).then_inc(route_exp, 1)

            def hidden(n, func, base, hbase, rws, width, hid_, hidT_):
                for g in range(n):
                    act.wait_ge(hid_biased, hbase + g + 1)
                    act.activation(hid_[0:rws, g, 0:width], hid_[0:rws, g, 0:width], func).then_inc(hid_ready, 1)
                for g in range(n):
                    act.wait_ge(hT_ps, hbase + g + 1)
                    act.activation(hidT_[:, g, 0:width].rearrange("p (c r) -> p c r", r=P)[:, :, 0:rws],
                                   hT_bank[g][:, 0:width].rearrange("p (c r) -> p c r", r=P)[:, :, 0:rws],
                                   ACT.Copy).then_inc(hT_sb, 1)

            def experts(layer):
                def body(t0, grp, n):
                    hidden(n, (ACT.Gelu, ACT.Silu)[layer], LS[layer] + t0, H[layer] + t0, P, FF, hid, hidT)
                groups(act, SLOT_TILES[layer], body)

            attention0()
            route(0)
            experts(0)
            attention1()
            route(1)

            def shared(t0, grp, n):
                turned(n, LT[1] + TILES[1] + t0, TT, zT_ps, xnT, zT_sb)
                hidden(n, ACT.Silu, 0, HS + t0, TT, SHARED, hid, hidT)
            groups(act, TILES[1], shared)
            experts(1)

            def take_normed(grp, n):
                act.wait_ge(fT_ps, grp + 1)
                act.activation(xnT[:, 0:n, 0:TT], xsT_bank[:, 0:n, 0:TT], ACT.Copy).then_inc(fT_sb, 1)

            def last(t0, grp, n, n_behind):
                hidden(n, ACT.Silu, 0, HF + t0, TT, FF, fhid, fhidT)
                if n_behind:
                    take_normed(grp + 1, n_behind)
            take_normed(0, G)
            pipelined(act, TILES[1], last)

        @block.vector
        def _(dve):
            seq = Seq(dve, dve_step)
            dve.wait_ge(tok_rows_loaded, 32)
            dve.wait_ge(consts, 2)

            def carry_wait():
                dve.tensor_copy(carrier[:, 1:2], carrier[:, 0:1])

            def announce(sem):
                dve.tensor_copy(carrier[:, 2:3], carrier[:, 0:1]).then_inc(sem, 1)

            def mean_var(n, rws, src, slot=0):
                carry_wait()
                for g in range(n):
                    seq.mark(dve.bn_stats(stats[0:rws, slot + g, :], src(g)))
                seq.sync()
                carry_wait()
                for g in range(n):
                    ins = dve.bn_aggr(mv[0:rws, slot + g, :], stats[0:rws, slot + g, :])
                ins.then_inc(mean_var_ready, 1)

            def mean_rstd(n, rws, src, at):
                mean_var(n, rws, src)
                dve.wait_ge(rstd_ready, at)

            def normalize(n, rws, src, dst, sem):
                for g in range(n):
                    dve.tensor_scalar(dst(g), src(g), mv[0:rws, g, 0:1], rs[0:rws, g:g + 1],
                                      ALU.subtract, ALU.mult).then_inc(sem, 1)

            def reduce(out_, in_, op):
                seq.mark(dve.tensor_reduce(out_, in_, AX.X, op))

            def keep_normed(layer, t0, n, ready, slot=0):
                rws = ROWS[layer]
                dve.wait_ge(zg_ready, ready)
                for g in range(n):
                    dve.tensor_copy(tile(Z, t0 + g, rws), xn[0:rws, slot + g, :]).then_inc(z_ready, 1)

            def take_logits(layer, t0, n, slot=0):
                rws, E = ROWS[layer], EXPERTS[layer]
                for g in range(n):
                    dve.wait_ge(logit_ps, LT[layer] + t0 + g + 1)
                    dve.tensor_tensor(logits[0:rws, bass.ds(t0 + g, 1), 0:E].rearrange("p a d -> p (a d)"),
                                      M[0:rws, slot + g, 0:E], router_b[layer][0:rws, :], ALU.add).then_inc(logits_ready, 1)

            def moments(lo, hi, wait=None):
                for t in range(lo, hi):
                    if wait:
                        wait(t)
                    seq.mark(dve.bn_stats(stats[:, t, :], R[:, t, :]))
                seq.sync()
                for t in range(lo, hi):
                    ins = dve.bn_aggr(mv[:, t, :], stats[:, t, :])
                ins.then_inc(mean_var_ready, 1)

            def norms(lo, hi, at, ready):
                dve.wait_ge(rstd_ready, at)
                for t in range(lo, hi):
                    dve.tensor_scalar(Z[:, t, :], R[:, t, :], mv[:, t, 0:1], rs[:, t:t + 1],
                                      ALU.subtract, ALU.mult).then_inc(ready, 1)

            def attention0():
                def embedded(t):
                    if t == 0:
                        dve.wait_ge(cls_set, 1)
                    else:
                        dve.wait_ge(emb_ps, t)
                        dve.tensor_tensor(R[:, t, :], M[:, (t - 1) % 4, 0:D], row["L0_tok_b"], ALU.add).then_inc(emb_sb, 1)
                        dve.wait_ge(emb_sb, t)
                for k, (lo, hi) in enumerate(EMBEDDED):
                    moments(lo, hi, embedded)
                    if k:
                        norms(*EMBEDDED[k - 1], k, xn_ready)
                norms(*EMBEDDED[-1], len(EMBEDDED), xn_ready)
                for w in WINDOW_ROWS:
                    if w in DVE_ROWS:
                        dve.wait_ge(qkv0_sb, position_of_window_row(w) + 1)
                        seq.step(query_key(dve, w))
                    else:
                        dve.wait_ge(products, POOL_ROWS.index(w) + 1)
                    reduce(s0[:, w, 0:heads_of(w)], prods_of(w, HDIM), ALU.add)
                seq.sync()
                n = SEQ * QHEADS
                flat = lambda t: t.rearrange("p w h g -> p (w h) g")
                each = lambda t: t[:, 0:n].unsqueeze(2).broadcast_to([P, n, HEADS])
                seq.step(dve.tensor_scalar(s0, s0, float(HDIM) ** -0.5, None, ALU.mult))
                reduce(mx[:, 0:n], flat(s0), ALU.max)
                seq.sync()
                dve.tensor_tensor(flat(s0), flat(s0), each(mx), ALU.subtract).then_inc(s0_shifted, 1)
                dve.wait_ge(p0_exp, 1)
                reduce(sm[:, 0:n], flat(p0), ALU.add)
                seq.sync()
                seq.step(dve.reciprocal(mx[:, 0:n], sm[:, 0:n]))
                dve.tensor_tensor(flat(p0), flat(p0), each(mx), ALU.mult).then_inc(p0_ready, 1)
                dve.wait_ge(p0_ready, 1)
                for w in WINDOW_ROWS:
                    if w in DVE_ROWS:
                        seq.sync()
                        seq.step(prob_value(dve, w))
                    else:
                        dve.wait_ge(weighted, POOL_ROWS.index(w) + 1)
                    reduce(mixed[:, 0:heads_of(w), w * HDIM:(w + 1) * HDIM], prods_of(w, HEADS), ALU.add)
                seq.sync()
                announce(mixed_ready)
                dve.wait_ge(rb0_ready, 1)
                for lo, hi in BIASED:
                    moments(lo, hi)
                at = len(EMBEDDED)
                for k, (lo, hi) in enumerate(BIASED):
                    norms(lo, hi, at + k + 1, zg_ready)
                at += len(BIASED)
                dve.wait_ge(proj0_ps, 1)
                for k, r in enumerate(MIXED_ROWS):
                    t = position_of_window_row(r)
                    seq.mark(dve.tensor_tensor(R[:, t, :], M[:, k // 4, P * (k % 4):P * (k % 4 + 1)], R[:, t, :], ALU.add))
                seq.sync()
                announce(attn0_done)
                for lo, hi in MIXED:
                    moments(lo, hi)
                for k, (lo, hi) in enumerate(MIXED):
                    norms(lo, hi, at + k + 1, zg_ready)
                dve.wait_ge(logit_ps, TILES[0])
                dve.tensor_tensor(logits[:, 0:SEQ, 0:8], PS[:, 0, 0:8 * SEQ].rearrange("p (t e) -> p t e", e=8),
                                  router_b[0].unsqueeze(1).broadcast_to([P, SEQ, 8]), ALU.add).then_inc(logits_ready, 1)

            def combine(layer, t0, n, onto, to):
                for k in range(2):
                    for g in range(n):
                        weight = choice[0:TT, bass.ds(t0 + g, 1), 2 + k:3 + k].rearrange("p a b -> p (a b)")
                        seq.mark(dve.scalar_tensor_tensor(
                            to[0:TT, g, :] if k and to is Rb else tile(onto, t0 + g, TT),
                            tile(Y[layer][k], t0 + g, TT), weight, tile(onto, t0 + g, TT), ALU.mult, ALU.add))
                    seq.sync()

            def sparse_keys(n):
                N = n * HEADS
                by_head = lambda k: minus_sparse[0:TT, k, :].unsqueeze(1).unsqueeze(3).broadcast_to([TT, n, HEADS, SEQ])
                g4 = lambda t: t[:, 0:N, :].rearrange("p (g h) j -> p g h j", g=n)
                seq.step(dve.tensor_tensor(g4(drop_key), g4(Sc), by_head(0), ALU.mult))
                seq.step(dve.tensor_tensor(g4(drop_key), g4(drop_key), by_head(1), ALU.add))

            def find_least(n):
                N = n * HEADS
                carry_wait()
                for r in range(N):
                    ins = dve.max(top8[:, r, :], drop_key[:, r, :])
                seq.mark(ins)

            def drop_keys(n):
                N = n * HEADS
                seq.sync()
                least = top8[:, 0:N, DROP - 1:DROP].broadcast_to([TT, N, SEQ])
                seq.mark(dve.tensor_tensor(drop_ge[:, 0:N], drop_key[:, 0:N], least, ALU.is_ge))
                seq.step(dve.tensor_tensor(drop_eq[:, 0:N], drop_key[:, 0:N], least, ALU.is_equal))
                reduce(drop_n[:, 0:N], drop_ge[:, 0:N], ALU.add)
                flat = lambda t: t[:, 0:N, :].rearrange("p r j -> p (r j)")
                seq.step(dve.tensor_tensor_scan(flat(drop_cum), flat(carry), flat(drop_eq), 0.0, ALU.mult, ALU.add))
                seq.step(dve.tensor_scalar(drop_n[:, 0:N], drop_n[:, 0:N], float(DROP), None, ALU.subtract))
                seq.step(dve.tensor_tensor(drop_cum[:, 0:N], drop_cum[:, 0:N],
                                           drop_n[:, 0:N].unsqueeze(2).broadcast_to([TT, N, SEQ]), ALU.is_le))
                seq.step(dve.tensor_tensor(drop_eq[:, 0:N], drop_eq[:, 0:N], drop_cum[:, 0:N], ALU.mult))
                seq.step(dve.tensor_tensor(drop_ge[:, 0:N], drop_ge[:, 0:N], drop_eq[:, 0:N], ALU.subtract))

            def attention1():
                L = LT[1]
                dve.wait_ge(l1_loaded, 16 * 12)
                dve.wait_ge(rows_loaded, 16 * 14)
                seq.mark(dve.tensor_scalar(minus_sparse[:, 0, :], row["L1_attn_sparse_w"], -1.0, None, ALU.mult))
                seq.mark(dve.tensor_scalar(minus_sparse[:, 1, :], row["L1_attn_sparse_b"], -1.0, None, ALU.mult))
                seq.mark(dve.tensor_tensor(pattern_b[:], row["L1_attn_ps_b3"], row["L1_attn_pattern_bias"], ALU.add))
                seq.sync()

                def front_in(j, n):
                    t0 = A * j
                    dve.wait_ge(gathered, 32 * (t0 + n))
                    combine(0, t0, n, R, R)
                    mean_var(n, TT, lambda g: tile(R, t0 + g, TT))

                def front_normed(j, n):
                    dve.wait_ge(rstd_ready, norm_in_at(j))
                    normalize(n, TT, lambda g: tile(R, A * j + g, TT), lambda g: xn[0:TT, g, :], xn_ready)
                    announce(experts_added)

                def pack(t0, g):
                    dve.wait_ge(scores_ps, t0 + g + 1)
                    for b in range(2):
                        ins = dve.tensor_reduce(
                            Sc[:, g * HEADS + 4 * b:g * HEADS + 4 * b + 4, :],
                            PS[0:TT, 0, 512 * b:512 * b + 4 * TT].rearrange("p (h i j) -> p h j i", h=4, i=IPT),
                            AX.X, ALU.max)
                    ins.then_inc(packed, 1)

                def pattern_logits(t0, n):
                    for g in range(n):
                        dve.wait_ge(l3_ps, t0 + g + 1)
                        seq.mark(dve.tensor_tensor(l3[:, g, :], M[0:TT, g, 0:3], pattern_b[0:TT, :], ALU.add))
                    seq.sync()
                    reduce(g1[:, 0:n], l3[:, 0:n], ALU.max)
                    seq.sync()
                    dve.tensor_tensor(l3[:, 0:n], l3[:, 0:n], g1[:, 0:n].unsqueeze(2).broadcast_to([TT, n, 3]),
                                      ALU.subtract).then_inc(l3_shifted, 1)

                def gate_keys(j, n):
                    dve.wait_ge(e3_done, j + 1)
                    reduce(g1[:, 0:n], e3[:, 0:n], ALU.add)
                    seq.sync()
                    seq.step(dve.reciprocal(g2[:, 0:n], g1[:, 0:n]))
                    seq.step(dve.tensor_tensor(e3[:, 0:n], e3[:, 0:n], g2[:, 0:n].unsqueeze(2).broadcast_to([TT, n, 3]),
                                               ALU.mult))
                    seq.step(dve.tensor_tensor(g1[:, 0:n], e3[:, 0:n, 0], e3[:, 0:n, 1], ALU.add))
                    seq.step(dve.tensor_scalar(g2[:, 0:n], g1[:, 0:n], 0.05, NEG, ALU.is_le, ALU.mult))
                    for g in range(n):
                        h = slice(g * HEADS, (g + 1) * HEADS)
                        seq.mark(dve.scalar_tensor_tensor(Sc[:, h, :], drop_ge[:, h, :], g2[:, g:g + 1], Sc[:, h, :],
                                                          ALU.mult, ALU.add))
                    seq.sync()

                def softmax(j, n):
                    N = n * HEADS
                    reduce(mx[0:TT, 0:N], Sc[:, 0:N, :], ALU.max)
                    seq.sync()
                    dve.tensor_tensor(Sc[:, 0:N, :], Sc[:, 0:N, :], mx[0:TT, 0:N].unsqueeze(2).broadcast_to([TT, N, SEQ]),
                                      ALU.subtract).then_inc(shifted, 1)
                    dve.wait_ge(exp_done, j + 1)
                    reduce(sm[0:TT, 0:N], Pc[:, 0:N, :], ALU.add)
                    seq.sync()
                    seq.step(dve.reciprocal(mx[0:TT, 0:N], sm[0:TT, 0:N]))
                    for g in range(n):
                        h = slice(g * HEADS, (g + 1) * HEADS)
                        dve.tensor_tensor(Pc[:, h, :], Pc[:, h, :],
                                          mx[0:TT, h].unsqueeze(2).broadcast_to([TT, HEADS, SEQ]),
                                          ALU.mult).then_inc(probs, 1)

                def residual(i, t0, n):
                    dve.wait_ge(rb_ready, i + 1)
                    for g in range(n):
                        dve.wait_ge(proj_ps, t0 + g + 1)
                        seq.mark(dve.tensor_tensor(tile(R, t0 + g, TT), M[0:TT, A + g, 0:D], tile(R, t0 + g, TT), ALU.add))
                    seq.sync()
                    mean_var(n, TT, lambda g: tile(R, t0 + g, TT), slot=A)

                def add_norm(i, t0, n):
                    dve.wait_ge(rstd_ready, norm_out_at(i, 0))
                    for g in range(n):
                        seq.mark(dve.tensor_scalar(Rb[0:TT, g, :], tile(R, t0 + g, TT), mv[0:TT, A + g, 0:1],
                                                   rs[0:TT, A + g:A + g + 1], ALU.subtract, ALU.mult))
                    seq.sync()
                    for g in range(n):
                        seq.mark(dve.tensor_tensor(tile(R, t0 + g, TT), tile(R, t0 + g, TT), Rb[0:TT, g, :], ALU.add))
                    mean_var(n, TT, lambda g: Rb[0:TT, g, :], slot=A)

                def step(f, nf, m, nm, b, nb, c, nc, ahead, na):
                    f0, b0, c0 = tiles_before(f, b, c)
                    if nc:
                        take_logits(1, c0, nc, slot=A)
                    if nm:
                        gate_keys(m, nm)
                        softmax(m, nm)
                    if na:
                        front_in(ahead, na)
                    if nf:
                        pattern_logits(f0, nf)
                    if na:
                        front_normed(ahead, na)
                    if nf:
                        pack(f0, 0)
                    if nb:
                        residual(b, b0, nb)
                    if nf > 1:
                        pack(f0, 1)
                    if nb:
                        add_norm(b, b0, nb)
                    if nf:
                        dve.wait_ge(packed, f0 + nf)
                        sparse_keys(nf)
                    if nb:
                        dve.wait_ge(rstd_ready, norm_out_at(b, 1))
                        scaled_norm(nb, Rb, row["L1_ffn_ln_in_g"], row["L1_ffn_ln_in_b"], slot=A)
                        keep_normed(1, b0, nb, L + b0 + nb, slot=A)
                    if nf:
                        find_least(nf)
                        drop_keys(nf)
                overlapped(dve, step, seq, 11 * A + 21)

            def scaled_norm(n, src, gain, shift, slot=0):
                both = lambda v: v[0:TT, :].unsqueeze(1).broadcast_to([TT, n, D])
                for g in range(n):
                    seq.mark(dve.tensor_scalar(xn[0:TT, slot + g, :], src[0:TT, g, :], mv[0:TT, slot + g, 0:1],
                                               rs[0:TT, slot + g:slot + g + 1],
                                               ALU.subtract, ALU.mult))
                seq.sync()
                seq.step(dve.tensor_tensor(xn[0:TT, slot:slot + n, :], xn[0:TT, slot:slot + n, :], both(gain), ALU.mult))
                for g in range(n):
                    dve.tensor_tensor(xn[0:TT, slot + g, :], xn[0:TT, slot + g, :], shift[0:TT, :], ALU.add).then_inc(zg_ready, 1)

            def route(layer):
                rws, T, E = ROWS[layer], TILES[layer], EXPERTS[layer]

                def buf(k, shape=(T, E)):
                    return small(k, list(shape))[0:rws]

                def each(t):
                    return t.unsqueeze(2).broadcast_to([rws, T, E])
                lg = logits[0:rws, 0:T, 0:E]
                top, sum_, w0, w1, tmp = (small(12, [5, T])[0:rws, k, :] for k in range(5))
                fall = falling[0:rws, 16 - E:16].unsqueeze(1).broadcast_to([rws, T, E])
                dve.wait_ge(logits_ready, 1 if layer == 0 else 1 + T)
                reduce(top, lg, ALU.max)
                seq.sync()
                d, p, M0, M1, key = buf(0), buf(1), buf(2), buf(3), buf(4)
                dve.tensor_tensor(d, lg, each(top), ALU.subtract).then_inc(route_shifted, 1)
                dve.wait_ge(route_shifted, layer + 1)

                def first_largest(v, largest, out_):
                    seq.step(dve.tensor_tensor(key, v, each(largest), ALU.is_ge))
                    seq.step(dve.tensor_tensor(key, key, fall, ALU.mult))
                    reduce(tmp, key, ALU.max)
                    seq.sync()
                    seq.step(dve.tensor_tensor(out_, key, each(tmp), ALU.is_equal))
                first_largest(lg, top, M0)
                dve.wait_ge(route_exp, layer + 1)
                seq.step(dve.scalar_tensor_tensor(d, M0, NEG, d, ALU.mult, ALU.add))
                reduce(tmp, d, ALU.max)
                seq.sync()
                first_largest(d, tmp, M1)
                seq.step(dve.tensor_tensor(routed[0:rws, 0:T, 0:E], M0, M1, ALU.add))
                if layer:
                    seq.step(dve.tensor_scalar(routed[0:rws, T - 1, 0:E], routed[0:rws, T - 1, 0:E],
                                               is_last[0:rws, 0:1], None, ALU.mult))
                announce(routed_ready)
                dve.wait_ge(rank_ps, layer + 1)
                per_tile, incl, excl = (buf(k, (E, T + 1)) for k in (5, 6, 7))
                totals, padded = small(13, [2, E])[0:rws, 0, :], small(13, [2, E])[0:rws, 1, :]
                n = T * E
                seq.step(dve.tensor_copy(per_tile[:, :, 0:T], PS[0:rws, 1, 0:n].rearrange("p (t e) -> p e t", e=E)))
                reduce(totals, per_tile[:, :, 0:T], ALU.add)
                seq.sync()
                seq.step(dve.tensor_scalar(count_i[0:rws, 0, 0:E], totals, float(P - 1), None, ALU.add))
                seq.step(dve.tensor_scalar(count_i[0:rws, 1, 0:E], count_i[0:rws, 0, 0:E], 7, 7,
                                           ALU.arith_shift_right, ALU.logical_shift_left))
                seq.step(dve.tensor_copy(padded, count_i[0:rws, 1, 0:E]))
                seq.step(dve.tensor_tensor(per_tile[:, :, T], padded, totals, ALU.subtract))
                flat = lambda t: t.rearrange("p e t -> p (e t)")
                seq.step(dve.tensor_tensor_scan(flat(incl), ones_f[0:rws, 0:E * (T + 1)], flat(per_tile), 0.0,
                                                ALU.mult, ALU.add))
                seq.step(dve.tensor_tensor(excl, incl, per_tile, ALU.subtract))
                slot = buf(8)
                seq.step(dve.tensor_tensor(slot, PS[0:rws, 0, 0:n].rearrange("p (t e) -> p t e", e=E),
                                           excl[:, :, 0:T].rearrange("p e t -> p t e"), ALU.add))
                for k, m in enumerate((M0, M1)):
                    seq.step(dve.tensor_tensor(key, slot, m, ALU.mult))
                    reduce(tmp, key, ALU.add)
                    seq.sync()
                    seq.step(dve.tensor_copy(choice[0:rws, 0:T, k].bitcast(I32), tmp))
                announce(slots_ready)
                NT = G * SLOT_GROUPS[layer]
                ends = small(9, [NT * (E - 1)])[0:1].rearrange("p (i e) -> p i e", e=E - 1)
                seq.step(dve.tensor_tensor(ends, slot0[0:1, 0:NT].unsqueeze(2).broadcast_to([1, NT, E - 1]),
                                           incl[0:1, 0:E - 1, T].unsqueeze(1).broadcast_to([1, NT, E - 1]), ALU.is_ge))
                last_end, group_of = small(14, [SLOT_GROUPS[layer], G])[0:1], small(15, [SLOT_GROUPS[layer]])[0:1]
                reduce(last_end.rearrange("p i g -> p (i g)"), ends, ALU.add)
                seq.sync()
                seq.step(dve.tensor_tensor(last_end, last_end,
                                           radix[:].unsqueeze(1).broadcast_to([1, SLOT_GROUPS[layer], G]), ALU.mult))
                reduce(group_of, last_end, ALU.add)
                seq.sync()
                dve.tensor_copy(expert_of[0:1, 0:SLOT_GROUPS[layer]], group_of).then_inc(routing_ready, 1)
                reduce(sum_, p, ALU.add)
                for m, w in ((M0, w0), (M1, w1)):
                    seq.step(dve.tensor_tensor(key, p, m, ALU.mult))
                    reduce(w, key, ALU.add)
                    seq.sync()
                seq.step(dve.reciprocal(tmp, sum_))
                for k, w in enumerate((w0, w1)):
                    seq.mark(dve.tensor_tensor(w if layer == 0 else choice[0:rws, 0:T, 2 + k], w, tmp, ALU.mult))
                seq.sync()
                if layer == 0:
                    seq.step(dve.scalar_tensor_tensor(sum_, w0, 1e-9, w1, ALU.add, ALU.add))
                    seq.step(dve.reciprocal(tmp, sum_))
                    for k, w in enumerate((w0, w1)):
                        seq.mark(dve.tensor_tensor(choice[0:rws, 0:T, 2 + k], w, tmp, ALU.mult))
                seq.sync()
                announce(weights_ready)

            def experts(layer):
                def inputs_turned(grp, n):
                    dve.wait_ge(xsT_ps, LSG[layer] + grp + 1)
                    dve.tensor_copy(xsT[:, 0:n, :], xsT_bank[:, 0:n, :]).then_inc(xsT_sb, 1)

                def body(t0, grp, n, n_behind):
                    e = experts_of_group(dve, layer, grp, n)
                    for g in range(n):
                        dve.wait_ge(up_ps, H[layer] + t0 + g + 1)
                        dve.tensor_tensor(hid[:, g, :], M[:, g, :], B1[layer][:, bass.ds(e[g], 1), :].rearrange("p a f -> p (a f)"),
                                          ALU.add).then_inc(hid_biased, 1)
                    if n_behind:
                        inputs_turned(grp + 1, n_behind)
                    if layer or not is_zero(t0):
                        dve.wait_ge(y_stored, 16 * (LSG[layer] + grp))
                    for g in range(n):
                        dve.wait_ge(y_ps, H[layer] + t0 + g + 1)
                        dve.tensor_tensor(ys[:, g, :], M[:, g, 0:D], B2[layer][:, bass.ds(e[g], 1), :].rearrange("p a f -> p (a f)"),
                                          ALU.add).then_inc(y_sb, 1)
                dve.wait_ge(routing_ready, layer + 1)
                inputs_turned(0, G)
                dve.wait_ge(w0_loaded, 16 * 4)
                if layer:
                    dve.wait_ge(w1b_loaded, 32)
                    dve.wait_ge(b2_loaded, 16)
                pipelined(dve, SLOT_TILES[layer], body)

            attention0()
            route(0)
            experts(0)
            dve.wait_ge(residual_loaded, 16)
            dve.wait_ge(choice_loaded, 16)
            attention1()
            route(1)

            def shared(t0, grp, n):
                for g in range(n):
                    dve.tensor_copy(xn[0:TT, g, :], tile(Z, t0 + g, TT)).then_inc(zg_ready, 1)
                for g in range(n):
                    dve.wait_ge(up_ps, HS + t0 + g + 1)
                    dve.tensor_tensor(hid[0:TT, g, 0:SHARED], M[0:TT, g, 0:SHARED], row["L1_ffn_sb1"][0:TT, :],
                                      ALU.add).then_inc(hid_biased, 1)
                for g in range(n):
                    dve.wait_ge(y_ps, HS + t0 + g + 1)
                    seq.mark(dve.tensor_tensor(Rb[0:TT, g, :], M[0:TT, g, 0:D], row["L1_ffn_sb2"][0:TT, :], ALU.add))
                seq.sync()
                for g in range(n):
                    dve.tensor_scalar(tile(S, t0 + g, TT), Rb[0:TT, g, :], 0.25, None, ALU.mult).then_inc(shared_ready, 1)
            groups(dve, TILES[1], shared, seq, G)
            experts(1)

            def mix(t0, n):
                dve.wait_ge(gathered, 32 * (TILES[1] + t0 + n))
                combine(1, t0, n, S, Rb)
                mean_var(n, TT, lambda g: Rb[0:TT, g, :])

            def norm_mixed(t0, grp, n):
                dve.wait_ge(rstd_ready, NORMS + 3 * A_GROUPS + grp + 1)
                scaled_norm(n, Rb, row["L1_ffn_ff_ln_g"], row["L1_ffn_ff_ln_b"])
                for g in range(n):
                    seq.mark(dve.tensor_tensor(tile(Z, t0 + g, TT), Rb[0:TT, g, :], tile(R, t0 + g, TT), ALU.add))
                seq.sync()
                for g in range(n):
                    seq.mark(dve.tensor_tensor(tile(Z, t0 + g, TT), tile(Z, t0 + g, TT), row["L1_ffn_ff_b2"][0:TT, :], ALU.add))

            def last(t0, grp, n, n_behind):
                for g in range(n):
                    dve.wait_ge(up_ps, HF + t0 + g + 1)
                    dve.tensor_tensor(fhid[0:TT, g, :], M[0:TT, g, :], row["L1_ffn_ff_b1"][0:TT, :],
                                      ALU.add).then_inc(hid_biased, 1)
                seq.sync()
                if n_behind:
                    mix(t0 + G, n_behind)
                for g in range(n):
                    dve.wait_ge(y_ps, HF + t0 + g + 1)
                    dve.tensor_tensor(tile(Z, t0 + g, TT), M[0:TT, g, 0:D], tile(Z, t0 + g, TT), ALU.add).then_inc(combined, 1)
                if n_behind:
                    norm_mixed(t0 + G, grp + 1, n_behind)
            mix(0, G)
            norm_mixed(0, 0, G)
            pipelined(dve, TILES[1], last, seq, 6 * G + 1)


def _laid_out(name, v):
    import numpy as np
    if name == "x":
        v = v.reshape(IMAGES, CHANNELS, GRID, 2, PATCH // 2, GRID, PATCH)
        return v.transpose(4, 6, 2, 5, 1, 3, 0).reshape(P, PATCHES, PIX, IMAGES)
    if name == "L0_tok_W":
        return v.reshape(D, CHANNELS, 2, P).transpose(3, 1, 2, 0).reshape(P, PIX, D)
    if name == "L0_attn_w_qkv":
        return np.concatenate([v[:QHEADS * HDIM], v[D:]]).T
    if name in ("L0_attn_w_proj", "L1_attn_qkv_w", "L1_attn_proj_w", "L1_attn_ps_w1",
                "L1_attn_ps_w2", "L1_attn_ps_w3"):
        return v.T
    if name in ("L0_ffn_w1", "L1_ffn_ew1"):
        return v.transpose(1, 0, 2)
    if name in ("L0_ffn_w2", "L1_ffn_ew2"):
        return v.reshape(v.shape[0], FC, P, D).transpose(2, 0, 1, 3)
    if name == "L1_ffn_sw2" or name == "L1_ffn_ff_w2":
        return v.reshape(-1, P, D).transpose(1, 0, 2)
    return v


def kernel(**inputs):
    import numpy as _np
    import concourse.bacc as _bacc
    from concourse import mybir as _mybir
    from concourse.bass_utils import run_bass_kernel_spmd as _run

    nc = _bacc.Bacc("TRN2", target_bir_lowering=False, num_devices=1)
    arrays, args = {}, {}
    for name, value in inputs.items():
        v = _laid_out(name, _np.asarray(value))
        v = _np.ascontiguousarray(v)
        arrays[f"in_{name}_dram"] = v
        args[name] = nc.dram_tensor(f"in_{name}_dram", v.shape, _mybir.dt.from_np(v.dtype), kind="ExternalInput").ap()
    out = nc.dram_tensor("out_0_dram", (IMAGES, SEQ, D), _mybir.dt.float32, kind="ExternalOutput").ap()
    vit_tower(nc, args, out)
    r = _run(nc, [arrays], core_ids=[0])
    return r.results[0]["out_0_dram"]
```
